# Optimizing a Trainium2 kernel written in Bass

```python
import numpy as np
import jax
import jax.numpy as jnp

def _softmax(x, axis=-1):
    return jax.nn.softmax(x, axis=axis)

def _gelu(x):
    return jax.nn.gelu(x, approximate=True)

def _silu(x):
    return jax.nn.silu(x)

def _sigmoid(x):
    return jax.nn.sigmoid(x)

def _layernorm(x, axis=-1, eps=1e-05):
    m = jnp.mean(x, axis=axis, keepdims=True)
    v = jnp.var(x, axis=axis, keepdims=True)
    return (x - m) / jnp.sqrt(v + eps)

def _scatter_add(tgt, idx, src, axis=0):
    return tgt.at[idx].add(src)

def _segment_sum(src, seg, n):
    return jax.ops.segment_sum(src, seg, n)
kernel_name = 'mk_gnn_preln_d4_gnn_r32_743ca8'

def setup_inputs(seed: int=0):
    np.random.seed(seed)
    _w = jnp.asarray

    def _rec_inputs():
        import jax
        import jax.numpy as jnp
        _gk = jax.random.key(seed)
        x = -6.415e-05 + 1 * jax.random.normal(jax.random.fold_in(_gk, 1), (625, 512), jnp.float32)
        src = jax.random.randint(jax.random.fold_in(_gk, 2), (20000,), 0, 625, jnp.int32)
        dst = jax.random.randint(jax.random.fold_in(_gk, 3), (20000,), 0, 625, jnp.int32)
        _o = jnp.argsort(dst, stable=True)
        src = src[_o]
        dst = dst[_o]
        edge_type_10 = jax.random.randint(jax.random.fold_in(_gk, 12), (20000,), 0, 10, jnp.int32)
        edge_weight = 0.000747931 + 0.998196 * jax.random.normal(jax.random.fold_in(_gk, 13), (20000,), jnp.float32)
        node_vec1 = jax.random.uniform(jax.random.fold_in(_gk, 14), (625, 1), jnp.float32, 0.0, 0.999957)
        return (x, src, dst, edge_type_10, edge_weight, node_vec1)
    x, src, dst, edge_type_10, edge_weight, node_vec1 = _rec_inputs()

    def _L0_gnn_setup():
        import jax, jax.numpy as jnp
        import numpy as np
        N_NODES = 625
        key = jax.random.key(seed)
        ks = jax.random.split(key, 6)
        d = 512
        E = 20000
        x = jax.random.normal(ks[0], (N_NODES, d), dtype=jnp.float32)
        edge_index = jax.random.randint(ks[1], (2, E), 0, N_NODES, dtype=jnp.int64)
        s = 1.0 / np.sqrt(d)
        W1 = jax.random.uniform(ks[2], (d, d), jnp.float32, -s, s)
        b1 = jax.random.uniform(ks[3], (d,), jnp.float32, -s, s)
        W2 = jax.random.uniform(ks[4], (d, d), jnp.float32, -s, s)
        b2 = jax.random.uniform(ks[5], (d,), jnp.float32, -s, s)
        return {'x': x, 'edge_index': edge_index, 'W1': W1, 'b1': b1, 'W2': W2, 'b2': b2}
    _L0_gnn_all = _L0_gnn_setup()
    _L0_gnn_in = {k: v for k, v in _L0_gnn_all.items() if k in ('W1', 'b1', 'W2', 'b2')}
    del _L0_gnn_all

    def _L1_gnn_setup():
        import jax, jax.numpy as jnp
        import numpy as np
        N = 50000
        E = 12500
        D_IN = 512
        D_HID = 64
        D_OUT = 512
        key = jax.random.key(seed)
        k1, k2, k3, k4 = jax.random.split(key, 4)
        x = jax.random.normal(k1, (N, D_IN), dtype=jnp.float32)
        edge_index = jax.random.randint(k2, (2, E), 0, N, dtype=jnp.int64)
        W1 = jax.random.normal(k3, (D_IN, D_HID), dtype=jnp.float32) * (1.0 / np.sqrt(D_IN))
        b1 = jnp.zeros((D_HID,), dtype=jnp.float32)
        W2 = jax.random.normal(k4, (D_HID, D_OUT), dtype=jnp.float32) * (1.0 / np.sqrt(D_HID))
        b2 = jnp.zeros((D_OUT,), dtype=jnp.float32)
        return {'x': x, 'edge_index': edge_index, 'W1': W1, 'b1': b1, 'W2': W2, 'b2': b2}
    _L1_gnn_all = _L1_gnn_setup()
    _L1_gnn_in = {k: v for k, v in _L1_gnn_all.items() if k in ('W1', 'b1', 'W2', 'b2')}
    del _L1_gnn_all

    def _L2_gnn_setup():
        import jax, jax.numpy as jnp
        import numpy as np
        N_NODES = 40962
        LATENT_DIM = 512
        N_EDGES = 20481
        NUM_BLOCKS = 4
        NUM_HEADS = 4
        NUM_FREQ = 32
        BASE_PERIOD = 16
        NOISE_EMB_DIM = 16
        EPS = 1e-05

        def _cond_layer_norm(x, cond, sw, sb, bw, bb):
            mu = jnp.mean(x, axis=-1, keepdims=True)
            var = jnp.var(x, axis=-1, keepdims=True)
            xn = (x - mu) * jax.lax.rsqrt(var + EPS)
            scale = cond @ sw + sb
            bias = cond @ bw + bb
            return xn * (1.0 + scale) + bias

        def _sparse_attention(x, src, dst, wq, bq, wk, bk, wv, bv, wo, bo):
            N, D = x.shape
            H, Dh = (NUM_HEADS, D // NUM_HEADS)
            q = (x @ wq + bq).reshape(N, H, Dh) * Dh ** (-0.5)
            k = (x @ wk + bk).reshape(N, H, Dh)
            v = (x @ wv + bv).reshape(N, H, Dh)
            scores = jnp.einsum('ehd,ehd->eh', q[src], k[dst])
            smax = jax.ops.segment_max(scores, src, num_segments=N)
            ex = jnp.exp(scores - smax[src])
            denom = jax.ops.segment_sum(ex, src, num_segments=N)
            attn = ex / denom[src]
            out = jax.ops.segment_sum(attn[:, :, None] * v[dst], src, num_segments=N)
            return out.reshape(N, D) @ wo + bo

        def _forward(x, edge_index, noise_levels, f_w1, f_b1, f_w2, f_b2, s1_w, s1_b, b1_w, b1_b, wq, bq, wk, bk, wv, bv, wo, bo, s2_w, s2_b, b2_w, b2_b, m_w1, m_b1, m_w2, m_b2):
            src, dst = (edge_index[0], edge_index[1])
            freqs = jnp.arange(1, NUM_FREQ + 1, dtype=x.dtype) * (2.0 * np.pi / BASE_PERIOD)
            ph = noise_levels * freqs
            emb = jnp.concatenate([jnp.sin(ph), jnp.cos(ph)], axis=-1)
            cond = jax.nn.silu(emb @ f_w1 + f_b1) @ f_w2 + f_b2
            for i in range(NUM_BLOCKS):
                y = _cond_layer_norm(x, cond, s1_w[i], s1_b[i], b1_w[i], b1_b[i])
                y = _sparse_attention(y, src, dst, wq[i], bq[i], wk[i], bk[i], wv[i], bv[i], wo[i], bo[i])
                x = x + y
                y = _cond_layer_norm(x, cond, s2_w[i], s2_b[i], b2_w[i], b2_b[i])
                y = jax.nn.relu(y @ m_w1[i] + m_b1[i]) @ m_w2[i] + m_b2[i]
                x = x + y
            return x
        key = jax.random.key(seed)
        ks = jax.random.split(key, 20)

        def w(k, shape, s=0.02):
            return jax.random.normal(k, shape, dtype=jnp.float32) * s
        D, B, C = (LATENT_DIM, NUM_BLOCKS, NOISE_EMB_DIM)
        z = lambda *s: jnp.zeros(s, jnp.float32)
        return {'latent_mesh_nodes': jax.random.normal(ks[0], (N_NODES, D), dtype=jnp.float32), 'edge_index': jax.random.randint(ks[1], (2, N_EDGES), 0, N_NODES, dtype=jnp.int32), 'noise_levels': jax.random.uniform(ks[2], (N_NODES, 1), dtype=jnp.float32), 'f_w1': w(ks[3], (2 * NUM_FREQ, C)), 'f_b1': z(C), 'f_w2': w(ks[4], (C, C)), 'f_b2': z(C), 's1_w': w(ks[5], (B, C, D)), 's1_b': z(B, D), 'b1_w': w(ks[6], (B, C, D)), 'b1_b': z(B, D), 'wq': w(ks[7], (B, D, D)), 'bq': z(B, D), 'wk': w(ks[8], (B, D, D)), 'bk': z(B, D), 'wv': w(ks[9], (B, D, D)), 'bv': z(B, D), 'wo': w(ks[10], (B, D, D)), 'bo': z(B, D), 's2_w': w(ks[11], (B, C, D)), 's2_b': z(B, D), 'b2_w': w(ks[12], (B, C, D)), 'b2_b': z(B, D), 'm_w1': w(ks[13], (B, D, D)), 'm_b1': z(B, D), 'm_w2': w(ks[14], (B, D, D)), 'm_b2': z(B, D)}
    _L2_gnn_all = _L2_gnn_setup()
    _L2_gnn_in = {k: v for k, v in _L2_gnn_all.items() if k in ('f_w1', 'f_b1', 'f_w2', 'f_b2', 's1_w', 's1_b', 'b1_w', 'b1_b', 'wq', 'bq', 'wk', 'bk', 'wv', 'bv', 'wo', 'bo', 's2_w', 's2_b', 'b2_w', 'b2_b', 'm_w1', 'm_b1', 'm_w2', 'm_b2')}
    del _L2_gnn_all

    def _L3_gnn_setup():
        import jax, jax.numpy as jnp
        import numpy as np
        N, E, H, D, C, L = (625, 10000, 8, 64, 512, 2)

        def layer_norm(x, g, b, eps=1e-05):
            mu = x.mean(-1, keepdims=True)
            var = ((x - mu) ** 2).mean(-1, keepdims=True)
            return (x - mu) / jnp.sqrt(var + eps) * g + b
        key = jax.random.key(seed)
        ks = jax.random.split(key, 14)
        s = 0.02
        x = jax.random.normal(ks[0], (N, C), jnp.float32)
        edge_index = jax.random.randint(ks[1], (2, E), 0, N, jnp.int32)
        edge_type = jax.random.randint(ks[2], (E,), 0, 10, jnp.int32)
        edge_repre = jax.random.normal(ks[3], (E,), jnp.float32)
        Wq = jax.random.normal(ks[4], (L, C, C), jnp.float32) * s
        Wk = jax.random.normal(ks[5], (L, C, C), jnp.float32) * s
        Wv = jax.random.normal(ks[6], (L, C, C), jnp.float32) * s
        Ws = jax.random.normal(ks[7], (L, C, C), jnp.float32) * s
        bq = jnp.zeros((L, C), jnp.float32)
        bk = jnp.zeros((L, C), jnp.float32)
        bv = jnp.zeros((L, C), jnp.float32)
        bs = jnp.zeros((L, C), jnp.float32)
        W1 = jax.random.normal(ks[8], (C, 2 * C), jnp.float32) * s
        b1 = jnp.zeros((2 * C,), jnp.float32)
        W2 = jax.random.normal(ks[9], (2 * C, C), jnp.float32) * s
        b2 = jnp.zeros((C,), jnp.float32)
        ln_g = jnp.ones((C,), jnp.float32)
        ln_b = jnp.zeros((C,), jnp.float32)
        return {'x': x, 'edge_index': edge_index, 'edge_type': edge_type, 'edge_repre': edge_repre, 'Wq': Wq, 'bq': bq, 'Wk': Wk, 'bk': bk, 'Wv': Wv, 'bv': bv, 'Ws': Ws, 'bs': bs, 'W1': W1, 'b1': b1, 'W2': W2, 'b2': b2, 'ln_g': ln_g, 'ln_b': ln_b}
    _L3_gnn_all = _L3_gnn_setup()
    _L3_gnn_in = {k: v for k, v in _L3_gnn_all.items() if k in ('Wq', 'bq', 'Wk', 'bk', 'Wv', 'bv', 'Ws', 'bs', 'W1', 'b1', 'W2', 'b2', 'ln_g', 'ln_b')}
    del _L3_gnn_all
    return {'x': x, 'src': src, 'dst': dst, 'edge_type_10': edge_type_10, 'edge_weight': edge_weight, 'node_vec1': node_vec1, 'L0_gnn_W1': _L0_gnn_in['W1'], 'L0_gnn_b1': _L0_gnn_in['b1'], 'L0_gnn_W2': _L0_gnn_in['W2'], 'L0_gnn_b2': _L0_gnn_in['b2'], 'L1_gnn_W1': _L1_gnn_in['W1'], 'L1_gnn_b1': _L1_gnn_in['b1'], 'L1_gnn_W2': _L1_gnn_in['W2'], 'L1_gnn_b2': _L1_gnn_in['b2'], 'L2_gnn_f_w1': _L2_gnn_in['f_w1'], 'L2_gnn_f_b1': _L2_gnn_in['f_b1'], 'L2_gnn_f_w2': _L2_gnn_in['f_w2'], 'L2_gnn_f_b2': _L2_gnn_in['f_b2'], 'L2_gnn_s1_w': _L2_gnn_in['s1_w'], 'L2_gnn_s1_b': _L2_gnn_in['s1_b'], 'L2_gnn_b1_w': _L2_gnn_in['b1_w'], 'L2_gnn_b1_b': _L2_gnn_in['b1_b'], 'L2_gnn_wq': _L2_gnn_in['wq'], 'L2_gnn_bq': _L2_gnn_in['bq'], 'L2_gnn_wk': _L2_gnn_in['wk'], 'L2_gnn_bk': _L2_gnn_in['bk'], 'L2_gnn_wv': _L2_gnn_in['wv'], 'L2_gnn_bv': _L2_gnn_in['bv'], 'L2_gnn_wo': _L2_gnn_in['wo'], 'L2_gnn_bo': _L2_gnn_in['bo'], 'L2_gnn_s2_w': _L2_gnn_in['s2_w'], 'L2_gnn_s2_b': _L2_gnn_in['s2_b'], 'L2_gnn_b2_w': _L2_gnn_in['b2_w'], 'L2_gnn_b2_b': _L2_gnn_in['b2_b'], 'L2_gnn_m_w1': _L2_gnn_in['m_w1'], 'L2_gnn_m_b1': _L2_gnn_in['m_b1'], 'L2_gnn_m_w2': _L2_gnn_in['m_w2'], 'L2_gnn_m_b2': _L2_gnn_in['m_b2'], 'L3_gnn_Wq': _L3_gnn_in['Wq'], 'L3_gnn_bq': _L3_gnn_in['bq'], 'L3_gnn_Wk': _L3_gnn_in['Wk'], 'L3_gnn_bk': _L3_gnn_in['bk'], 'L3_gnn_Wv': _L3_gnn_in['Wv'], 'L3_gnn_bv': _L3_gnn_in['bv'], 'L3_gnn_Ws': _L3_gnn_in['Ws'], 'L3_gnn_bs': _L3_gnn_in['bs'], 'L3_gnn_W1': _L3_gnn_in['W1'], 'L3_gnn_b1': _L3_gnn_in['b1'], 'L3_gnn_W2': _L3_gnn_in['W2'], 'L3_gnn_b2': _L3_gnn_in['b2'], 'L3_gnn_ln_g': _L3_gnn_in['ln_g'], 'L3_gnn_ln_b': _L3_gnn_in['ln_b']}

def reference(x, src, dst, edge_type_10, edge_weight, node_vec1, L0_gnn_W1, L0_gnn_b1, L0_gnn_W2, L0_gnn_b2, L1_gnn_W1, L1_gnn_b1, L1_gnn_W2, L1_gnn_b2, L2_gnn_f_w1, L2_gnn_f_b1, L2_gnn_f_w2, L2_gnn_f_b2, L2_gnn_s1_w, L2_gnn_s1_b, L2_gnn_b1_w, L2_gnn_b1_b, L2_gnn_wq, L2_gnn_bq, L2_gnn_wk, L2_gnn_bk, L2_gnn_wv, L2_gnn_bv, L2_gnn_wo, L2_gnn_bo, L2_gnn_s2_w, L2_gnn_s2_b, L2_gnn_b2_w, L2_gnn_b2_b, L2_gnn_m_w1, L2_gnn_m_b1, L2_gnn_m_w2, L2_gnn_m_b2, L3_gnn_Wq, L3_gnn_bq, L3_gnn_Wk, L3_gnn_bk, L3_gnn_Wv, L3_gnn_bv, L3_gnn_Ws, L3_gnn_bs, L3_gnn_W1, L3_gnn_b1, L3_gnn_W2, L3_gnn_b2, L3_gnn_ln_g, L3_gnn_ln_b):
    import jax
    import jax.numpy as jnp

    def _L0_gnn_ref(x, edge_index, W1, b1, W2, b2):
        import jax, jax.numpy as jnp
        import numpy as np
        N_NODES = 625
        eps = 0.0
        src, dst = (edge_index[0], edge_index[1])
        agg = jax.ops.segment_sum(x[src], dst, num_segments=N_NODES)
        h = (1.0 + eps) * x + agg
        h = jax.nn.relu(h @ W1 + b1)
        out = h @ W2 + b2
        return out

    def _L1_gnn_ref(x, edge_index, W1, b1, W2, b2):
        import jax, jax.numpy as jnp
        import numpy as np
        N = 50000
        E = 12500
        D_IN = 512
        D_HID = 64
        D_OUT = 512
        h = jax.nn.relu(x @ W1 + b1) @ W2 + b2
        row, col = (edge_index[0], edge_index[1])
        agg = jax.ops.segment_sum(h[col], row, num_segments=h.shape[0])
        return h + agg

    def _L2_gnn_ref(latent_mesh_nodes, edge_index, noise_levels, f_w1, f_b1, f_w2, f_b2, s1_w, s1_b, b1_w, b1_b, wq, bq, wk, bk, wv, bv, wo, bo, s2_w, s2_b, b2_w, b2_b, m_w1, m_b1, m_w2, m_b2):
        import jax, jax.numpy as jnp
        import numpy as np
        N_NODES = 40962
        LATENT_DIM = 512
        N_EDGES = 20481
        NUM_BLOCKS = 4
        NUM_HEADS = 4
        NUM_FREQ = 32
        BASE_PERIOD = 16
        NOISE_EMB_DIM = 16
        EPS = 1e-05

        def _cond_layer_norm(x, cond, sw, sb, bw, bb):
            mu = jnp.mean(x, axis=-1, keepdims=True)
            var = jnp.var(x, axis=-1, keepdims=True)
            xn = (x - mu) * jax.lax.rsqrt(var + EPS)
            scale = cond @ sw + sb
            bias = cond @ bw + bb
            return xn * (1.0 + scale) + bias

        def _sparse_attention(x, src, dst, wq, bq, wk, bk, wv, bv, wo, bo):
            N, D = x.shape
            H, Dh = (NUM_HEADS, D // NUM_HEADS)
            q = (x @ wq + bq).reshape(N, H, Dh) * Dh ** (-0.5)
            k = (x @ wk + bk).reshape(N, H, Dh)
            v = (x @ wv + bv).reshape(N, H, Dh)
            scores = jnp.einsum('ehd,ehd->eh', q[src], k[dst])
            smax = jax.ops.segment_max(scores, src, num_segments=N)
            ex = jnp.exp(scores - smax[src])
            denom = jax.ops.segment_sum(ex, src, num_segments=N)
            attn = ex / denom[src]
            out = jax.ops.segment_sum(attn[:, :, None] * v[dst], src, num_segments=N)
            return out.reshape(N, D) @ wo + bo

        def _forward(x, edge_index, noise_levels, f_w1, f_b1, f_w2, f_b2, s1_w, s1_b, b1_w, b1_b, wq, bq, wk, bk, wv, bv, wo, bo, s2_w, s2_b, b2_w, b2_b, m_w1, m_b1, m_w2, m_b2):
            src, dst = (edge_index[0], edge_index[1])
            freqs = jnp.arange(1, NUM_FREQ + 1, dtype=x.dtype) * (2.0 * np.pi / BASE_PERIOD)
            ph = noise_levels * freqs
            emb = jnp.concatenate([jnp.sin(ph), jnp.cos(ph)], axis=-1)
            cond = jax.nn.silu(emb @ f_w1 + f_b1) @ f_w2 + f_b2
            for i in range(NUM_BLOCKS):
                y = _cond_layer_norm(x, cond, s1_w[i], s1_b[i], b1_w[i], b1_b[i])
                y = _sparse_attention(y, src, dst, wq[i], bq[i], wk[i], bk[i], wv[i], bv[i], wo[i], bo[i])
                x = x + y
                y = _cond_layer_norm(x, cond, s2_w[i], s2_b[i], b2_w[i], b2_b[i])
                y = jax.nn.relu(y @ m_w1[i] + m_b1[i]) @ m_w2[i] + m_b2[i]
                x = x + y
            return x
        return _forward(latent_mesh_nodes, edge_index, noise_levels, f_w1, f_b1, f_w2, f_b2, s1_w, s1_b, b1_w, b1_b, wq, bq, wk, bk, wv, bv, wo, bo, s2_w, s2_b, b2_w, b2_b, m_w1, m_b1, m_w2, m_b2)

    def _L3_gnn_ref(x, edge_index, edge_type, edge_repre, Wq, bq, Wk, bk, Wv, bv, Ws, bs, W1, b1, W2, b2, ln_g, ln_b):
        import jax, jax.numpy as jnp
        import numpy as np
        N, E, H, D, C, L = (625, 10000, 8, 64, 512, 2)

        def layer_norm(x, g, b, eps=1e-05):
            mu = x.mean(-1, keepdims=True)
            var = ((x - mu) ** 2).mean(-1, keepdims=True)
            return (x - mu) / jnp.sqrt(var + eps) * g + b
        src, dst = (edge_index[0], edge_index[1])
        enc = x
        scale = 1.0 / jnp.sqrt(jnp.float32(D))
        for l in range(L):
            q = (x @ Wq[l] + bq[l]).reshape(N, H, D)
            k = (x @ Wk[l] + bk[l]).reshape(N, H, D)
            v = (x @ Wv[l] + bv[l]).reshape(N, H, D)
            a = (q[dst] * k[src]).sum(-1) * scale
            amax = jax.ops.segment_max(a, dst, num_segments=N)
            amax = jnp.where(jnp.isfinite(amax), amax, 0.0)
            e = jnp.exp(a - amax[dst])
            denom = jax.ops.segment_sum(e, dst, num_segments=N)
            alpha = e / (denom[dst] + 1e-16)
            agg = jax.ops.segment_sum(alpha[:, :, None] * v[src], dst, num_segments=N).reshape(N, C)
            x = agg + (x @ Ws[l] + bs[l]) + enc
        x = layer_norm(x, ln_g, ln_b)
        x = jax.nn.relu(x @ W1 + b1) @ W2 + b2 + x
        x = layer_norm(x, ln_g, ln_b)
        return x + enc
    edge_index = jnp.stack([src, dst])
    h = jnp.maximum(_layernorm(x, axis=-1), 0.0)
    x = x + _L0_gnn_ref(h, edge_index, L0_gnn_W1, L0_gnn_b1, L0_gnn_W2, L0_gnn_b2)
    h = jnp.maximum(_layernorm(x, axis=-1), 0.0)
    x = x + _L1_gnn_ref(h, edge_index, L1_gnn_W1, L1_gnn_b1, L1_gnn_W2, L1_gnn_b2)
    h = jnp.maximum(_layernorm(x, axis=-1), 0.0)
    x = x + _L2_gnn_ref(h, edge_index, node_vec1, L2_gnn_f_w1, L2_gnn_f_b1, L2_gnn_f_w2, L2_gnn_f_b2, L2_gnn_s1_w, L2_gnn_s1_b, L2_gnn_b1_w, L2_gnn_b1_b, L2_gnn_wq, L2_gnn_bq, L2_gnn_wk, L2_gnn_bk, L2_gnn_wv, L2_gnn_bv, L2_gnn_wo, L2_gnn_bo, L2_gnn_s2_w, L2_gnn_s2_b, L2_gnn_b2_w, L2_gnn_b2_b, L2_gnn_m_w1, L2_gnn_m_b1, L2_gnn_m_w2, L2_gnn_m_b2)
    h = jnp.maximum(_layernorm(x, axis=-1), 0.0)
    x = x + _L3_gnn_ref(h, edge_index, edge_type_10, edge_weight, L3_gnn_Wq, L3_gnn_bq, L3_gnn_Wk, L3_gnn_bk, L3_gnn_Wv, L3_gnn_bv, L3_gnn_Ws, L3_gnn_bs, L3_gnn_W1, L3_gnn_b1, L3_gnn_W2, L3_gnn_b2, L3_gnn_ln_g, L3_gnn_ln_b)
    return x

_drawn_inputs = setup_inputs


def setup_inputs(seed=0):
    import zlib

    import numpy as np

    out = dict(_drawn_inputs(seed))
    spreads = {'L1_gnn_b1': (0.0, 0.1),
     'L1_gnn_b2': (0.0, 0.1),
     'L2_gnn_f_b1': (0.0, 2.0),
     'L2_gnn_f_b2': (0.0, 0.8),
     'L2_gnn_s1_b': (0.0, 2.0),
     'L2_gnn_b1_b': (0.0, 2.0),
     'L2_gnn_bq': (0.0, 2.0),
     'L2_gnn_bk': (0.0, 2.0),
     'L2_gnn_bv': (0.0, 0.8),
     'L2_gnn_bo': (0.0, 0.494),
     'L2_gnn_s2_b': (0.0, 0.8),
     'L2_gnn_b2_b': (0.0, 0.8),
     'L2_gnn_m_b1': (0.0, 0.8),
     'L2_gnn_m_b2': (0.0, 0.5),
     'L3_gnn_bq': (0.0, 2.0),
     'L3_gnn_bk': (0.0, 2.0),
     'L3_gnn_bv': (0.0, 0.777),
     'L3_gnn_bs': (0.0, 0.692),
     'L3_gnn_b1': (0.0, 2.0),
     'L3_gnn_b2': (0.0, 2.0),
     'L3_gnn_ln_g': (1.0, 0.566),
     'L3_gnn_ln_b': (0.0, 0.622)}
    factors = {'node_vec1': 8.0,
     'L0_gnn_b1': 8.0,
     'L0_gnn_b2': 6.649,
     'L2_gnn_f_w1': 8.0,
     'L2_gnn_f_w2': 8.0,
     'L2_gnn_s1_w': 8.0,
     'L2_gnn_b1_w': 8.0,
     'L2_gnn_wq': 33.171,
     'L2_gnn_wk': 38.415,
     'L2_gnn_s2_w': 8.0,
     'L2_gnn_b2_w': 8.0,
     'L2_gnn_m_w1': 3.153,
     'L3_gnn_Wq': 64.0,
     'L3_gnn_Wk': 64.0,
     'L3_gnn_W1': 4.902,
     'L3_gnn_W2': 3.824}
    for name, (base, spread) in spreads.items():
        noise = np.random.default_rng([zlib.crc32(name.encode()), seed]).standard_normal(out[name].shape)
        drawn = base * np.exp(spread * noise) if base else spread * noise
        out[name] = jnp.asarray(drawn.astype(out[name].dtype))
    for name, factor in factors.items():
        out[name] = (out[name] * factor).astype(out[name].dtype)
    return out
```

```python
from contextlib import ExitStack

import concourse.bass as bass
import numpy as np
from concourse import mybir

FP32, F32R = mybir.dt.float32, mybir.dt.float32r
BF16, FP16, I32 = mybir.dt.bfloat16, mybir.dt.float16, mybir.dt.int32
ALU = mybir.AluOpType
ACT = mybir.ActivationFunctionType

N, D, E = 625, 512, 20000
TILES, R = 5, 125
C = D // 128
H2 = 314
W = 2 * H2
SLOTS = 4
PASSES = ((0, 0), (0, 1), (1, 0))
NOEDGE = -1.0e30
EPS = 1e-5
BLOCKS, HEADS2 = 4, 4
LAYERS, HEADS3 = 2, 8
SCALE2, SCALE3 = float(np.sqrt(D // HEADS2)), float(np.sqrt(D // HEADS3))
HID = 64
RING_P = 5
LAG = 3
SMALL_RING = 8
COND = 16
ET = E // R
CHUNKS = 5
CT = ET // CHUNKS
PACK = 4096.0

ROUND = 1.5 * 2 ** 23


class Jobs:

    def __init__(self, ring, names, times=1):
        self.filled, self.drained, counts = ring
        self.at = {n: (i % SLOTS, i // SLOTS) for i, n in enumerate(names)}
        assert len(self.at) == len(names)
        self.before = list(counts)
        self.uses = [sum(i % SLOTS == s for i in range(len(names))) for s in range(SLOTS)]
        counts[:] = [b + times * n for b, n in zip(counts, self.uses)]

    def count(self, name, it):
        s, k = self.at[name]
        return it * self.uses[s] + (self.before[s] + k)

    def wait_filled(self, eng, name, it=0):
        s = self.at[name][0]
        eng.wait_ge(self.filled[s], self.count(name, it) + 1)
        return s

    def wait_drained(self, eng, name, it=0):
        eng.wait_ge(self.drained[self.at[name][0]], self.count(name, it) + 1)

    def acquire(self, eng, name, it=0):
        n = self.count(name, it)
        if not isinstance(n, int) or n > 0:
            eng.wait_ge(self.drained[self.at[name][0]], n)
        return self.at[name][0]


class Steps:

    def __init__(self, sem, per_body=0):
        self.sem, self.per_body, self.n, self.it = sem, per_body, 0, 0

    def body(self, it):
        assert isinstance(it, int) and it == 0 or self.n in (0, self.per_body), (self.sem, self.n)
        self.it, self.n = it, 0

    def done(self, ins):
        ins.then_inc(self.sem, 1)
        self.n += 1

    def wait(self, eng):
        eng.wait_ge(self.sem, self.it * self.per_body + self.n)

    def end(self):
        assert self.n == self.per_body, (self.n, self.per_body)


def halves(ap):
    return ap.rearrange("p (a b) -> p a b", a=2)


def attention_jobs(heads, spot1, spot2):
    names = []
    for h in range(heads):
        for t in range(TILES):
            names.append(f"s{h}_{t}")
            u = h * TILES + t - LAG
            if u >= 0:
                names.append(f"t{u // TILES}_{u % TILES}")
            if u >= 0 and u % TILES == TILES - 1:
                names += spot1(h)
                names.append(f"pv{u // TILES}")
            if t == TILES - 2:
                names += spot2(h)
    for u in range(heads * TILES - LAG, heads * TILES):
        names.append(f"t{u // TILES}_{u % TILES}")
    return names + [f"pv{heads - 1}"]


def build(nc, a, out):
    sizes = dict(res=10240, mask=12576, w0=16384, w1=16384, w2=16384, yt=20480, qk=20096, v=20480,
                 p=12576, pt=25120, ot=20096, ws=8192, cond=2528, rows=6144, small=4096)
    origin, at = (nc.sbuf_base + 31) // 32 * 32, {}
    for name, size in sizes.items():
        at[name] = origin
        origin += size
    assert origin <= nc.sbuf_usable_end, (origin, nc.sbuf_usable_end)

    def sb(name, region, shape, dtype=FP32, skip=0):
        return nc.alloc_sbuf_tensor_at(name, shape, dtype, offset=at[region] + skip, align_bytes=16)

    small_used = [0]

    def small(name, shape, dtype=FP32):
        t = sb(name, "small", shape, dtype, small_used[0])
        small_used[0] += (int(np.prod(shape[1:])) * 4 + 31) // 32 * 32
        assert small_used[0] <= sizes["small"], small_used
        return t

    def pair(name, region, shape, skip=0):
        size = int(np.prod(shape[1:])) * 4
        return [sb(name + "_hi", region, shape, F32R, skip), sb(name + "_lo", region, shape, F32R, skip + size)]

    ps = [nc.alloc_psum_tensor(f"ps{s}", [128, 1024], FP32) for s in range(SLOTS)]

    def wide(s, p0=0, p1=128):
        return ps[s][p0:p1, :].rearrange("p (a b) -> p a b", a=2)[:, :, 0:H2]

    def blocks(s, n, p=128):
        return ps[s][0:p, 0:128 * n].rearrange("p (a b) -> p a b", a=n)[:, :, 0:R]

    res = sb("res", "res", [R, TILES, D])
    mask = sb("mask", "mask", [R, TILES, W])
    x = sb("x", "v", [R, TILES, D])
    x_spill = nc.dram_tensor("x_spill", [R, TILES, D], FP32, kind="Internal").ap()
    mask_spill = nc.dram_tensor("mask_spill", [R, TILES, W], FP32, kind="Internal").ap()
    w_raw = [sb(f"w{s}_raw", f"w{s}", [128, C, D], FP32, C * D * 4) for s in range(3)]
    w = [pair(f"w{s}", f"w{s}", [128, C, D]) for s in range(3)]
    ident = small("ident", [128, 128])
    stats = small("stats", [R, TILES, 6])
    mv = small("mv", [R, TILES, 2])
    rstd = small("rstd", [R, TILES])
    nmr = small("nmr", [R, TILES])
    neg_half = small("neg_half", [R, 1])
    low = small("low", [R, SMALL_RING])
    denom = small("denom", [R, SMALL_RING])
    rinv = small("rinv", [R, SMALL_RING])
    b0c = small("b0c", [128, C])
    bq2 = small("bq2", [128, BLOCKS * C])
    bk2 = small("bk2", [128, BLOCKS * C])
    bm2 = small("bm2", [128, BLOCKS * C])
    bq3 = small("bq3", [128, LAYERS * C])
    bk3 = small("bk3", [128, LAYERS * C])
    bs3 = small("bs3", [128, LAYERS * C])
    b1c3 = small("b1c3", [128, 2 * C])
    xn = sb("xn", "p", [R, 2, D])
    y1 = sb("y1", "p", [R, D], skip=2 * D * 4)
    y2 = sb("y2", "p", [R, 2, D], skip=3 * D * 4)
    vtmp = sb("vtmp", "ot", [R, 2, D])
    ftmp = sb("ftmp", "p", [128, 2, W])
    prob = sb("prob", "p", [R, RING_P, W])
    yt = pair("yt", "yt", [128, C, W])
    q = [pair(f"q{n}", "qk", [128, W], 2 * n * W * 4) for n in range(2)]
    k = [pair(f"k{n}", "qk", [128, W], (4 + 2 * n) * W * 4) for n in range(2)]
    v = pair("v", "v", [R, TILES, D])
    ht = pair("ht", "v", [128, C, W])
    pt = pair("pt", "pt", [R, TILES, W])
    ot = pair("ot", "ot", [128, C, W])
    rows = [sb(f"row{n}", "rows", [R, D], FP32, n * D * 4) for n in range(3)]
    cond = sb("cond", "cond", [128, W], F32R)
    ws_raw = sb("ws_raw", "ws", [128, 2, D])
    ws = sb("ws", "ws", [128, 2, D], F32R, 2 * D * 4)

    def sem(name):
        return nc.alloc_semaphore(name)

    def row(ap):
        return ap.rearrange("(a n) -> a n", a=1).to_broadcast([R, D])

    s_own = sem("waits_of_their_own")

    def own(eng):
        eng.sem_inc(s_own, 1)

    def matmul3(pe, out_ap, lhs, rhs, count, last=None):
        for kk in range(count):
            for n, (i, j) in enumerate(PASSES):
                ins = pe.matmul(out_ap, lhs(i, kk), rhs(j, kk), start=kk == 0 and n == 0,
                                stop=kk == count - 1 and n == 2)
        return ins

    def pe_wide(pe, jobs, name, it, lhs, rhs, count, m=128):
        s = jobs.acquire(pe, name, it)
        for half in range(2):
            ins = matmul3(pe, ps[s][0:m, 512 * half:512 * half + H2], lhs,
                          lambda j, kk: rhs(j, kk)[:, H2 * half:H2 * half + H2], count)
        ins.then_inc(jobs.filled[s], 1)

    def pe_natural(pe, jobs, name, it, lhs, rhs, count):
        s = jobs.acquire(pe, name, it)
        matmul3(pe, ps[s][0:R, 0:D], lhs, rhs, count).then_inc(jobs.filled[s], 1)

    def pe_transposes(pe, jobs, name, it, source, count, rows_in, rows_out):
        s = jobs.acquire(pe, name, it)
        for b in range(count):
            ins = pe.transpose(ps[s][0:rows_out, 128 * b:128 * b + rows_in], source(b),
                               ident[0:rows_in, 0:rows_in])
        ins.then_inc(jobs.filled[s], 1)

    def t_slice(t):
        return slice(t * R, (t + 1) * R)

    def proj(weights, act):
        return (lambda c: (lambda i, kk: weights[i][:, kk, c * 128:(c + 1) * 128])), (lambda j, kk: act[j][:, kk, :])

    def split_weights(pool, steps, slot, split_sem, pieces=range(C), cols=D):
        for kk in pieces:
            own(pool)
            steps.done(pool.tensor_scalar(w[slot][0][:, kk, 0:cols], w_raw[slot][:, kk, 0:cols], 1.0, 1.0,
                                          ALU.mult, ALU.mult))
            steps.wait(pool)
            pool.tensor_tensor(w[slot][1][:, kk, 0:cols], w_raw[slot][:, kk, 0:cols],
                               w[slot][0][:, kk, 0:cols].bitcast(FP32), ALU.subtract).then_inc(split_sem, 1)

    def dve_stats(dve, steps, t, source, stats_done):
        steps.done(dve.bn_stats(stats[:, t, :], source))
        steps.wait(dve)
        own(dve)
        dve.bn_aggr(mv[:, t, :], stats[:, t, :]).then_inc(stats_done, 1)

    def pool_rstd(pool, steps, t, rstd_done):
        own(pool)
        steps.done(pool.tensor_scalar(rstd[:, t:t + 1], mv[:, t, 1:2], EPS, 1.0, ALU.add, ALU.mult))
        steps.wait(pool)
        steps.done(pool.tensor_tensor(rstd[:, t:t + 1], rstd[:, t:t + 1], neg_half[:, :], ALU.pow))
        steps.wait(pool)
        own(pool)
        pool.tensor_scalar(nmr[:, t:t + 1], mv[:, t, 0:1], rstd[:, t:t + 1], -1.0, ALU.mult,
                           ALU.mult).then_inc(rstd_done, 1)

    def act_hi(act, jobs, name, it, out_ap, in_ap, hi_done, bias=0.0):
        jobs.wait_filled(act, name, it)
        act.activation(out_ap, in_ap, ACT.Identity, bias=bias).then_inc(hi_done, 1)

    def pe_scores(pe, jobs, h, t, it, qs, ks, r0, r1):
        pe_wide(pe, jobs, f"s{h}_{t}", it, lambda i, kk: qs[i][r0:r1, t_slice(t)], lambda j, kk: ks[j][r0:r1, :], 1, R)

    def pe_prob_transposes(pe, jobs, u, it, units, scaled):
        pe.wait_ge(scaled, it * units + u + 1)
        pe_transposes(pe, jobs, f"t{u // TILES}_{u % TILES}", it,
                      lambda b: prob[:, u % RING_P, b * R:(b + 1) * R], TILES, R, R)

    def pe_values(pe, jobs, h, c, it):
        jobs.wait_drained(pe, f"t{h}_{TILES - 1}", it)
        pe_wide(pe, jobs, f"pv{h}", it, lambda i, kk: v[i][:, kk, c * 128:(c + 1) * 128],
                lambda j, kk: pt[j][:, kk, :], TILES)

    def dve_scores(dve, jobs, u, it, scale):
        name = f"s{u // TILES}_{u % TILES}"
        s = jobs.wait_filled(dve, name, it)
        o = u % SMALL_RING
        own(dve)
        dve.tensor_tensor_reduce(out=halves(prob[:, u % RING_P, :]), in0=wide(s, 0, R),
                                 in1=halves(mask[:, u % TILES, :]), scale=-scale, scalar=1e20, op0=ALU.add,
                                 op1=ALU.min, accum_out=low[:, o:o + 1]).then_inc(jobs.drained[s], 1)

    def act_exp(act, jobs, u, it, exp_done):
        jobs.wait_drained(act, f"s{u // TILES}_{u % TILES}", it)
        o = u % SMALL_RING
        act.activation(prob[:, u % RING_P, :], prob[:, u % RING_P, :], ACT.Exp, bias=low[:, o:o + 1], scale=-1.0,
                       accum_out=denom[:, o:o + 1]).then_inc(exp_done, 1)

    def dve_inverse(dve, steps, u, it, units, exp_done, rinv_done):
        dve.wait_ge(exp_done, it * units + u + 1)
        o = u % SMALL_RING
        steps.done(dve.tensor_scalar(rinv[:, o:o + 1], denom[:, o:o + 1], 1e-16, None, ALU.add))
        steps.wait(dve)
        dve.reciprocal(rinv[:, o:o + 1], rinv[:, o:o + 1]).then_inc(rinv_done, 1)

    def pool_scale(pool, u, it, units, rinv_done, scaled):
        pool.wait_ge(rinv_done, it * units + u + 1)
        o = u % SMALL_RING
        own(pool)
        pool.tensor_scalar(prob[:, u % RING_P, :], prob[:, u % RING_P, :], rinv[:, o:o + 1], 1.0, ALU.mult,
                           ALU.mult).then_inc(scaled, 1)

    def pt_view(part, t):
        return pt[part][:, :, t_slice(t)]

    cnt = sb("cnt", "p", [R, TILES, W])
    ids = [sb(n, "rows", [R, ET], I32, skip) for n, skip in (("dst_i", 0), ("src_i", 640))]
    dstf = sb("dstf", "rows", [R, ET], FP32, 1280)
    srcf = sb("srcf", "rows", [R, ET], FP32, 1920)
    srcm = sb("srcm", "rows", [R, ET], FP32, 2560)
    srcv = sb("srcv", "rows", [R, ET], FP32, 3200)
    upper = sb("upper", "rows", [R, ET], FP32, 3840)
    node = sb("node", "qk", [R, W], FP16)
    OH = 4
    oh_d = sb("oh_d", "qk", [R, OH, W], BF16, 1280)
    oh_s = sb("oh_s", "qk", [R, OH, H2], BF16, 1280 + OH * W * 2)
    above = sb("above", "ws", [R, 2, H2])
    below = sb("below", "ws", [R, 2, H2], FP32, 2 * H2 * 4)
    quotient = sb("quotient", "cond", [R, H2])
    h_pair = pair("h", "yt", [R, TILES, D])

    def bank(n, cols=H2):
        return ps[n // 2][0:R, 512 * (n % 2):512 * (n % 2) + cols]

    s_ids, s_x, s_node, s_idf = sem("ids_loaded"), sem("x_loaded"), sem("node_made"), sem("ids_ready")
    s_wl = [sem(f"w{n}_loaded") for n in range(3)]
    s_small = sem("columns_loaded")
    s_oh, s_ohu = sem("onehots_ready"), sem("onehots_used")
    s_cf, s_unp = sem("counts_filled"), sem("counts_unpacked")
    s_added, s_zero = sem("counts_added"), sem("counts_zeroed")
    s_st, s_rs, s_hn, s_hh, s_hl = sem("a_stats"), sem("a_rstd"), sem("a_norm"), sem("a_hhi"), sem("a_hlo")
    s_pa, s_va = sem("a_pool_steps"), sem("a_dve_steps")
    s_ws0 = [sem(f"l0_w{n}_split") for n in range(3)]

    def column(dst, src):
        return dst, src

    with nc.Block() as block:
        @block.sync
        def _(sp):
            sp.dma_start(ids[0][:], a["dst"].rearrange("(p t) -> p t", t=ET)).then_inc(s_ids, 16)
            sp.dma_start(ids[1][:], a["src"].rearrange("(p t) -> p t", t=ET)).then_inc(s_ids, 16)
            sp.dma_start(x[:], a["x"].rearrange("(t p) f -> p t f", p=R)).then_inc(s_x, 16)
            for n, name in enumerate(("L0_gnn_W1", "L0_gnn_W2")):
                sp.dma_start(w_raw[n][:], a[name].rearrange("(c p) n -> p c n", p=128)).then_inc(s_wl[n], 16)
            with nc.allow_non_contiguous_dma("bias columns"):
                for dst, name, pat in ((b0c, "L0_gnn_b1", 1), (bq2, "L2_gnn_bq", 2), (bk2, "L2_gnn_bk", 2),
                                       (bm2, "L2_gnn_m_b1", 2), (bq3, "L3_gnn_bq", 2), (bk3, "L3_gnn_bk", 2),
                                       (bs3, "L3_gnn_bs", 2), (b1c3, "L3_gnn_b1", 1)):
                    src = a[name] if pat == 1 else a[name].rearrange("b n -> (b n)")
                    sp.dma_start(dst[:], src.rearrange("(c p) -> p c", p=128)).then_inc(s_small, 16)
            sp.wait_ge(s_small, 8 * 16)

        @block.gpsimd
        def _(pool):
            steps = Steps(s_pa)
            pool.iota(node[:], [[1, W]], base=0, channel_multiplier=0,
                      allow_small_or_imprecise_dtypes=True).then_inc(s_node, 1)
            steps.done(pool.memset(ident[:], 0.0))
            pool.memset(cnt[:], 0.0).then_inc(s_zero, 1)
            steps.wait(pool)
            steps.done(pool.affine_select(out=ident[:], in_=ident[:], compare_op=ALU.not_equal, fill=1.0, base=0,
                                          pattern=[[-1, 128]], channel_multiplier=1))
            steps.done(pool.memset(neg_half[:], -0.5))
            steps.wait(pool)

            def add(c):
                for m in range(TILES):
                    n = c * TILES + m
                    pool.wait_ge(s_unp, 2 * n + 2)
                    pool.wait_ge(s_zero if n < TILES else s_added, 1 if n < TILES else 2 * (n - TILES) + 2)
                    pool.tensor_tensor(cnt[:, m, 0:H2], cnt[:, m, 0:H2], below[:, n % 2, :],
                                       ALU.add).then_inc(s_added, 1)
                    pool.tensor_tensor(cnt[:, m, H2:W], cnt[:, m, H2:W], above[:, n % 2, :],
                                       ALU.add).then_inc(s_added, 1)

            for t in range(TILES):
                pool.wait_ge(s_st, t + 1)
                pool_rstd(pool, steps, t, s_rs)
            for c in range(CHUNKS):
                add(c)
                if c < 2:
                    pool.wait_ge(s_wl[c], 16)
                    split_weights(pool, steps, c, s_ws0[c])
            pool.wait_ge(s_added, 2 * CHUNKS * TILES)
            for m in range(TILES):
                block_m = cnt[:, m, t_slice(m)]
                steps.done(pool.tensor_tensor(block_m, block_m, ident[0:R, 0:R], ALU.add))
            steps.wait(pool)

        @block.vector
        def _(dve):
            steps = Steps(s_va)
            dve.wait_ge(s_ids, 32)
            dve.tensor_copy(dstf[:], ids[0][:]).then_inc(s_idf, 1)
            steps.done(dve.tensor_copy(srcf[:], ids[1][:]))
            steps.wait(dve)
            steps.done(dve.tensor_scalar(upper[:], srcf[:], float(H2), None, ALU.is_ge))
            steps.wait(dve)
            dve.tensor_scalar(srcv[:], upper[:], PACK - 1, 1.0, ALU.mult, ALU.add).then_inc(s_idf, 1)
            dve.scalar_tensor_tensor(out=srcm[:], in0=upper[:], scalar=-float(H2), in1=srcf[:], op0=ALU.mult,
                                     op1=ALU.add).then_inc(s_idf, 1)
            dve.wait_ge(s_idf, 3)
            dve.wait_ge(s_node, 1)

            def onehots(tile, o, first):
                if not first:
                    dve.wait_ge(s_ohu, tile - OH + 1)
                dve.tensor_scalar(oh_d[:, o, :], node[:], dstf[:, bass.ds(tile, 1)], None,
                                  ALU.is_equal).then_inc(s_oh, 1)
                dve.tensor_scalar(oh_s[:, o, :], node[:, 0:H2], srcm[:, bass.ds(tile, 1)],
                                  srcv[:, bass.ds(tile, 1)], ALU.is_equal, ALU.mult).then_inc(s_oh, 1)

            def unpack(c):
                for m in range(TILES):
                    n = c * TILES + m
                    b = n % 8
                    dve.wait_ge(s_cf, c + 1)
                    if n >= 2:
                        dve.wait_ge(s_added, 2 * (n - 2) + 2)
                    steps.done(dve.tensor_scalar(quotient[:], bank(b), -2001.0, 1 / PACK, ALU.add, ALU.mult))
                    steps.wait(dve)
                    dve.tensor_scalar(above[:, n % 2, :], quotient[:], ROUND, -ROUND, ALU.add,
                                      ALU.add).then_inc(s_unp, 1)
                    dve.wait_ge(s_unp, 2 * n + 1)
                    dve.scalar_tensor_tensor(out=below[:, n % 2, :], in0=above[:, n % 2, :], scalar=-PACK,
                                             in1=bank(b), op0=ALU.mult, op1=ALU.add).then_inc(s_unp, 1)

            for c in range(CHUNKS):
                for o in range(OH):
                    onehots(c * CT + o, o, c == 0)
                if c > 0:
                    unpack(c - 1)
                else:
                    dve.wait_ge(s_x, 16)
                    for t in range(TILES):
                        dve_stats(dve, steps, t, x[:, t, :], s_st)
                with dve.Fori(1, CT // OH) as j:
                    for o in range(OH):
                        onehots(j * OH + (c * CT + o), o, False)
                if c == 1:
                    for t in range(TILES):
                        dve.wait_ge(s_hh, t + 1)
                        dve.tensor_tensor(h_pair[1][:, t, :], res[:, t, :], h_pair[0][:, t, :].bitcast(FP32),
                                          ALU.subtract).then_inc(s_hl, 1)
            unpack(CHUNKS - 1)

        @block.scalar
        def _(act):
            act.wait_ge(s_x, 16)
            for t in range(TILES):
                act.wait_ge(s_rs, t + 1)
                act.activation(res[:, t, :], x[:, t, :], ACT.Relu, bias=nmr[:, t:t + 1],
                               scale=rstd[:, t:t + 1]).then_inc(s_hn, 1)
                act.wait_ge(s_hn, t + 1)
                act.activation(h_pair[0][:, t, :], res[:, t, :], ACT.Copy).then_inc(s_hh, 1)

        @block.tensor
        def _(pe):
            def edge_tile(c, tile, o, start, stop):
                pe.wait_ge(s_oh, 2 * tile + 2)
                for m in range(TILES):
                    ins = pe.matmul(bank((c * TILES + m) % 8), oh_d[:, o, t_slice(m)], oh_s[:, o, :], start=start,
                                    stop=stop)
                ins.then_inc(s_ohu, 1)
                return ins

            for c in range(CHUNKS):
                if c > 0:
                    pe.wait_ge(s_unp, 2 * min(c * TILES, max(0, (c + 1) * TILES - 8)))
                for o in range(OH):
                    edge_tile(c, c * CT + o, o, o == 0, False)
                with pe.Fori(1, CT // OH - 1) as j:
                    for o in range(OH):
                        edge_tile(c, j * OH + (c * CT + o), o, False, False)
                for o in range(OH):
                    ins = edge_tile(c, c * CT + CT - OH + o, o, False, o == OH - 1)
                pe.wait_ge(s_ohu, (c + 1) * CT)
                pe.sem_inc(s_cf, 1)

    bi = pair("bi", "pt", [R, TILES, W])
    ai = pair("ai", "ot", [R, TILES, W])
    agg = pair("agg", "qk", [128, C, W])
    ft = pair("ft", "yt", [128, C, W])
    rtmp = sb("rtmp", "rows", [128, 2, W])
    b2row = sb("b2row", "cond", [R, D])
    ht1 = pair("ht1", "qk", [128, C, W])
    r_sum = sb("r_sum", "cond", [R, TILES, HID])
    r_nat = pair("r_nat", "yt", [R, TILES, 128])
    r_act = sb("r_act", "yt", [R, TILES, HID], FP32, 2 * TILES * 128 * 4)
    b1row = sb("b1row", "yt", [R, HID], FP32, 2 * TILES * 128 * 4 + TILES * HID * 4)
    gt = pair("gt", "rows", [128, W])
    W2COL = 4 * HID
    w_l1 = [t[:].rearrange("p c n -> p (c n)") for t in (w_raw[2], w[2][0], w[2][1])]

    names = [f"b{t}" for t in range(TILES)] + [f"g{c}" for c in range(C)] + [f"f{c}" for c in range(C)]
    names += [f"o{t}" for t in range(TILES)] + [f"y{t}" for t in range(TILES)] + ["r", "ga"]
    names += [f"p{t}" for t in range(TILES)]
    ring = ([sem(f"slot{s}_filled") for s in range(SLOTS)], [sem(f"slot{s}_drained") for s in range(SLOTS)], [0] * SLOTS)
    jobs = Jobs(ring, names)
    s_hi, s_ai, s_relu, s_fd = sem("g_hi"), sem("g_ai_split"), sem("g_relu"), sem("g_f_split")
    s_row, s_xb, s_st, s_rs, s_hn = sem("g_rows"), sem("g_bias_added"), sem("g_stats"), sem("g_rstd"), sem("g_norm")
    s_pg, s_vg, s_w2, s_r, s_pad, s_w2z = (sem("g_pool_steps"), sem("g_dve_steps"), sem("g_w2_split"),
                                           sem("g_r_split"), sem("g_pads"), sem("g_w2_zeroed"))
    s_r1 = sem("g_b1row")

    with nc.Block() as block:
        @block.sync
        def _(sp):
            sp.dma_start(b2row[:], row(a["L0_gnn_b2"])).then_inc(s_row, 16)
            sp.wait_ge(s_w2z, 1)
            sp.dma_start(w_raw[2][:].rearrange("p c n -> p (c n)")[:, 0:W2COL].rearrange("p (c n) -> p c n", c=C),
                         a["L1_gnn_W1"].rearrange("(c p) n -> p c n", p=128)).then_inc(s_wl[2], 16)
            sp.dma_start(w_l1[0][0:HID, W2COL:W2COL + D], a["L1_gnn_W2"]).then_inc(s_wl[2], 16)
            sp.dma_start(w_l1[0][HID:HID + 1, W2COL:W2COL + D],
                         a["L1_gnn_b2"].rearrange("(a n) -> a n", a=1)).then_inc(s_wl[2], 16)
            jobs.wait_filled(sp, f"o{TILES - 1}")
            sp.dma_start(b1row[:], a["L1_gnn_b1"].rearrange("(a n) -> a n", a=1).to_broadcast([R, HID])).then_inc(s_r1, 16)

        @block.gpsimd
        def _(pool):
            steps = Steps(s_pg)
            pool.memset(w_l1[0][:, W2COL:W2COL + D], 0.0).then_inc(s_w2z, 1)
            pool.memset(mask[:, :, N:W], 0.0).then_inc(s_pad, 1)
            pool.memset(bi[0][:, :, N:W].bitcast(FP32), 0.0).then_inc(s_pad, 1)
            pool.memset(bi[1][:, :, N:W].bitcast(FP32), 0.0).then_inc(s_pad, 1)
            for t in range(TILES):
                steps.done(pool.tensor_scalar(ai[0][:, t, :], cnt[:, t, :], 1.0, 1.0, ALU.mult, ALU.mult))
                steps.wait(pool)
                pool.tensor_tensor(ai[1][:, t, :], cnt[:, t, :], ai[0][:, t, :].bitcast(FP32),
                                   ALU.subtract).then_inc(s_ai, 1)
            pool.wait_ge(s_row, 16)
            for t in range(TILES):
                pool.tensor_tensor(x[:, t, :], x[:, t, :], b2row[:], ALU.add).then_inc(s_xb, 1)
            pool.wait_ge(s_wl[2], 48)
            steps.done(pool.tensor_scalar(w_l1[1][:, 0:W2COL + D], w_l1[0][:, 0:W2COL + D], 1.0, 1.0, ALU.mult,
                                          ALU.mult))
            steps.wait(pool)
            pool.tensor_tensor(w_l1[2][:, 0:W2COL + D], w_l1[0][:, 0:W2COL + D],
                               w_l1[1][:, 0:W2COL + D].bitcast(FP32), ALU.subtract).then_inc(s_w2, 1)
            for t in range(TILES):
                pool.wait_ge(s_st, t + 1)
                pool_rstd(pool, steps, t, s_rs)
            jobs.wait_filled(pool, f"y{TILES - 1}")
            pool.memset(r_nat[0][:].bitcast(FP32), 0.0).then_inc(s_pad, 1)
            pool.memset(r_nat[1][:].bitcast(FP32), 0.0).then_inc(s_pad, 1)
            pool.wait_ge(s_pad, 5)
            pool.memset(r_nat[0][:, :, HID:HID + 1].bitcast(FP32), 1.0).then_inc(s_pad, 1)

        @block.scalar
        def _(act):
            act.wait_ge(s_pad, 3)
            for t in range(TILES):
                s = jobs.wait_filled(act, f"b{t}")
                act.activation(mask[:, t, 0:N].rearrange("p (a b) -> p a b", a=TILES), blocks(s, TILES, R),
                               ACT.Copy).then_inc(s_hn, 1)
                act.activation(bi[0][:, t, 0:N].rearrange("p (a b) -> p a b", a=TILES), blocks(s, TILES, R),
                               ACT.Copy).then_inc(s_hi, 1)
            for c in range(C):
                s = jobs.at[f"g{c}"][0]
                act_hi(act, jobs, f"g{c}", 0, halves(agg[0][:, c, :]), wide(s), s_hi)
            for c in range(C):
                s = jobs.wait_filled(act, f"f{c}")
                if c >= 2:
                    act.wait_ge(s_fd, c - 1)
                act.activation(halves(rtmp[:, c % 2, :]), wide(s), ACT.Relu,
                               bias=b0c[:, c:c + 1]).then_inc(jobs.drained[s], 1)
            for t in range(TILES):
                act.wait_ge(s_rs, t + 1)
                act.activation(res[:, t, :], x[:, t, :], ACT.Relu, bias=nmr[:, t:t + 1],
                               scale=rstd[:, t:t + 1]).then_inc(s_hn, 1)
                s = jobs.at[f"y{t}"][0]
                act_hi(act, jobs, f"y{t}", 0, ht1[0][:, :, t_slice(t)], blocks(s, C), s_hi)
            s = jobs.at["ga"][0]
            act_hi(act, jobs, "ga", 0, halves(gt[0][:]), wide(s), s_hi)

        @block.vector
        def _(dve):
            steps = Steps(s_vg)
            hi = 0

            def lo(name, out_ap, in_ap, hi_ap):
                nonlocal hi
                hi += 1
                dve.wait_ge(s_hi, hi)
                s = jobs.at[name][0]
                dve.tensor_tensor(out_ap, in_ap(s), hi_ap.bitcast(FP32), ALU.subtract).then_inc(jobs.drained[s], 1)

            dve.wait_ge(s_pad, 3)
            for t in range(TILES):
                five = lambda ap: ap[:, t, 0:N].rearrange("p (a b) -> p a b", a=TILES)
                lo(f"b{t}", five(bi[1]), lambda s: blocks(s, TILES, R), five(bi[0]))
            for c in range(C):
                lo(f"g{c}", halves(agg[1][:, c, :]), wide, halves(agg[0][:, c, :]))
            for c in range(C):
                jobs.wait_drained(dve, f"f{c}")
                steps.done(dve.tensor_copy(ft[0][:, c, :], rtmp[:, c % 2, :]))
                steps.wait(dve)
                dve.tensor_tensor(ft[1][:, c, :], rtmp[:, c % 2, :], ft[0][:, c, :].bitcast(FP32),
                                  ALU.subtract).then_inc(s_fd, 1)
            dve.wait_ge(s_xb, TILES)

            def residual(name, t):
                s = jobs.wait_filled(dve, name)
                dve.tensor_tensor(x[:, t, :], ps[s][0:R, 0:D], x[:, t, :], ALU.add).then_inc(jobs.drained[s], 1)

            for t in range(TILES):
                residual(f"o{t}", t)
                jobs.wait_drained(dve, f"o{t}")
                dve_stats(dve, steps, t, x[:, t, :], s_st)
            for t in range(TILES):
                lo(f"y{t}", ht1[1][:, :, t_slice(t)], lambda s: blocks(s, C), ht1[0][:, :, t_slice(t)])
            s = jobs.wait_filled(dve, "r")
            dve.wait_ge(s_r1, 16)
            dve.wait_ge(s_pad, 6)
            dve.tensor_tensor(r_sum[:], ps[s][0:R, 0:TILES * HID].rearrange("p (a b) -> p a b", a=TILES),
                              b1row[:].rearrange("p (a b) -> p a b", a=1).to_broadcast([R, TILES, HID]),
                              ALU.add).then_inc(jobs.drained[s], 1)
            jobs.wait_drained(dve, "r")
            steps.done(dve.tensor_scalar(r_act[:], r_sum[:], 0.0, None, ALU.max))
            steps.wait(dve)
            steps.done(dve.tensor_copy(r_nat[0][:, :, 0:HID], r_act[:]))
            steps.wait(dve)
            dve.tensor_tensor(r_nat[1][:, :, 0:HID], r_act[:], r_nat[0][:, :, 0:HID].bitcast(FP32),
                              ALU.subtract).then_inc(s_r, 1)
            lo("ga", halves(gt[1][:]), wide, halves(gt[0][:]))
            for t in range(TILES):
                residual(f"p{t}", t)

        @block.tensor
        def _(pe):
            for t in range(TILES):
                pe_transposes(pe, jobs, f"b{t}", 0, lambda b: cnt[:, b, t_slice(t)], TILES, R, R)
            jobs.wait_drained(pe, f"b{TILES - 1}")
            for c in range(C):
                pe_wide(pe, jobs, f"g{c}", 0, lambda i, kk: h_pair[i][:, kk, c * 128:(c + 1) * 128],
                        lambda j, kk: bi[j][:, kk, :], TILES)
            jobs.wait_drained(pe, f"g{C - 1}")
            lhs, rhs = proj(w[0], agg)
            for c in range(C):
                pe_wide(pe, jobs, f"f{c}", 0, lhs(c), rhs, C)
            pe.wait_ge(s_fd, C)
            for t in range(TILES):
                pe_natural(pe, jobs, f"o{t}", 0, lambda i, kk: ft[i][:, kk, t_slice(t)],
                           lambda j, kk: w[1][j][:, kk, :], C)
            for t in range(TILES):
                pe.wait_ge(s_hn, TILES + t + 1)
                pe_transposes(pe, jobs, f"y{t}", 0, lambda b: res[:, t, b * 128:(b + 1) * 128], C, R, 128)
            pe.wait_ge(s_w2, 1)
            jobs.wait_drained(pe, f"y{TILES - 1}")
            s = jobs.acquire(pe, "r")
            for t in range(TILES):
                ins = matmul3(pe, ps[s][0:R, t * HID:(t + 1) * HID], lambda i, kk: ht1[i][:, kk, t_slice(t)],
                              lambda j, kk: w_l1[1 + j][:, kk * HID:(kk + 1) * HID], C)
            ins.then_inc(jobs.filled[s], 1)
            pe.wait_ge(s_r, 1)
            pe.wait_ge(s_ai, TILES)
            pe_wide(pe, jobs, "ga", 0, lambda i, kk: r_nat[i][:, kk, :], lambda j, kk: ai[j][:, kk, :], TILES)
            jobs.wait_drained(pe, "ga")
            for t in range(TILES):
                pe_natural(pe, jobs, f"p{t}", 0, lambda i, kk: gt[i][:, t_slice(t)],
                           lambda j, kk: w_l1[1 + j][:, W2COL:W2COL + D], 1)

    scratch = sb("scratch", "ot", [R, TILES, W])
    noise = sb("noise", "qk", [64, W])
    phase = sb("phase", "qk", [64, W], FP32, W * 4)
    turns = sb("turns", "qk", [64, W], I32, 2 * W * 4)
    angle = sb("angle", "qk", [64, W], FP32, 3 * W * 4)
    emb = sb("emb", "qk", [64, W], FP32, 4 * W * 4)
    pre = sb("pre", "qk", [COND, W], FP32, 5 * W * 4)
    sig = sb("sig", "qk", [COND, W], FP32, 6 * W * 4)
    act1 = sb("act1", "rows", [32, W])
    f_w1 = sb("f_w1", "rows", [64, COND], FP32, W * 4 + 16)
    f_w2 = sb("f_w2", "rows", [COND + 1, 128], FP32, W * 4 + 16 + 64)
    f_b1 = sb("f_b1", "rows", [COND, 1], FP32, W * 4 + 592)
    freq = sb("freq", "rows", [64, 1], FP32, W * 4 + 624)
    quarter = sb("quarter", "rows", [64, 1], FP32, W * 4 + 656)
    shift = sb("shift", "rows", [64, 1], FP32, W * 4 + 688)
    one_row = sb("one_row", "rows", [1, D], FP32, W * 4 + 720)
    cond_hi = sb("cond_hi", "qk", [128, W], F32R, 7 * W * 4)
    TWO_PI_HIGH = 6.28125
    TWO_PI_LOW = 2 * np.pi - TWO_PI_HIGH

    jobs = Jobs(ring, ["c1", "c2"])
    s_in, s_k, s_fw, s_sp = sem("c_loaded"), sem("c_constants"), sem("c_f_w2_ready"), sem("c_spilled")
    s_st, s_rs, s_hn = sem("c_stats"), sem("c_rstd"), sem("c_norm")
    s_diag, s_max, s_ln, s_m = sem("c_diagonal"), sem("c_clamped"), sem("c_logs"), sem("c_masks")
    s_ang, s_sin, s_ex, s_a1 = sem("c_angle"), sem("c_sin"), sem("c_exp"), sem("c_act1")
    s_pc, s_vc, s_c2, s_wsz = sem("c_pool_steps"), sem("c_dve_steps"), sem("c_cond_hi"), sem("ws_constant_rows")
    s_wsl, s_wss, s_rows = sem("ws_loaded"), sem("ws_split"), [sem(f"row{n}_loaded") for n in range(3)]
    s_wl2 = [sem(f"l2_w{n}_loaded") for n in range(3)]
    s_wsp = [sem(f"l2_w{n}_split") for n in range(3)]

    def block_of(name, it):
        ap = a[name][bass.ds(it, 1)] if not isinstance(it, int) else a[name][it:it + 1]
        return ap

    def load_w(sp, n, name, it, loaded):
        sp.dma_start(w_raw[n][:], block_of(name, it).rearrange("a (c p) n -> p (a c) n", p=128)).then_inc(loaded[n], 16)

    def load_ws(sp, which, it):
        for quad in range(4):
            for n, kind in enumerate("sb"):
                sp.dma_start(ws_raw[32 * quad:32 * quad + COND, n, :],
                             block_of(f"L2_gnn_{kind}{which}_w", it).rearrange("a c n -> (a c) n")).then_inc(s_wsl, 16)
                sp.dma_start(ws_raw[32 * quad + COND:32 * quad + COND + 1, n, :],
                             block_of(f"L2_gnn_{kind}{which}_b", it)).then_inc(s_wsl, 16)
    WS_DMAS = 16

    def load_row(sp, n, name, it):
        sp.dma_start(rows[n][:], block_of(name, it).to_broadcast([R, D])).then_inc(s_rows[n], 16)

    with nc.Block() as block:
        @block.sync
        def _(sp):
            sp.dma_start(x_spill, x[:]).then_inc(s_sp, 16)
            sp.dma_start(noise[:, 0:N], a["node_vec1"].rearrange("n a -> a n").to_broadcast([64, N])).then_inc(s_in, 16)
            sp.dma_start(f_w1[:], a["L2_gnn_f_w1"]).then_inc(s_in, 16)
            sp.dma_start(f_b1[:], a["L2_gnn_f_b1"].rearrange("(n a) -> n a", a=1)).then_inc(s_in, 16)
            for n, name in enumerate(("L2_gnn_wv", "L2_gnn_wq", "L2_gnn_wk")):
                load_w(sp, n, name, 0, s_wl2)
            sp.wait_ge(s_k, 5)
            for quad in range(4):
                cols = slice(32 * quad, 32 * quad + COND)
                sp.dma_start(f_w2[0:COND, cols], a["L2_gnn_f_w2"]).then_inc(s_fw, 16)
                sp.dma_start(f_w2[COND:COND + 1, cols], a["L2_gnn_f_b2"].rearrange("(a n) -> a n", a=1)).then_inc(s_fw, 16)
                sp.dma_start(f_w2[COND:COND + 1, 32 * quad + COND:32 * quad + COND + 2], one_row[:, 0:2]).then_inc(s_fw, 16)
                sp.dma_start(ws_raw[32 * quad + COND + 1:32 * quad + COND + 2, 0, :], one_row[:]).then_inc(s_wsz, 16)
            load_ws(sp, 1, 0)
            sp.wait_ge(s_wsz, 64)
            sp.wait_ge(s_m, 2)
            sp.dma_start(mask_spill, cnt[:]).then_inc(s_sp, 16)
            sp.wait_ge(s_sp, 32)

        @block.gpsimd
        def _(pool):
            steps = Steps(s_pc)
            for quad in range(2):
                part = slice(32 * quad, 32 * quad + 32)
                steps.done(pool.iota(freq[part, :], [[0, 1]], base=1, channel_multiplier=1,
                                     allow_small_or_imprecise_dtypes=True))
                steps.done(pool.memset(quarter[part, :], 0.25 * quad))
                steps.done(pool.memset(shift[part, :], float(np.pi / 2) * quad))
                steps.wait(pool)
            for count, tile, value in ((1, f_w2, 0.0), (2, one_row, 1.0), (3, ws_raw, 0.0), (4, act1, 1.0)):
                pool.memset(tile[:], value).then_inc(s_k, 1)
                pool.wait_ge(s_k, count)
            pool.memset(noise[:, N:W], 0.0).then_inc(s_k, 1)
            pool.wait_ge(s_k, 5)
            steps.done(pool.tensor_scalar(freq[:], freq[:], float(np.float32(2 * np.pi / 16)), 1.0, ALU.mult, ALU.mult))
            steps.wait(pool)
            for m in range(TILES):
                for counts in (mask, cnt):
                    block_m = counts[:, m, t_slice(m)]
                    pool.tensor_tensor(block_m, block_m, ident[0:R, 0:R], ALU.subtract).then_inc(s_diag, 1)
            pool.wait_ge(s_diag, 2 * TILES)
            for part in (*yt, *pt):
                steps.done(pool.memset(part[:, :, N:W].bitcast(FP32), 0.0))
                steps.wait(pool)
            for t in range(TILES):
                pool.wait_ge(s_st, t + 1)
                pool_rstd(pool, steps, t, s_rs)
            pool.wait_ge(s_wl2[0], 16)
            split_weights(pool, steps, 0, s_wsp[0])

        @block.vector
        def _(dve):
            steps = Steps(s_vc)
            for t in range(TILES):
                dve_stats(dve, steps, t, x[:, t, :], s_st)
            dve.wait_ge(s_in, 48)
            dve.wait_ge(s_k, 5)
            dve.wait_ge(s_pc, 7)
            steps.done(dve.tensor_scalar(phase[:], noise[:], freq[:, 0:1], None, ALU.mult))
            steps.wait(dve)
            steps.done(dve.tensor_scalar(turns[:], phase[:], float(1 / (2 * np.pi)), quarter[:, 0:1], ALU.mult, ALU.add))
            steps.wait(dve)
            steps.done(dve.scalar_tensor_tensor(out=angle[:], in0=turns[:], scalar=-TWO_PI_HIGH, in1=phase[:],
                                                op0=ALU.mult, op1=ALU.add))
            steps.wait(dve)
            steps.done(dve.scalar_tensor_tensor(out=phase[:], in0=turns[:], scalar=-TWO_PI_LOW, in1=angle[:],
                                                op0=ALU.mult, op1=ALU.add))
            steps.wait(dve)
            steps.done(dve.tensor_scalar(angle[:], phase[:], shift[:, 0:1], 3.14159, ALU.add, ALU.min))
            steps.wait(dve)
            dve.tensor_scalar(phase[:], angle[:], -3.14159, None, ALU.max).then_inc(s_ang, 1)

            def masks(n, counts, over):
                dve.wait_ge(s_diag, 2 * TILES)
                if n:
                    dve.wait_ge(s_m, n)
                dve.tensor_scalar(scratch[:], counts[:], 1.0, None, ALU.max).then_inc(s_max, 1)
                steps.done(dve.tensor_scalar(counts[:], counts[:], 0.0, NOEDGE, ALU.is_equal, ALU.mult))
                steps.wait(dve)
                dve.wait_ge(s_ln, n + 1)
                dve.scalar_tensor_tensor(out=counts[:], in0=scratch[:], scalar=over, in1=counts[:], op0=ALU.mult,
                                         op1=ALU.add).then_inc(s_m, 1)

            def act_one():
                dve.wait_ge(s_ex, 1)
                steps.done(dve.tensor_scalar(sig[:], sig[:], 1.0, None, ALU.add))
                steps.wait(dve)
                steps.done(dve.reciprocal(sig[:], sig[:]))
                steps.wait(dve)
                dve.tensor_tensor(act1[0:COND, :], pre[:], sig[:], ALU.mult).then_inc(s_a1, 1)

            masks(0, mask, SCALE2)
            act_one()
            masks(1, cnt, SCALE3)
            dve.wait_ge(s_c2, 2)
            s = jobs.at["c2"][0]
            dve.tensor_tensor(halves(cond[64:128, :]), wide(s, 64, 128), halves(cond_hi[64:128, :].bitcast(FP32)),
                              ALU.subtract).then_inc(jobs.drained[s], 1)

        @block.scalar
        def _(act):
            act.wait_ge(s_sp, 16)
            for t in range(TILES):
                act.wait_ge(s_rs, t + 1)
                act.activation(res[:, t, :], x[:, t, :], ACT.Relu, bias=nmr[:, t:t + 1],
                               scale=rstd[:, t:t + 1]).then_inc(s_hn, 1)
            act.wait_ge(s_ang, 1)
            act.activation(emb[:], phase[:], ACT.Sin).then_inc(s_sin, 1)
            s = jobs.wait_filled(act, "c1")
            act.activation(halves(pre[:]), wide(s, 0, COND), ACT.Identity, bias=f_b1[:, 0:1]).then_inc(jobs.drained[s], 1)
            jobs.wait_drained(act, "c1")
            act.activation(sig[:], pre[:], ACT.Exp, scale=-1.0).then_inc(s_ex, 1)
            for n in range(2):
                act.wait_ge(s_max, n + 1)
                act.activation(scratch[:], scratch[:], ACT.Ln).then_inc(s_ln, 1)
            s = jobs.wait_filled(act, "c2")
            act.activation(halves(cond[0:64, :]), wide(s, 0, 64), ACT.Copy).then_inc(s_c2, 1)
            act.activation(halves(cond_hi[64:128, :]), wide(s, 64, 128), ACT.Copy).then_inc(s_c2, 1)

        @block.tensor
        def _(pe):
            pe.wait_ge(s_sin, 1)
            s = jobs.acquire(pe, "c1")
            for half in range(2):
                ins = pe.matmul(ps[s][0:COND, 512 * half:512 * half + H2], f_w1[:], emb[:, half * H2:half * H2 + H2],
                                start=True, stop=True)
            ins.then_inc(jobs.filled[s], 1)
            pe.wait_ge(s_a1, 1)
            pe.wait_ge(s_fw, 12 * 16)
            s = jobs.acquire(pe, "c2")
            for half in range(2):
                ins = pe.matmul(ps[s][:, 512 * half:512 * half + H2], f_w2[:], act1[0:COND + 1, half * H2:half * H2 + H2],
                                start=True, stop=True)
            ins.then_inc(jobs.filled[s], 1)

    names = ["n1_0", "a1_0"]
    for t in range(1, TILES):
        names += [f"n1_{t}", f"a1_{t}", f"v{t - 1}"]
    names += [f"v{TILES - 1}", "q0", "k0"]
    attn = attention_jobs(HEADS2, lambda h: [f"q{h + 1}"] if h + 1 < HEADS2 else [],
                          lambda h: ["q1", "k1"] if h == 0 else [f"k{h + 1}"] if h + 1 < HEADS2 else [])
    names += attn
    ln2 = ["o0", "o1", "o2", "n2_0", "a2_0", "o3", "n2_1", "a2_1", "o4", "n2_2", "a2_2", "n2_3", "a2_3", "n2_4", "a2_4"]
    names += ln2 + [f"f{c}" for c in range(C)] + [f"p{t}" for t in range(TILES)]
    jobs = Jobs(ring, names, BLOCKS)
    UNITS = HEADS2 * TILES
    hi_index = {n: i for i, n in enumerate(n for n in names if n[0] in "aqkt" or n[:2] == "pv")}
    s_hi, s_st, s_rs, s_hn = sem("m_hi"), sem("m_stats"), sem("m_rstd"), sem("m_norm")
    s_ex, s_ri, s_sc = sem("m_exp"), sem("m_inverse"), sem("m_scaled")
    s_vh, s_vd, s_fd, s_xb = sem("m_v_hi"), sem("m_v_split"), sem("m_f_split"), sem("m_bias_added")
    s_pm, s_vm, s_xb2, s_w2h = sem("m_pool_steps"), sem("m_dve_steps"), sem("m_bias2_added"), sem("m_w2_hi")
    POOL_STEPS, DVE_STEPS = 2 * 2 * TILES + 6 + 5 * C, 2 * (2 * TILES) + UNITS + C + 0

    def body(eng, run, last_differs):
        n = BLOCKS - 1 if last_differs else BLOCKS
        with eng.Fori(0, n) as it:
            run(it, True)
        if last_differs:
            run(BLOCKS - 1, False)

    def split_ws(pool, steps, done_before):
        own(pool)
        steps.done(pool.tensor_scalar(ws[:], ws_raw[:], 1.0, 1.0, ALU.mult, ALU.mult))
        for n, quad in enumerate((1, 3)):
            steps.wait(pool)
            rows_q = slice(32 * quad, 32 * quad + 32)
            steps.done(pool.tensor_tensor(ws[rows_q], ws_raw[rows_q], ws[rows_q].bitcast(FP32), ALU.subtract))
        steps.wait(pool)
        pool.sem_inc(s_wss, 2)

    with nc.Block() as block:
        @block.sync
        def _(sp):
            for n, name in enumerate(("L2_gnn_bv", "L2_gnn_bo", "L2_gnn_m_b2")):
                load_row(sp, n, name, 0)

            def run(it, more):
                jobs.wait_filled(sp, f"v{TILES - 1}", it)
                load_w(sp, 0, "L2_gnn_wo", it, s_wl2)
                if more:
                    jobs.wait_drained(sp, f"v{TILES - 1}", it)
                    load_row(sp, 0, "L2_gnn_bv", it + 1)
                sp.wait_ge(s_wss, it * 4 + 2)
                load_ws(sp, 2, it)
                if more:
                    sp.wait_ge(s_xb, it * TILES + TILES)
                    load_row(sp, 1, "L2_gnn_bo", it + 1)
                jobs.wait_filled(sp, f"q{HEADS2 - 1}", it)
                load_w(sp, 1, "L2_gnn_m_w1", it, s_wl2)
                jobs.wait_filled(sp, f"k{HEADS2 - 1}", it)
                load_w(sp, 2, "L2_gnn_m_w2", it, s_wl2)
                if more:
                    jobs.wait_filled(sp, f"o{TILES - 1}", it)
                    load_w(sp, 0, "L2_gnn_wv", it + 1, s_wl2)
                    sp.wait_ge(s_wss, it * 4 + 4)
                    load_ws(sp, 1, it + 1)
                    jobs.wait_filled(sp, f"f{C - 1}", it)
                    load_w(sp, 1, "L2_gnn_wq", it + 1, s_wl2)
                    sp.wait_ge(s_xb2, it * TILES + TILES)
                    load_row(sp, 2, "L2_gnn_m_b2", it + 1)
                    jobs.wait_filled(sp, f"p{TILES - 1}", it)
                    load_w(sp, 2, "L2_gnn_wk", it + 1, s_wl2)
            body(sp, run, True)

        @block.gpsimd
        def _(pool):
            steps = Steps(s_pm, POOL_STEPS)
            pool.wait_ge(s_wsl, WS_DMAS * 16)
            pool.wait_ge(s_wsz, 64)
            pre_steps = Steps(sem("m_pool_first"))
            split_ws(pool, pre_steps, 0)

            def run(it, more):
                steps.body(it)

                def add_row(n, t):
                    pool.wait_ge(s_hn, it * 2 * TILES + TILES)
                    pool.wait_ge(s_rows[n], it * 16 + 16)
                    pool.tensor_tensor(res[:, t, :], res[:, t, :], rows[n][:], ALU.add).then_inc(s_xb, 1)

                def weights(n, loads, pieces=range(C)):
                    pool.wait_ge(s_wl2[n], it * 32 + 16 * loads)
                    split_weights(pool, steps, n, s_wsp[n], pieces)

                for t in range(TILES):
                    pool.wait_ge(s_st, it * 2 * TILES + t + 1)
                    pool_rstd(pool, steps, t, s_rs)
                weights(1, 1)
                weights(2, 1)
                for u in range(UNITS):
                    pool_scale(pool, u, it, UNITS, s_ri, s_sc)
                    if u < TILES:
                        add_row(1, u)
                    if u == 6:
                        jobs.wait_filled(pool, f"n1_{TILES - 1}", it)
                        pool.wait_ge(s_wsl, (it * 2 + 2) * WS_DMAS * 16)
                        split_ws(pool, steps, 0)
                    if 8 <= u < 8 + C:
                        weights(0, 2, [u - 8])
                    if UNITS - C <= u:
                        weights(1, 2, [u - (UNITS - C)])
                for t in range(TILES):
                    pool.wait_ge(s_st, it * 2 * TILES + TILES + t + 1)
                    pool_rstd(pool, steps, t, s_rs)
                if more:
                    jobs.wait_filled(pool, f"n2_{TILES - 1}", it)
                    pool.wait_ge(s_wsl, (it * 2 + 3) * WS_DMAS * 16)
                    split_ws(pool, steps, 0)
                    weights(0, 3)
                    steps.end()
            body(pool, run, True)

        def modulate(dve, steps, it, name, t, norm_index):
            s = jobs.wait_filled(dve, name, it)
            dve.wait_ge(s_hn, it * 2 * TILES + norm_index * TILES + t + 1)
            if t > 0:
                jobs.wait_drained(dve, f"{name[:3]}{t - 1}", it)
            steps.done(dve.tensor_tensor(y1[:], xn[:, t % 2, :], ps[s][0:R, 0:D], ALU.mult))
            steps.wait(dve)
            dve.tensor_tensor(y2[:, t % 2, :], y1[:], ps[s][0:R, D:2 * D], ALU.add).then_inc(jobs.drained[s], 1)

        @block.vector
        def _(dve):
            first = Steps(sem("m_dve_first"))
            for t in range(TILES):
                dve_stats(dve, first, t, res[:, t, :], s_st)
            steps = Steps(s_vm, DVE_STEPS)

            def run(it, more):
                steps.body(it)

                def wait_hi(name):
                    dve.wait_ge(s_hi, it * len(hi_index) + hi_index[name] + 1)
                    return jobs.at[name][0]

                def prob_lo(name):
                    if name:
                        t = int(name[3])
                        s = wait_hi(name)
                        dve.tensor_tensor(pt_view(1, t), blocks(s, TILES, R), pt_view(0, t).bitcast(FP32),
                                          ALU.subtract).then_inc(jobs.drained[s], 1)

                held = None
                for name in names[:names.index("f0")]:
                    kind = name[0]
                    if kind != "s":
                        held = prob_lo(held)
                    if kind == "n":
                        modulate(dve, steps, it, name, int(name[3]), int(name[1]) - 1)
                    elif kind == "a":
                        t = int(name[3])
                        s = wait_hi(name)
                        dve.tensor_tensor(yt[1][:, :, t_slice(t)], blocks(s, C), yt[0][:, :, t_slice(t)].bitcast(FP32),
                                          ALU.subtract).then_inc(jobs.drained[s], 1)
                    elif kind == "v":
                        t = int(name[1])
                        s = jobs.wait_filled(dve, name, it)
                        dve.wait_ge(s_rows[0], it * 16 + 16)
                        if t >= 2:
                            dve.wait_ge(s_vd, it * TILES + t - 1)
                        dve.tensor_tensor(vtmp[:, t % 2, :], ps[s][0:R, 0:D], rows[0][:], ALU.add).then_inc(jobs.drained[s], 1)
                        if t > 0:
                            v_lo(dve, it, t - 1)
                        if t == TILES - 1:
                            v_lo(dve, it, t)
                    elif kind in "qk":
                        h = int(name[1])
                        s = wait_hi(name)
                        buf, bias = (q, bq2) if kind == "q" else (k, bk2)
                        dve.scalar_tensor_tensor(out=halves(buf[h % 2][1][:]), in0=wide(s),
                                                 scalar=bias[:, bass.ds(it * C + h, 1)],
                                                 in1=halves(buf[h % 2][0][:]).bitcast(FP32), op0=ALU.add,
                                                 op1=ALU.subtract).then_inc(jobs.drained[s], 1)
                    elif kind == "s":
                        u = int(name[1]) * TILES + int(name[3])
                        dve_scores(dve, jobs, u, it, 1 / SCALE2)
                        if u > 0:
                            dve_inverse(dve, steps, u - 1, it, UNITS, s_ex, s_ri)
                        held = prob_lo(held)
                        if u == UNITS - 1:
                            dve_inverse(dve, steps, u, it, UNITS, s_ex, s_ri)
                    elif kind == "t":
                        held = name
                    elif kind == "p":
                        h = int(name[2])
                        s = wait_hi(name)
                        dve.tensor_tensor(halves(ot[1][:, h, :]), wide(s), halves(ot[0][:, h, :]).bitcast(FP32),
                                          ALU.subtract).then_inc(jobs.drained[s], 1)
                    elif kind == "o":
                        t = int(name[1])
                        dve.wait_ge(s_xb, it * TILES + t + 1)
                        residual(dve, steps, it, name, t)
                for c in range(C):
                    dve.wait_ge(s_w2h, it * C + c + 1)
                    dve.tensor_tensor(w[2][1][:, c, :], w_raw[2][:, c, :], w[2][0][:, c, :].bitcast(FP32),
                                      ALU.subtract).then_inc(s_wsp[2], 1)
                    for t in range(c, TILES, C):
                        dve.wait_ge(s_hn, it * 2 * TILES + 2 * TILES)
                        dve.wait_ge(s_rows[2], it * 16 + 16)
                        dve.tensor_tensor(res[:, t, :], res[:, t, :], rows[2][:], ALU.add).then_inc(s_xb2, 1)
                    jobs.wait_drained(dve, f"f{c}", it)
                    steps.done(dve.tensor_copy(ht[0][:, c, :], ftmp[:, c % 2, :]))
                    steps.wait(dve)
                    dve.tensor_tensor(ht[1][:, c, :], ftmp[:, c % 2, :], ht[0][:, c, :].bitcast(FP32),
                                      ALU.subtract).then_inc(s_fd, 1)
                for t in range(TILES):
                    dve.wait_ge(s_xb2, it * TILES + TILES)
                    residual(dve, steps, it, f"p{t}", t)
                steps.end()

            def v_lo(dve, it, t):
                dve.wait_ge(s_vh, it * TILES + t + 1)
                dve.tensor_tensor(v[1][:, t, :], vtmp[:, t % 2, :], v[0][:, t, :].bitcast(FP32),
                                  ALU.subtract).then_inc(s_vd, 1)

            def residual(dve, steps, it, name, t):
                s = jobs.wait_filled(dve, name, it)
                dve.tensor_tensor(res[:, t, :], ps[s][0:R, 0:D], res[:, t, :], ALU.add).then_inc(jobs.drained[s], 1)
                jobs.wait_drained(dve, name, it)
                dve_stats(dve, steps, t, res[:, t, :], s_st)
            body(dve, run, False)

        @block.scalar
        def _(act):
            def run(it, more):
                for name in names[:names.index("f0")]:
                    kind = name[0]
                    s = jobs.at[name][0]
                    if kind == "n":
                        t, first = int(name[3]), name[1] == "1"
                        index = 0 if first else TILES
                        act.wait_ge(s_rs, it * 2 * TILES + index + t + 1)
                        if t >= 2:
                            jobs.wait_drained(act, f"{name[:3]}{t - 2}", it)
                        act.activation(xn[:, t % 2, :], res[:, t, :], ACT.Identity, bias=nmr[:, t:t + 1],
                                       scale=rstd[:, t:t + 1]).then_inc(s_hn, 1)
                    elif kind == "a":
                        act_hi(act, jobs, name, it, yt[0][:, :, t_slice(int(name[3]))], blocks(s, C), s_hi)
                    elif kind == "v":
                        t = int(name[1])
                        jobs.wait_drained(act, name, it)
                        act.activation(v[0][:, t, :], vtmp[:, t % 2, :], ACT.Copy).then_inc(s_vh, 1)
                    elif kind in "qk":
                        h = int(name[1])
                        buf, bias = (q, bq2) if kind == "q" else (k, bk2)
                        act_hi(act, jobs, name, it, halves(buf[h % 2][0][:]), wide(s), s_hi, bias[:, bass.ds(it * C + h, 1)])
                    elif kind == "s":
                        act_exp(act, jobs, int(name[1]) * TILES + int(name[3]), it, s_ex)
                    elif kind == "t":
                        act_hi(act, jobs, name, it, pt_view(0, int(name[3])), blocks(s, TILES, R), s_hi)
                    elif kind == "p":
                        act_hi(act, jobs, name, it, halves(ot[0][:, int(name[2]), :]), wide(s), s_hi)
                for c in range(C):
                    act.wait_ge(s_wl2[2], it * 32 + 32)
                    act.activation(w[2][0][:, c, :], w_raw[2][:, c, :], ACT.Copy).then_inc(s_w2h, 1)
                    s = jobs.wait_filled(act, f"f{c}", it)
                    if c >= 2:
                        act.wait_ge(s_fd, it * C + c - 1)
                    act.activation(halves(ftmp[:, c % 2, :]), wide(s), ACT.Relu,
                                   bias=bm2[:, bass.ds(it * C + c, 1)]).then_inc(jobs.drained[s], 1)
            body(act, run, False)

        @block.tensor
        def _(pe):
            def weights_ready(n, it, which):
                pe.wait_ge(s_wsp[n], it * 2 * C + which * C)

            def run(it, more):
                lhs_q, rhs_y = proj(w[1], yt)
                lhs_k, _ = proj(w[2], yt)
                for name in names:
                    kind = name[0]
                    if kind == "n":
                        t = int(name[3])
                        pe.wait_ge(s_wss, it * 4 + 2 * int(name[1]))
                        s = jobs.acquire(pe, name, it)
                        for n in range(2):
                            ins = pe.matmul(ps[s][0:R, D * n:D * n + D], cond[:, t_slice(t)], ws[:, n, :], start=True,
                                            stop=True)
                        ins.then_inc(jobs.filled[s], 1)
                    elif kind == "a":
                        t = int(name[3])
                        jobs.wait_drained(pe, f"n{name[1:]}", it)
                        pe_transposes(pe, jobs, name, it, lambda b: y2[:, t % 2, b * 128:(b + 1) * 128], C, R, 128)
                    elif kind == "v":
                        t = int(name[1])
                        if t == 0:
                            weights_ready(0, it, 1)
                        jobs.wait_drained(pe, f"a1_{t}", it)
                        pe_natural(pe, jobs, name, it, lambda i, kk: yt[i][:, kk, t_slice(t)],
                                   lambda j, kk: w[0][j][:, kk, :], C)
                    elif kind in "qk":
                        h = int(name[1])
                        if h == 0:
                            weights_ready(1 if kind == "q" else 2, it, 1)
                        pe_wide(pe, jobs, name, it, (lhs_q if kind == "q" else lhs_k)(h), rhs_y, C)
                    elif kind == "s":
                        h, t = int(name[1]), int(name[3])
                        if t == 0:
                            jobs.wait_drained(pe, f"q{h}", it)
                            jobs.wait_drained(pe, f"k{h}", it)
                        pe_scores(pe, jobs, h, t, it, q[h % 2], k[h % 2], 0, 128)
                    elif kind == "t":
                        pe_prob_transposes(pe, jobs, int(name[1]) * TILES + int(name[3]), it, UNITS, s_sc)
                    elif name[:2] == "pv":
                        h = int(name[2])
                        if h == 0:
                            pe.wait_ge(s_vd, it * TILES + TILES)
                        pe_values(pe, jobs, h, h, it)
                    elif kind == "o":
                        t = int(name[1])
                        if t == 0:
                            jobs.wait_drained(pe, f"pv{HEADS2 - 1}", it)
                            weights_ready(0, it, 2)
                        pe_natural(pe, jobs, name, it, lambda i, kk: ot[i][:, kk, t_slice(t)],
                                   lambda j, kk: w[0][j][:, kk, :], C)
                    elif kind == "f":
                        c = int(name[1])
                        if c == 0:
                            jobs.wait_drained(pe, f"a2_{TILES - 1}", it)
                            weights_ready(1, it, 2)
                        pe_wide(pe, jobs, name, it, lhs_q(c), rhs_y, C)
                    else:
                        t = int(name[1])
                        if t == 0:
                            pe.wait_ge(s_fd, it * C + C)
                            weights_ready(2, it, 2)
                        pe_natural(pe, jobs, name, it, lambda i, kk: ht[i][:, kk, t_slice(t)],
                                   lambda j, kk: w[2][j][:, kk, :], C)
            body(pe, run, False)

    enc = sb("enc", "ot", [128, C, W])
    acc = sb("acc", "ot", [128, C, W], FP32, C * W * 4)

    jobs = Jobs(ring, [f"a{t}" for t in range(TILES)])
    s_x, s_st, s_rs, s_hn, s_sum = sem("e_x_loaded"), sem("e_stats"), sem("e_rstd"), sem("e_norm"), sem("e_sum")
    s_hi, s_enc, s_pad, s_sp = sem("e_hi"), sem("e_enc"), sem("e_pads"), sem("e_spilled")
    s_pe_, s_ve_ = sem("e_pool_steps"), sem("e_dve_steps")
    s_wl3 = [sem(f"l3_w{n}_loaded") for n in range(3)]
    s_wsp3 = [sem(f"l3_w{n}_split") for n in range(3)]
    s_mask, s_row3 = sem("mask_loaded"), [sem(f"l3_row{n}_loaded") for n in range(3)]

    def load_row3(sp, n, src):
        sp.dma_start(rows[n][:], src).then_inc(s_row3[n], 16)

    with nc.Block() as block:
        @block.sync
        def _(sp):
            sp.dma_start(x[:], x_spill).then_inc(s_x, 16)
            for n, name in enumerate(("L3_gnn_Wv", "L3_gnn_Wq", "L3_gnn_Wk")):
                load_w(sp, n, name, 0, s_wl3)
            sp.dma_start(mask[:], mask_spill).then_inc(s_mask, 16)
            load_row3(sp, 0, block_of("L3_gnn_bv", 0).to_broadcast([R, D]))
            sp.wait_ge(s_sum, TILES)
            sp.dma_start(x_spill, x[:]).then_inc(s_sp, 16)
            sp.wait_ge(s_sp, 16)

        @block.gpsimd
        def _(pool):
            steps = Steps(s_pe_)
            pool.memset(enc[:, :, N:W], 0.0).then_inc(s_pad, 1)
            for t in range(TILES):
                pool.wait_ge(s_st, t + 1)
                pool_rstd(pool, steps, t, s_rs)
            pool.wait_ge(s_wl3[0], 16)
            split_weights(pool, steps, 0, s_wsp3[0])

        @block.vector
        def _(dve):
            steps = Steps(s_ve_)
            dve.wait_ge(s_x, 16)
            for t in range(TILES):
                dve.tensor_tensor(x[:, t, :], x[:, t, :], res[:, t, :], ALU.add).then_inc(s_sum, 1)
                dve.wait_ge(s_sum, t + 1)
                dve_stats(dve, steps, t, x[:, t, :], s_st)
            for t in range(TILES):
                dve.wait_ge(s_hi, t + 1)
                s = jobs.at[f"a{t}"][0]
                dve.tensor_tensor(yt[1][:, :, t_slice(t)], blocks(s, C), yt[0][:, :, t_slice(t)].bitcast(FP32),
                                  ALU.subtract).then_inc(jobs.drained[s], 1)

        @block.scalar
        def _(act):
            for t in range(TILES):
                act.wait_ge(s_rs, t + 1)
                act.activation(res[:, t, :], x[:, t, :], ACT.Relu, bias=nmr[:, t:t + 1],
                               scale=rstd[:, t:t + 1]).then_inc(s_hn, 1)
            for t in range(TILES):
                s = jobs.wait_filled(act, f"a{t}")
                act.activation(enc[:, :, t_slice(t)], blocks(s, C), ACT.Copy).then_inc(s_enc, 1)
                act.activation(yt[0][:, :, t_slice(t)], blocks(s, C), ACT.Copy).then_inc(s_hi, 1)

        @block.tensor
        def _(pe):
            for t in range(TILES):
                pe.wait_ge(s_hn, t + 1)
                pe_transposes(pe, jobs, f"a{t}", 0, lambda b: res[:, t, b * 128:(b + 1) * 128], C, R, 128)

    def spot1(h):
        return [f"k{h // 2 + 1}"] if h % 2 and h // 2 + 1 < C else ["w3"] if h == 6 else []

    def spot2(h):
        return ([f"q{h // 2 + 1}"] if h // 2 + 1 < C else []) if h % 2 == 0 else [f"w{h // 2}"] if h < 6 else []

    names = [f"v{t}" for t in range(TILES)] + ["q0", "k0"] + attention_jobs(HEADS3, spot1, spot2)
    jobs = Jobs(ring, names, LAYERS)
    UNITS3 = HEADS3 * TILES
    hi_index3 = {n: i for i, n in enumerate(n for n in names if n[0] in "qkt")}
    into_acc = {c: [n for n in names if n in (f"w{c}", f"pv{2 * c}", f"pv{2 * c + 1}")] for c in range(C)}
    s_hi, s_ex, s_ri, s_sc = sem("t_hi"), sem("t_exp"), sem("t_inverse"), sem("t_scaled")
    s_vh, s_vd, s_acc, s_xh, s_xt = sem("t_v_hi"), sem("t_v_split"), sem("t_acc_set"), sem("t_x_hi"), sem("t_x_split")
    s_pt, s_vt = sem("t_pool_steps"), sem("t_dve_steps")

    def layers(eng, run):
        with eng.Fori(0, LAYERS - 1) as it:
            run(it, True)
        run(LAYERS - 1, False)

    def layers_alike(eng, run):
        with eng.Fori(0, LAYERS) as it:
            run(it)

    def load_half(sp, n, src):
        sp.dma_start(w_raw[n][:], src.rearrange("(c p) n -> p c n", p=128)).then_inc(s_wl3[n], 16)

    with nc.Block() as block:
        @block.sync
        def _(sp):
            def run(it, more):
                jobs.wait_filled(sp, f"v{TILES - 1}", it)
                load_w(sp, 0, "L3_gnn_Ws", it, s_wl3)
                if more:
                    jobs.wait_drained(sp, f"v{TILES - 1}", it)
                    load_row3(sp, 0, block_of("L3_gnn_bv", it + 1).to_broadcast([R, D]))
                jobs.wait_filled(sp, f"q{C - 1}", it)
                if more:
                    load_w(sp, 1, "L3_gnn_Wq", it + 1, s_wl3)
                else:
                    load_half(sp, 1, a["L3_gnn_W1"][:, 0:D])
                jobs.wait_filled(sp, f"k{C - 1}", it)
                if more:
                    load_w(sp, 2, "L3_gnn_Wk", it + 1, s_wl3)
                else:
                    load_half(sp, 2, a["L3_gnn_W1"][:, D:2 * D])
                jobs.wait_filled(sp, f"w{C - 1}", it)
                if more:
                    load_w(sp, 0, "L3_gnn_Wv", it + 1, s_wl3)
                else:
                    load_half(sp, 0, a["L3_gnn_W2"][0:D, :])
            layers(sp, run)

        @block.gpsimd
        def _(pool):
            per = 2 * C + C + C
            steps = Steps(s_pt, per)
            first = Steps(sem("t_pool_first"))
            for n in (1, 2):
                pool.wait_ge(s_wl3[n], 16)
                split_weights(pool, first, n, s_wsp3[n])

            def run(it, more):
                steps.body(it)
                for u in range(UNITS3):
                    pool_scale(pool, u, it, UNITS3, s_ri, s_sc)
                    for n, from_unit, loads, per_layer in ((0, 3, 2, 2), (1, 28, 2, 1), (2, 32, 2, 1)):
                        if from_unit <= u < from_unit + C:
                            pool.wait_ge(s_wl3[n], it * 16 * per_layer + 16 * loads)
                            split_weights(pool, steps, n, s_wsp3[n], [u - from_unit])
                pool.wait_ge(s_wl3[0], it * 32 + 48)
                split_weights(pool, steps, 0, s_wsp3[0])
                steps.end()
            layers_alike(pool, lambda it: run(it, True))

        @block.vector
        def _(dve):
            steps = Steps(s_vt, UNITS3)
            dve.sem_inc(s_xt, 1)

            def run(it):
                steps.body(it)

                def wait_hi(name):
                    dve.wait_ge(s_hi, it * len(hi_index3) + hi_index3[name] + 1)
                    return jobs.at[name][0]

                def v_lo(t):
                    dve.wait_ge(s_vh, it * TILES + t + 1)
                    dve.tensor_tensor(v[1][:, t, :], xn[:, t % 2, :], v[0][:, t, :].bitcast(FP32),
                                      ALU.subtract).then_inc(s_vd, 1)

                def prob_lo(name):
                    if name:
                        t = int(name[3])
                        s = wait_hi(name)
                        dve.tensor_tensor(pt_view(1, t), blocks(s, TILES, R), pt_view(0, t).bitcast(FP32),
                                          ALU.subtract).then_inc(jobs.drained[s], 1)

                held = None
                for name in names:
                    kind = name[0]
                    if kind != "s":
                        held = prob_lo(held)
                    if kind == "v":
                        t = int(name[1])
                        s = jobs.wait_filled(dve, name, it)
                        dve.wait_ge(s_row3[0], it * 16 + 16)
                        if t >= 2:
                            dve.wait_ge(s_vd, it * TILES + t - 1)
                        dve.tensor_tensor(xn[:, t % 2, :], ps[s][0:R, 0:D], rows[0][:], ALU.add).then_inc(jobs.drained[s], 1)
                        if t > 0:
                            v_lo(t - 1)
                        if t == TILES - 1:
                            v_lo(t)
                    elif kind in "qk":
                        c = int(name[1])
                        s = wait_hi(name)
                        buf, bias = (q, bq3) if kind == "q" else (k, bk3)
                        dve.scalar_tensor_tensor(out=halves(buf[c % 2][1][:]), in0=wide(s),
                                                 scalar=bias[:, bass.ds(it * C + c, 1)],
                                                 in1=halves(buf[c % 2][0][:]).bitcast(FP32), op0=ALU.add,
                                                 op1=ALU.subtract).then_inc(jobs.drained[s], 1)
                    elif kind == "s":
                        u = int(name[1]) * TILES + int(name[3])
                        if u == 0:
                            dve.wait_ge(s_mask, 16)
                        dve_scores(dve, jobs, u, it, 1 / SCALE3)
                        if u > 0:
                            dve_inverse(dve, steps, u - 1, it, UNITS3, s_ex, s_ri)
                        held = prob_lo(held)
                        if u == UNITS3 - 1:
                            dve_inverse(dve, steps, u, it, UNITS3, s_ex, s_ri)
                    elif kind == "t":
                        held = name
                    else:
                        c = int(name[1]) if kind == "w" else int(name[2]) // 2
                        p0, p1 = (0, 128) if kind == "w" else (64 * (int(name[2]) % 2), 64 * (int(name[2]) % 2) + 64)
                        s = jobs.wait_filled(dve, name, it)
                        dve.wait_ge(s_acc, it * C + c + 1)
                        before = into_acc[c][:into_acc[c].index(name)]
                        if before:
                            jobs.wait_drained(dve, before[-1], it)
                        if kind == "w":
                            dve.scalar_tensor_tensor(out=halves(acc[:, c, :]), in0=wide(s),
                                                     scalar=bs3[:, bass.ds(it * C + c, 1)], in1=halves(acc[:, c, :]),
                                                     op0=ALU.add, op1=ALU.add).then_inc(jobs.drained[s], 1)
                        else:
                            dve.tensor_tensor(halves(acc[p0:p1, c, :]), wide(s, p0, p1), halves(acc[p0:p1, c, :]),
                                              ALU.add).then_inc(jobs.drained[s], 1)
                for c in range(C):
                    dve.wait_ge(s_xh, it * C + c + 1)
                    dve.tensor_tensor(yt[1][:, c, :], acc[:, c, :], yt[0][:, c, :].bitcast(FP32),
                                      ALU.subtract).then_inc(s_xt, 1)
                steps.end()
            layers_alike(dve, run)

        @block.scalar
        def _(act):
            def run(it):
                act.wait_ge(s_xt, it * C + 1)
                for c in range(C):
                    act.activation(acc[:, c, :], enc[:, c, :], ACT.Copy).then_inc(s_acc, 1)
                for name in names:
                    kind = name[0]
                    s = jobs.at[name][0]
                    if kind == "v":
                        t = int(name[1])
                        jobs.wait_drained(act, name, it)
                        act.activation(v[0][:, t, :], xn[:, t % 2, :], ACT.Copy).then_inc(s_vh, 1)
                    elif kind in "qk":
                        c = int(name[1])
                        buf, bias = (q, bq3) if kind == "q" else (k, bk3)
                        act_hi(act, jobs, name, it, halves(buf[c % 2][0][:]), wide(s), s_hi, bias[:, bass.ds(it * C + c, 1)])
                    elif kind == "s":
                        act_exp(act, jobs, int(name[1]) * TILES + int(name[3]), it, s_ex)
                    elif kind == "t":
                        act_hi(act, jobs, name, it, pt_view(0, int(name[3])), blocks(s, TILES, R), s_hi)
                for c in range(C):
                    jobs.wait_drained(act, into_acc[c][-1], it)
                    if c == 0:
                        jobs.wait_filled(act, f"w{C - 1}", it)
                    act.activation(yt[0][:, c, :], acc[:, c, :], ACT.Copy).then_inc(s_xh, 1)
            layers_alike(act, run)

        @block.tensor
        def _(pe):
            def run(it):
                pe.wait_ge(s_xt, it * C + 1)
                ops = {n: proj(w[slot], yt) for n, slot in (("q", 1), ("k", 2), ("w", 0))}
                for name in names:
                    kind = name[0]
                    if kind == "v":
                        t = int(name[1])
                        if t == 0:
                            pe.wait_ge(s_wsp3[0], it * 2 * C + C)
                        pe_natural(pe, jobs, name, it, lambda i, kk: yt[i][:, kk, t_slice(t)],
                                   lambda j, kk: w[0][j][:, kk, :], C)
                    elif kind in "qkw":
                        c = int(name[1])
                        if c == 0 and kind == "w":
                            pe.wait_ge(s_wsp3[0], it * 2 * C + 2 * C)
                        elif c == 0:
                            pe.wait_ge(s_wsp3[1 if kind == "q" else 2], it * C + C)
                        lhs, rhs = ops[kind]
                        pe_wide(pe, jobs, name, it, lhs(c), rhs, C)
                    elif kind == "s":
                        h, t = int(name[1]), int(name[3])
                        c, r0 = h // 2, 64 * (h % 2)
                        if t == 0:
                            jobs.wait_drained(pe, f"q{c}", it)
                            jobs.wait_drained(pe, f"k{c}", it)
                        pe_scores(pe, jobs, h, t, it, q[c % 2], k[c % 2], r0, r0 + 64)
                    elif kind == "t":
                        pe_prob_transposes(pe, jobs, int(name[1]) * TILES + int(name[3]), it, UNITS3, s_sc)
                    else:
                        h = int(name[2])
                        if h == 0:
                            pe.wait_ge(s_vd, it * TILES + TILES)
                        pe_values(pe, jobs, h, h // 2, it)
            layers_alike(pe, run)

    z = sb("z", "pt", [R, TILES, D])
    nrm = sb("nrm", "pt", [R, TILES, D], FP32, TILES * D * 4)
    ut = [sb("ut_hi", "qk", [128, 2 * C, W], F32R), sb("ut_lo", "qk", [128, 2 * C, W], F32R, 2 * C * W * 4)]
    xo = sb("xo", "mask", [R, TILES, D])

    names = [f"n{t}" for t in range(TILES)] + [f"a{t}" for t in range(TILES)] + [f"f{c}" for c in range(2 * C)]
    names += [f"p{t}" for t in range(TILES)]
    jobs = Jobs(ring, names)
    s_st, s_rs, s_hn, s_hi, s_fd = sem("d_stats"), sem("d_rstd"), sem("d_norm"), sem("d_hi"), sem("d_f_split")
    s_pd, s_vd_, s_n, s_nb, s_xo = sem("d_pool_steps"), sem("d_dve_steps"), sem("d_affine"), sem("d_bias_added"), sem("d_xo_loaded")
    s_xs, s_o, s_out = sem("d_residual"), sem("d_result"), sem("d_stored")

    def lo_t(dve, t):
        dve.wait_ge(s_hi, t + 1)
        s = jobs.at[f"a{t}"][0]
        dve.tensor_tensor(yt[1][:, :, t_slice(t)], blocks(s, C), yt[0][:, :, t_slice(t)].bitcast(FP32),
                          ALU.subtract).then_inc(jobs.drained[s], 1)

    def hi_t(act, t):
        s = jobs.at[f"a{t}"][0]
        act_hi(act, jobs, f"a{t}", 0, yt[0][:, :, t_slice(t)], blocks(s, C), s_hi)

    with nc.Block() as block:
        @block.sync
        def _(sp):
            load_row3(sp, 1, row(a["L3_gnn_ln_g"]))
            load_row3(sp, 2, row(a["L3_gnn_ln_b"]))
            load_row3(sp, 0, row(a["L3_gnn_b2"]))
            sp.dma_start(xo[:], x_spill).then_inc(s_xo, 16)
            jobs.wait_filled(sp, f"f{C - 1}")
            load_half(sp, 1, a["L3_gnn_W2"][D:2 * D, :])
            for t in range(TILES):
                sp.wait_ge(s_o, t + 1)
                sp.dma_start(out[t * R:(t + 1) * R, :], xo[:, t, :]).then_inc(s_out, 16)
            sp.wait_ge(s_out, 16 * TILES)

        @block.gpsimd
        def _(pool):
            steps = Steps(s_pd)
            for t in range(TILES):
                pool.wait_ge(s_st, t + 1)
                pool_rstd(pool, steps, t, s_rs)
            pool.wait_ge(s_xo, 16)
            pool.wait_ge(s_row3[0], 16 * (LAYERS + 1))
            for t in range(TILES):
                pool.tensor_tensor(xo[:, t, :], xo[:, t, :], res[:, t, :], ALU.add).then_inc(s_xs, 1)
                jobs.wait_filled(pool, f"a{t}")
                pool.tensor_tensor(nrm[:, t, :], nrm[:, t, :], rows[0][:], ALU.add).then_inc(s_nb, 1)
            pool.wait_ge(s_wl3[1], 16 * (LAYERS + 2))
            split_weights(pool, steps, 1, s_wsp3[1])
            for t in range(TILES):
                pool.wait_ge(s_st, TILES + t + 1)
                pool_rstd(pool, steps, t, s_rs)

        @block.vector
        def _(dve):
            steps = Steps(s_vd_)

            def affine(t, n, out_ap):
                dve.wait_ge(s_hn, n * TILES + t + 1)
                if n + t > 0:
                    dve.wait_ge(s_n, n * TILES + t)
                steps.done(dve.tensor_tensor(y1[:], xn[:, t % 2, :], rows[1][:], ALU.mult))
                steps.wait(dve)
                dve.tensor_tensor(out_ap, y1[:], rows[2][:], ALU.add).then_inc(s_n, 1)

            for t in range(TILES):
                jobs.wait_drained(dve, f"n{t}")
                dve_stats(dve, steps, t, z[:, t, :], s_st)
            dve.wait_ge(s_row3[1], 16)
            dve.wait_ge(s_row3[2], 16)
            for t in range(TILES):
                affine(t, 0, nrm[:, t, :])
                if t > 0:
                    lo_t(dve, t - 1)
            lo_t(dve, TILES - 1)
            for c in range(2 * C):
                jobs.wait_drained(dve, f"f{c}")
                steps.done(dve.tensor_copy(ut[0][:, c, :], ftmp[:, c % 2, :]))
                steps.wait(dve)
                dve.tensor_tensor(ut[1][:, c, :], ftmp[:, c % 2, :], ut[0][:, c, :].bitcast(FP32),
                                  ALU.subtract).then_inc(s_fd, 1)
            dve.wait_ge(s_nb, TILES)

            def result(t):
                affine(t, 1, y2[:, t % 2, :])
                dve.wait_ge(s_n, TILES + t + 1)
                dve.tensor_tensor(xo[:, t, :], y2[:, t % 2, :], xo[:, t, :], ALU.add).then_inc(s_o, 1)

            for t in range(TILES):
                s = jobs.wait_filled(dve, f"p{t}")
                dve.tensor_tensor(z[:, t, :], ps[s][0:R, 0:D], nrm[:, t, :], ALU.add).then_inc(jobs.drained[s], 1)
                jobs.wait_drained(dve, f"p{t}")
                dve_stats(dve, steps, t, z[:, t, :], s_st)
                if t >= 2:
                    if t >= 4:
                        dve.wait_ge(s_o, t - 3)
                    result(t - 2)
            for t in (TILES - 2, TILES - 1):
                dve.wait_ge(s_o, t - 1)
                result(t)

        @block.scalar
        def _(act):
            for t in range(TILES):
                s = jobs.wait_filled(act, f"n{t}")
                act.activation(z[:, t, :], ps[s][0:R, 0:D], ACT.Copy).then_inc(jobs.drained[s], 1)

            def normalise(t, n):
                act.wait_ge(s_rs, n * TILES + t + 1)
                if t >= 2:
                    act.wait_ge(s_n, n * TILES + t - 1)
                act.activation(xn[:, t % 2, :], z[:, t, :], ACT.Identity, bias=nmr[:, t:t + 1],
                               scale=rstd[:, t:t + 1]).then_inc(s_hn, 1)

            for t in range(TILES):
                normalise(t, 0)
                if t > 0:
                    hi_t(act, t - 1)
            hi_t(act, TILES - 1)
            for c in range(2 * C):
                s = jobs.wait_filled(act, f"f{c}")
                if c >= 2:
                    act.wait_ge(s_fd, c - 1)
                act.activation(halves(ftmp[:, c % 2, :]), wide(s), ACT.Relu,
                               bias=b1c3[:, c:c + 1]).then_inc(jobs.drained[s], 1)
            for t in range(TILES):
                normalise(t, 1)

        @block.tensor
        def _(pe):
            for t in range(TILES):
                pe_transposes(pe, jobs, f"n{t}", 0, lambda b: acc[:, b, t_slice(t)], C, 128, R)
            for t in range(TILES):
                pe.wait_ge(s_n, t + 1)
                pe_transposes(pe, jobs, f"a{t}", 0, lambda b: nrm[:, t, b * 128:(b + 1) * 128], C, R, 128)
            jobs.wait_drained(pe, f"a{TILES - 1}")
            for c in range(2 * C):
                if c % C == 0:
                    pe.wait_ge(s_wsp3[1 + c // C], C * (LAYERS + 1))
                lhs, rhs = proj(w[1 + c // C], yt)
                pe_wide(pe, jobs, f"f{c}", 0, lhs(c % C), rhs, C)
            pe.wait_ge(s_fd, 2 * C)
            pe.wait_ge(s_wsp3[0], C * (2 * LAYERS + 1))
            pe.wait_ge(s_wsp3[1], C * (LAYERS + 2))
            for t in range(TILES):
                pe_natural(pe, jobs, f"p{t}", 0, lambda i, kk: ut[i][:, kk, t_slice(t)],
                           lambda j, kk: w[kk // C][j][:, kk % C, :], 2 * C)


INPUTS = ["x", "src", "dst", "node_vec1"]
INPUTS += [f"L{n}_gnn_{p}" for n in (0, 1) for p in ("W1", "b1", "W2", "b2")]
INPUTS += [f"L2_gnn_{p}" for p in ("f_w1", "f_b1", "f_w2", "f_b2", "s1_w", "s1_b", "b1_w", "b1_b", "wq", "bq", "wk",
                                   "bk", "wv", "bv", "wo", "bo", "s2_w", "s2_b", "b2_w", "b2_b", "m_w1", "m_b1",
                                   "m_w2", "m_b2")]
INPUTS += [f"L3_gnn_{p}" for p in ("Wq", "bq", "Wk", "bk", "Wv", "bv", "Ws", "bs", "W1", "b1", "W2", "b2", "ln_g",
                                   "ln_b")]


def program(nc, shapes):
    a = {n: nc.dram_tensor(n, s, mybir.dt.from_np(d), kind="ExternalInput").ap() for n, (s, d) in shapes.items()}
    out = nc.dram_tensor("out", [N, D], FP32, kind="ExternalOutput").ap()
    build(nc, a, out)


def kernel(**inputs):
    import concourse.bacc as bacc
    from concourse.bass_utils import run_bass_kernel_spmd

    nc = bacc.Bacc("TRN2", target_bir_lowering=False, num_devices=1)
    arrays = {n: np.ascontiguousarray(inputs[n]) for n in INPUTS}
    program(nc, {n: (list(v.shape), v.dtype) for n, v in arrays.items()})
    r = run_bass_kernel_spmd(nc, [arrays], core_ids=[0])
    return r.results[0]["out"]
```

```python
from contextlib import ExitStack

import concourse.bass as bass
import numpy as np
from concourse import mybir

FP32, F32R = mybir.dt.float32, mybir.dt.float32r
BF16, FP16, I32 = mybir.dt.bfloat16, mybir.dt.float16, mybir.dt.int32
ALU = mybir.AluOpType
ACT = mybir.ActivationFunctionType

N, D, E = 625, 512, 20000
TILES, R = 5, 125
C = D // 128
H2 = 314
W = 2 * H2
SLOTS = 4
PASSES = ((0, 0), (0, 1), (1, 0))
NOEDGE = -1.0e30
EPS = 1e-5
BLOCKS, HEADS2 = 4, 4
LAYERS, HEADS3 = 2, 8
SCALE2, SCALE3 = float(np.sqrt(D // HEADS2)), float(np.sqrt(D // HEADS3))
HID = 64
RING_P = 5
LAG = 3
SMALL_RING = 8
COND = 16
ET = E // R
CHUNKS = 5
CT = ET // CHUNKS
PACK = 4096.0

ROUND = 1.5 * 2 ** 23


class Jobs:

    def __init__(self, ring, names, times=1):
        self.filled, self.drained, counts = ring
        self.at = {n: (i % SLOTS, i // SLOTS) for i, n in enumerate(names)}
        assert len(self.at) == len(names)
        self.before = list(counts)
        self.uses = [sum(i % SLOTS == s for i in range(len(names))) for s in range(SLOTS)]
        counts[:] = [b + times * n for b, n in zip(counts, self.uses)]

    def count(self, name, it):
        s, k = self.at[name]
        return it * self.uses[s] + (self.before[s] + k)

    def wait_filled(self, eng, name, it=0):
        s = self.at[name][0]
        eng.wait_ge(self.filled[s], self.count(name, it) + 1)
        return s

    def wait_drained(self, eng, name, it=0):
        eng.wait_ge(self.drained[self.at[name][0]], self.count(name, it) + 1)

    def acquire(self, eng, name, it=0):
        n = self.count(name, it)
        if not isinstance(n, int) or n > 0:
            eng.wait_ge(self.drained[self.at[name][0]], n)
        return self.at[name][0]


class Steps:

    def __init__(self, sem, per_body=0):
        self.sem, self.per_body, self.n, self.it = sem, per_body, 0, 0

    def body(self, it):
        assert isinstance(it, int) and it == 0 or self.n in (0, self.per_body), (self.sem, self.n)
        self.it, self.n = it, 0

    def done(self, ins):
        ins.then_inc(self.sem, 1)
        self.n += 1

    def wait(self, eng):
        eng.wait_ge(self.sem, self.it * self.per_body + self.n)

    def end(self):
        assert self.n == self.per_body, (self.n, self.per_body)


def halves(ap):
    return ap.rearrange("p (a b) -> p a b", a=2)


def attention_jobs(heads, spot1, spot2):
    names = []
    for h in range(heads):
        for t in range(TILES):
            names.append(f"s{h}_{t}")
            u = h * TILES + t - LAG
            if u >= 0:
                names.append(f"t{u // TILES}_{u % TILES}")
            if u >= 0 and u % TILES == TILES - 1:
                names += spot1(h)
                names.append(f"pv{u // TILES}")
            if t == TILES - 2:
                names += spot2(h)
    for u in range(heads * TILES - LAG, heads * TILES):
        names.append(f"t{u // TILES}_{u % TILES}")
    return names + [f"pv{heads - 1}"]


def build(nc, a, out):
    sizes = dict(res=10240, mask=12576, w0=16384, w1=16384, w2=16384, yt=20480, qk=20096, v=20480,
                 p=12576, pt=25120, ot=20096, ws=8192, cond=2528, rows=6144, small=4096)
    origin, at = (nc.sbuf_base + 31) // 32 * 32, {}
    for name, size in sizes.items():
        at[name] = origin
        origin += size
    assert origin <= nc.sbuf_usable_end, (origin, nc.sbuf_usable_end)

    def sb(name, region, shape, dtype=FP32, skip=0):
        return nc.alloc_sbuf_tensor_at(name, shape, dtype, offset=at[region] + skip, align_bytes=16)

    small_used = [0]

    def small(name, shape, dtype=FP32):
        t = sb(name, "small", shape, dtype, small_used[0])
        small_used[0] += (int(np.prod(shape[1:])) * 4 + 31) // 32 * 32
        assert small_used[0] <= sizes["small"], small_used
        return t

    def pair(name, region, shape, skip=0):
        size = int(np.prod(shape[1:])) * 4
        return [sb(name + "_hi", region, shape, F32R, skip), sb(name + "_lo", region, shape, F32R, skip + size)]

    ps = [nc.alloc_psum_tensor(f"ps{s}", [128, 1024], FP32) for s in range(SLOTS)]

    def wide(s, p0=0, p1=128):
        return ps[s][p0:p1, :].rearrange("p (a b) -> p a b", a=2)[:, :, 0:H2]

    def blocks(s, n, p=128):
        return ps[s][0:p, 0:128 * n].rearrange("p (a b) -> p a b", a=n)[:, :, 0:R]

    res = sb("res", "res", [R, TILES, D])
    mask = sb("mask", "mask", [R, TILES, W])
    x = sb("x", "v", [R, TILES, D])
    x_spill = nc.dram_tensor("x_spill", [R, TILES, D], FP32, kind="Internal").ap()
    mask_spill = nc.dram_tensor("mask_spill", [R, TILES, W], FP32, kind="Internal").ap()
    w_raw = [sb(f"w{s}_raw", f"w{s}", [128, C, D], FP32, C * D * 4) for s in range(3)]
    w = [pair(f"w{s}", f"w{s}", [128, C, D]) for s in range(3)]
    ident = small("ident", [128, 128])
    stats = small("stats", [R, TILES, 6])
    mv = small("mv", [R, TILES, 2])
    rstd = small("rstd", [R, TILES])
    nmr = small("nmr", [R, TILES])
    neg_half = small("neg_half", [R, 1])
    offset = small("offset", [R, 1])
    low = small("low", [R, SMALL_RING])
    denom = small("denom", [R, SMALL_RING])
    rinv = small("rinv", [R, SMALL_RING])
    b0c = small("b0c", [128, C])
    bq2 = small("bq2", [128, BLOCKS * C])
    bk2 = small("bk2", [128, BLOCKS * C])
    bm2 = small("bm2", [128, BLOCKS * C])
    bq3 = small("bq3", [128, LAYERS * C])
    bk3 = small("bk3", [128, LAYERS * C])
    bs3 = small("bs3", [128, LAYERS * C])
    b1c3 = small("b1c3", [128, 2 * C])
    xn = sb("xn", "p", [R, 2, D])
    y1 = sb("y1", "p", [R, D], skip=2 * D * 4)
    y2 = sb("y2", "p", [R, 2, D], skip=3 * D * 4)
    vtmp = sb("vtmp", "ot", [R, 2, D])
    ftmp = sb("ftmp", "p", [128, 2, W])
    prob = sb("prob", "p", [R, RING_P, W])
    yt = pair("yt", "yt", [128, C, W])
    q = [pair(f"q{n}", "qk", [128, W], 2 * n * W * 4) for n in range(2)]
    k = [pair(f"k{n}", "qk", [128, W], (4 + 2 * n) * W * 4) for n in range(2)]
    v = pair("v", "v", [R, TILES, D])
    ht = pair("ht", "v", [128, C, W])
    pt = pair("pt", "pt", [R, TILES, W])
    ot = pair("ot", "ot", [128, C, W])
    rows = [sb(f"row{n}", "rows", [R, D], FP32, n * D * 4) for n in range(3)]
    cond = sb("cond", "cond", [128, W], F32R)
    ws_raw = sb("ws_raw", "ws", [128, 2, D])
    ws = sb("ws", "ws", [128, 2, D], F32R, 2 * D * 4)

    def sem(name):
        return nc.alloc_semaphore(name)

    def row(ap):
        return ap.rearrange("(a n) -> a n", a=1).to_broadcast([R, D])

    s_own = sem("waits_of_their_own")

    def own(eng):
        eng.sem_inc(s_own, 1)

    def matmul3(pe, out_ap, lhs, rhs, count, ready=None):
        for kk in range(count):
            if ready:
                if kk == 0:
                    own(pe)
                ready(kk)
            for n, (i, j) in enumerate(PASSES):
                ins = pe.matmul(out_ap, lhs(i, kk), rhs(j, kk), start=kk == 0 and n == 0,
                                stop=kk == count - 1 and n == 2)
        return ins

    def pe_wide(pe, jobs, name, it, lhs, rhs, count, m=128, ready=None, parts=(0, 1)):
        s = jobs.acquire(pe, name, it) if 0 in parts else jobs.at[name][0]
        for half in parts:
            ins = matmul3(pe, ps[s][0:m, 512 * half:512 * half + H2], lhs,
                          lambda j, kk: rhs(j, kk)[:, H2 * half:H2 * half + H2], count, None if half else ready)
        if 1 in parts:
            ins.then_inc(jobs.filled[s], 1)

    def pe_natural(pe, jobs, name, it, lhs, rhs, count, ready=None):
        s = jobs.acquire(pe, name, it)
        matmul3(pe, ps[s][0:R, 0:D], lhs, rhs, count, ready).then_inc(jobs.filled[s], 1)

    def pe_transposes(pe, jobs, name, it, source, count, rows_in, rows_out):
        s = jobs.acquire(pe, name, it)
        for b in range(count):
            ins = pe.transpose(ps[s][0:rows_out, 128 * b:128 * b + rows_in], source(b),
                               ident[0:rows_in, 0:rows_in])
        ins.then_inc(jobs.filled[s], 1)

    def t_slice(t):
        return slice(t * R, (t + 1) * R)

    def proj(weights, act):
        return (lambda c: (lambda i, kk: weights[i][:, kk, c * 128:(c + 1) * 128])), (lambda j, kk: act[j][:, kk, :])

    def split_weights(pool, steps, slot, split_sem, pieces=range(C), cols=D):
        for kk in pieces:
            own(pool)
            steps.done(pool.tensor_scalar(w[slot][0][:, kk, 0:cols], w_raw[slot][:, kk, 0:cols], 1.0, 1.0,
                                          ALU.mult, ALU.mult))
            steps.wait(pool)
            pool.tensor_tensor(w[slot][1][:, kk, 0:cols], w_raw[slot][:, kk, 0:cols],
                               w[slot][0][:, kk, 0:cols].bitcast(FP32), ALU.subtract).then_inc(split_sem, 1)

    def dve_stats(dve, steps, t, source, stats_done):
        steps.done(dve.bn_stats(stats[:, t, :], source))
        steps.wait(dve)
        own(dve)
        dve.bn_aggr(mv[:, t, :], stats[:, t, :]).then_inc(stats_done, 1)

    def pool_rstd(pool, steps, t, rstd_done):
        own(pool)
        steps.done(pool.tensor_scalar(rstd[:, t:t + 1], mv[:, t, 1:2], EPS, 1.0, ALU.add, ALU.mult))
        steps.wait(pool)
        steps.done(pool.tensor_tensor(rstd[:, t:t + 1], rstd[:, t:t + 1], neg_half[:, :], ALU.pow))
        steps.wait(pool)
        own(pool)
        pool.tensor_scalar(nmr[:, t:t + 1], mv[:, t, 0:1], rstd[:, t:t + 1], -1.0, ALU.mult,
                           ALU.mult).then_inc(rstd_done, 1)

    def act_hi(act, jobs, name, it, out_ap, in_ap, hi_done, bias=0.0):
        jobs.wait_filled(act, name, it)
        act.activation(out_ap, in_ap, ACT.Identity, bias=bias).then_inc(hi_done, 1)

    def pe_scores(pe, jobs, h, t, it, qs, ks, r0, r1):
        pe_wide(pe, jobs, f"s{h}_{t}", it, lambda i, kk: qs[i][r0:r1, t_slice(t)], lambda j, kk: ks[j][r0:r1, :], 1, R)

    def pe_prob_transposes(pe, jobs, u, it, units, scaled):
        pe.wait_ge(scaled, it * units + u + 1)
        pe_transposes(pe, jobs, f"t{u // TILES}_{u % TILES}", it,
                      lambda b: prob[:, u % RING_P, b * R:(b + 1) * R], TILES, R, R)

    def pe_values(pe, jobs, h, c, it):
        for part, tile in ((0, 2), (1, TILES - 1)):
            jobs.wait_drained(pe, f"t{h}_{tile}", it)
            if part == 0:
                own(pe)
            pe_wide(pe, jobs, f"pv{h}", it, lambda i, kk: v[i][:, kk, c * 128:(c + 1) * 128],
                    lambda j, kk: pt[j][:, kk, :], TILES, parts=(part,))

    def dve_scores(dve, jobs, u, it, scale):
        name = f"s{u // TILES}_{u % TILES}"
        s = jobs.wait_filled(dve, name, it)
        o = u % SMALL_RING
        own(dve)
        dve.tensor_tensor_reduce(out=halves(prob[:, u % RING_P, :]), in0=wide(s, 0, R),
                                 in1=halves(mask[:, u % TILES, :]), scale=-scale, scalar=1e20, op0=ALU.add,
                                 op1=ALU.min, accum_out=low[:, o:o + 1]).then_inc(jobs.drained[s], 1)

    def act_exp(act, jobs, u, it, exp_done):
        jobs.wait_drained(act, f"s{u // TILES}_{u % TILES}", it)
        o = u % SMALL_RING
        act.activation(prob[:, u % RING_P, :], prob[:, u % RING_P, :], ACT.Exp, bias=low[:, o:o + 1], scale=-1.0,
                       accum_out=denom[:, o:o + 1]).then_inc(exp_done, 1)

    def dve_inverse(dve, steps, u, it, units, exp_done, rinv_done):
        dve.wait_ge(exp_done, it * units + u + 1)
        o = u % SMALL_RING
        steps.done(dve.tensor_scalar(rinv[:, o:o + 1], denom[:, o:o + 1], 1e-16, None, ALU.add))
        steps.wait(dve)
        dve.reciprocal(rinv[:, o:o + 1], rinv[:, o:o + 1]).then_inc(rinv_done, 1)

    def pool_scale(pool, u, it, units, rinv_done, scaled):
        pool.wait_ge(rinv_done, it * units + u + 1)
        o = u % SMALL_RING
        own(pool)
        pool.tensor_scalar(prob[:, u % RING_P, :], prob[:, u % RING_P, :], rinv[:, o:o + 1], 1.0, ALU.mult,
                           ALU.mult).then_inc(scaled, 1)

    def pt_view(part, t):
        return pt[part][:, :, t_slice(t)]

    cnt = sb("cnt", "p", [R, TILES, W])
    ids = [sb(n, "rows", [R, ET], I32, skip) for n, skip in (("dst_i", 0), ("src_i", 640))]
    dstf = sb("dstf", "rows", [R, ET], FP32, 1280)
    srcf = sb("srcf", "rows", [R, ET], FP32, 1920)
    srcm = sb("srcm", "rows", [R, ET], FP32, 2560)
    srcv = sb("srcv", "rows", [R, ET], FP32, 3200)
    upper = sb("upper", "rows", [R, ET], FP32, 3840)
    node = sb("node", "qk", [R, W], FP16)
    OH = 8
    oh_d = sb("oh_d", "qk", [R, OH, W], BF16, 1280)
    oh_s = sb("oh_s", "qk", [R, OH, H2], BF16, 1280 + OH * W * 2)
    HALF = TILES * H2 * 4 + 8
    words = sb("words", "pt", [R, TILES, H2])
    quotient = sb("quotient", "pt", [R, TILES, H2], FP32, HALF)
    above = sb("above", "ot", [R, TILES, H2])
    below = sb("below", "ot", [R, TILES, H2], FP32, HALF)
    h_pair = pair("h", "yt", [R, TILES, D])

    def bank(n, cols=H2):
        return ps[n // 2][0:R, 512 * (n % 2):512 * (n % 2) + cols]

    s_ids, s_x, s_node, s_idf = sem("ids_loaded"), sem("x_loaded"), sem("node_made"), sem("ids_ready")
    s_wl = [sem(f"w{n}_loaded") for n in range(3)]
    s_small = sem("columns_loaded")
    s_oh, s_ohu = sem("onehots_ready"), sem("onehots_used")
    s_cf, s_words = sem("counts_filled"), sem("counts_moved")
    s_last = sem("last_counts_added")
    s_quot, s_above, s_below = sem("quotients"), sem("counts_above"), sem("counts_below")
    s_added, s_zero = sem("counts_added"), sem("counts_set")
    s_st, s_rs, s_hn, s_hh, s_hl = sem("a_stats"), sem("a_rstd"), sem("a_norm"), sem("a_hhi"), sem("a_hlo")
    s_pa, s_va = sem("a_pool_steps"), sem("a_dve_steps")
    s_ws0 = [sem(f"l0_w{n}_split") for n in range(3)]

    with nc.Block() as block:
        @block.sync
        def _(sp):
            sp.dma_start(ids[0][:], a["dst"].rearrange("(p t) -> p t", t=ET)).then_inc(s_ids, 16)
            sp.dma_start(ids[1][:], a["src"].rearrange("(p t) -> p t", t=ET)).then_inc(s_ids, 16)
            sp.dma_start(x[:], a["x"].rearrange("(t p) f -> p t f", p=R)).then_inc(s_x, 16)
            for n, name in enumerate(("L0_gnn_W1", "L0_gnn_W2")):
                sp.dma_start(w_raw[n][:], a[name].rearrange("(c p) n -> p c n", p=128)).then_inc(s_wl[n], 16)
            with nc.allow_non_contiguous_dma("bias columns"):
                for dst, name, pat in ((b0c, "L0_gnn_b1", 1), (bq2, "L2_gnn_bq", 2), (bk2, "L2_gnn_bk", 2),
                                       (bm2, "L2_gnn_m_b1", 2), (bq3, "L3_gnn_bq", 2), (bk3, "L3_gnn_bk", 2),
                                       (bs3, "L3_gnn_bs", 2), (b1c3, "L3_gnn_b1", 1)):
                    src = a[name] if pat == 1 else a[name].rearrange("b n -> (b n)")
                    sp.dma_start(dst[:], src.rearrange("(c p) -> p c", p=128)).then_inc(s_small, 16)
            sp.wait_ge(s_small, 8 * 16)

        @block.gpsimd
        def _(pool):
            steps = Steps(s_pa)
            pool.iota(node[:], [[1, W]], base=0, channel_multiplier=0,
                      allow_small_or_imprecise_dtypes=True).then_inc(s_node, 1)
            steps.done(pool.memset(ident[:], 0.0))
            steps.done(pool.memset(cnt[:], 0.0))
            steps.wait(pool)
            steps.done(pool.affine_select(out=ident[:], in_=ident[:], compare_op=ALU.not_equal, fill=1.0, base=0,
                                          pattern=[[-1, 128]], channel_multiplier=1))
            steps.done(pool.memset(neg_half[:], -0.5))
            steps.done(pool.memset(offset[:], -2001.0 / PACK))
            steps.wait(pool)
            for m in range(TILES):
                block_m = cnt[:, m, t_slice(m)]
                pool.tensor_tensor(block_m, block_m, ident[0:R, 0:R], ALU.add).then_inc(s_zero, 1)

            def add(c):
                for m in range(TILES):
                    n = c * TILES + m
                    before = (s_zero, TILES) if c == 0 else (s_added, 2 * (n - TILES) + 2)
                    pool.wait_ge(*before)
                    pool.wait_ge(s_above, n + 1)
                    if c < CHUNKS - 1:
                        pool.wait_ge(s_below, n + 1)
                        pool.tensor_tensor(cnt[:, m, 0:H2], cnt[:, m, 0:H2], below[:, m, :],
                                           ALU.add).then_inc(s_added, 1)
                    pool.tensor_tensor(cnt[:, m, H2:W], cnt[:, m, H2:W], above[:, m, :],
                                       ALU.add).then_inc(s_added if c < CHUNKS - 1 else s_last, 1)

            for t in range(TILES):
                pool.wait_ge(s_st, t + 1)
                pool_rstd(pool, steps, t, s_rs)
            for c in range(CHUNKS):
                add(c)
                if c < 2:
                    pool.wait_ge(s_wl[c], 16)
                    split_weights(pool, steps, c, s_ws0[c])

        @block.vector
        def _(dve):
            steps = Steps(s_va)
            dve.wait_ge(s_ids, 32)
            dve.tensor_copy(dstf[:], ids[0][:]).then_inc(s_idf, 1)
            steps.done(dve.tensor_copy(srcf[:], ids[1][:]))
            steps.wait(dve)
            steps.done(dve.tensor_scalar(upper[:], srcf[:], float(H2), None, ALU.is_ge))
            steps.wait(dve)
            dve.tensor_scalar(srcv[:], upper[:], PACK - 1, 1.0, ALU.mult, ALU.add).then_inc(s_idf, 1)
            dve.scalar_tensor_tensor(out=srcm[:], in0=upper[:], scalar=-float(H2), in1=srcf[:], op0=ALU.mult,
                                     op1=ALU.add).then_inc(s_idf, 1)
            dve.wait_ge(s_idf, 3)
            dve.wait_ge(s_node, 1)

            def onehots(tile, o, first):
                if not first:
                    dve.wait_ge(s_ohu, tile - OH + 1)
                dve.tensor_scalar(oh_d[:, o, :], node[:], dstf[:, bass.ds(tile, 1)], None,
                                  ALU.is_equal).then_inc(s_oh, 1)
                dve.tensor_scalar(oh_s[:, o, :], node[:, 0:H2], srcm[:, bass.ds(tile, 1)],
                                  srcv[:, bass.ds(tile, 1)], ALU.is_equal, ALU.mult).then_inc(s_oh, 1)

            def unpack_above(c, tiles):
                for m in tiles:
                    n = c * TILES + m
                    dve.wait_ge(s_quot, n + 1)
                    if c > 0:
                        dve.wait_ge(s_added, 2 * (n - TILES) + 2)
                    dve.tensor_scalar(above[:, m, :], quotient[:, m, :], ROUND, -ROUND, ALU.add,
                                      ALU.add).then_inc(s_above, 1)

            def unpack_below(c, tiles):
                for m in tiles:
                    n = c * TILES + m
                    dve.wait_ge(s_above, n + 1)
                    dve.scalar_tensor_tensor(out=below[:, m, :], in0=above[:, m, :], scalar=-PACK,
                                             in1=words[:, m, :], op0=ALU.mult, op1=ALU.add).then_inc(s_below, 1)

            for c in range(CHUNKS):
                for o in range(OH):
                    onehots(c * CT + o, o, c == 0)
                if c == 0:
                    dve.wait_ge(s_x, 16)
                    for t in range(TILES):
                        dve_stats(dve, steps, t, x[:, t, :], s_st)
                for o in range(OH):
                    onehots(c * CT + OH + o, o, False)
                    if c > 0 and o < TILES:
                        unpack_above(c - 1, (o,))
                    if c > 0 and o > OH - TILES - 1:
                        unpack_below(c - 1, (o + TILES - OH,))
                with dve.Fori(2, CT // OH) as j:
                    for o in range(OH):
                        onehots(j * OH + (c * CT + o), o, False)
                if c == 1:
                    for t in range(TILES):
                        dve.wait_ge(s_hh, t + 1)
                        dve.tensor_tensor(h_pair[1][:, t, :], res[:, t, :], h_pair[0][:, t, :].bitcast(FP32),
                                          ALU.subtract).then_inc(s_hl, 1)
            unpack_above(CHUNKS - 1, range(TILES))
            unpack_below(CHUNKS - 1, range(TILES))
            for m in range(TILES):
                dve.wait_ge(s_below, (CHUNKS - 1) * TILES + m + 1)
                dve.tensor_tensor(cnt[:, m, 0:H2], cnt[:, m, 0:H2], below[:, m, :], ALU.add).then_inc(s_last, 1)

        @block.scalar
        def _(act):
            act.wait_ge(s_x, 16)
            for t in range(TILES):
                act.wait_ge(s_rs, t + 1)
                act.activation(res[:, t, :], x[:, t, :], ACT.Relu, bias=nmr[:, t:t + 1],
                               scale=rstd[:, t:t + 1]).then_inc(s_hn, 1)
                act.wait_ge(s_hn, t + 1)
                act.activation(h_pair[0][:, t, :], res[:, t, :], ACT.Copy).then_inc(s_hh, 1)
            for c in range(CHUNKS):
                act.wait_ge(s_cf, c + 1)
                for m in range(TILES):
                    n = c * TILES + m
                    if c > 0:
                        act.wait_ge(s_below, n - TILES + 1)
                    act.activation(words[:, m, :], bank(n % 8), ACT.Copy).then_inc(s_words, 1)
                for m in range(TILES):
                    act.wait_ge(s_words, c * TILES + m + 1)
                    act.activation(quotient[:, m, :], words[:, m, :], ACT.Identity, bias=offset[:, 0:1],
                                   scale=1 / PACK).then_inc(s_quot, 1)

        @block.tensor
        def _(pe):
            def edge_tile(c, tile, o, start, stop):
                pe.wait_ge(s_oh, 2 * tile + 2)
                for m in range(TILES):
                    ins = pe.matmul(bank((c * TILES + m) % 8), oh_d[:, o, t_slice(m)], oh_s[:, o, :], start=start,
                                    stop=stop)
                ins.then_inc(s_ohu, 1)
                return ins

            for c in range(CHUNKS):
                if c > 0:
                    pe.wait_ge(s_words, (c + 1) * TILES - 8)
                for o in range(OH):
                    edge_tile(c, c * CT + o, o, o == 0, False)
                with pe.Fori(1, CT // OH - 1) as j:
                    for o in range(OH):
                        edge_tile(c, j * OH + (c * CT + o), o, False, False)
                for o in range(OH):
                    ins = edge_tile(c, c * CT + CT - OH + o, o, False, o == OH - 1)
                pe.wait_ge(s_ohu, (c + 1) * CT)
                pe.sem_inc(s_cf, 1)

    bi = pair("bi", "pt", [R, TILES, W])
    ai_hi = sb("ai_hi", "ot", [R, TILES, W], F32R)
    ai_lo = sb("ai_lo", "ot", [R, 3, W], F32R, TILES * W * 4)
    ai_lo2 = sb("ai_lo2", "v", [R, 2, W], F32R, TILES * D * 4)

    def ai(part, t):
        return ai_hi[:, t, :] if part == 0 else ai_lo[:, t, :] if t < 3 else ai_lo2[:, t - 3, :]

    agg = pair("agg", "qk", [128, C, W])
    ft = pair("ft", "yt", [128, C, W])
    rtmp = sb("rtmp", "rows", [128, 2, W])
    b2row = sb("b2row", "cond", [R, D])
    ht1 = pair("ht1", "qk", [128, C, W])
    r_sum = sb("r_sum", "pt", [R, TILES, HID], FP32, 8 * W * 4)
    r_nat = pair("r_nat", "yt", [R, TILES, 128])
    r_act = sb("r_act", "yt", [R, TILES, HID], FP32, 2 * TILES * 128 * 4)
    b1row = sb("b1row", "yt", [R, HID], FP32, 2 * TILES * 128 * 4 + TILES * HID * 4)
    gt = pair("gt", "rows", [128, W])
    MASKS_AFTER_G, MASKS_AFTER_F = ((0, 1), (2, 3), (4,), (5, 6)), ((7,), (8,), (9,), ())
    W2COL = 4 * HID
    w_l1 = [t[:].rearrange("p c n -> p (c n)") for t in (w_raw[2], w[2][0], w[2][1])]

    scratch = sb("scratch", "v", [R, W], FP32, TILES * D * 4 + 2 * W * 4)
    one_row = sb("one_row", "v", [1, D], FP32, TILES * D * 4 + 3 * W * 4)
    noise = sb("noise", "pt", [64, W])
    phase = sb("phase", "pt", [64, W], FP32, W * 4)
    turns = sb("turns", "pt", [64, W], I32, 2 * W * 4)
    angle = sb("angle", "pt", [64, W], FP32, 3 * W * 4)
    emb = sb("emb", "pt", [64, W], FP32, 4 * W * 4)
    pre = sb("pre", "pt", [COND, W], FP32, 5 * W * 4)
    sig = sb("sig", "pt", [COND, W], FP32, 6 * W * 4)
    cond_hi = sb("cond_hi", "pt", [128, W], F32R, 7 * W * 4)
    CONST = 8 * W * 4 + TILES * HID * 4
    act1 = sb("act1", "pt", [32, W], FP32, CONST)
    f_w1 = sb("f_w1", "pt", [64, COND], FP32, CONST + W * 4)
    f_w2 = sb("f_w2", "pt", [COND + 1, 128], FP32, CONST + W * 4 + 64)
    f_b1 = sb("f_b1", "pt", [COND, 1], FP32, CONST + W * 4 + 592)
    freq = sb("freq", "pt", [64, 1], FP32, CONST + W * 4 + 624)
    quarter = sb("quarter", "pt", [64, 1], FP32, CONST + W * 4 + 656)
    shift = sb("shift", "pt", [64, 1], FP32, CONST + W * 4 + 688)
    TWO_PI_HIGH = 6.28125
    TWO_PI_LOW = 2 * np.pi - TWO_PI_HIGH

    names = [f"b{t}" for t in range(TILES)] + [f"g{c}" for c in range(C)] + [f"f{c}" for c in range(C)]
    tail = ["o0", "o1", "o2", "c1", "o3", "y0", "o4", "y1", "r", "y2", "y3", "y4", "ga", "c2"]
    names += tail
    names += [f"p{t}" for t in range(TILES)]
    ring = ([sem(f"slot{s}_filled") for s in range(SLOTS)], [sem(f"slot{s}_drained") for s in range(SLOTS)], [0] * SLOTS)
    jobs = Jobs(ring, names)
    s_hi, s_ai, s_fd = sem("g_hi"), sem("g_ai_split"), sem("g_f_split")
    s_row, s_xb, s_st, s_rs, s_hn = sem("g_rows"), sem("g_bias_added"), sem("g_stats"), sem("g_rstd"), sem("g_norm")
    s_pg, s_vg, s_w2, s_r, s_pad, s_w2z = (sem("g_pool_steps"), sem("g_dve_steps"), sem("g_w2_split"),
                                           sem("g_r_split"), sem("g_pads"), sem("g_w2_zeroed"))
    s_r1 = sem("g_b1row")
    s_in, s_k, s_fw, s_sp = sem("c_loaded"), sem("c_constants"), sem("c_f_w2_ready"), sem("spilled")
    s_max, s_ln, s_m = sem("c_clamped"), sem("c_logs"), sem("c_masks")
    s_ang, s_sin, s_ex, s_a1 = sem("c_angle"), sem("c_sin"), sem("c_exp"), sem("c_act1")
    s_c2, s_xs, s_wszero, s_wsz = sem("c_cond_hi"), sem("x_spilled"), sem("ws_zeroed"), sem("ws_constant_rows")
    s_wsl, s_wss, s_rows = sem("ws_loaded"), sem("ws_split"), [sem(f"row{n}_loaded") for n in range(3)]
    s_wl2 = [sem(f"l2_w{n}_loaded") for n in range(3)]
    s_wsp = [sem(f"l2_w{n}_split") for n in range(3)]

    def block_of(name, it):
        ap = a[name][bass.ds(it, 1)] if not isinstance(it, int) else a[name][it:it + 1]
        return ap

    def load_w(sp, n, name, it, loaded):
        sp.dma_start(w_raw[n][:], block_of(name, it).rearrange("a (c p) n -> p (a c) n", p=128)).then_inc(loaded[n], 16)

    def load_ws(sp, which, it):
        for quad in range(4):
            for n, kind in enumerate("sb"):
                sp.dma_start(ws_raw[32 * quad:32 * quad + COND, n, :],
                             block_of(f"L2_gnn_{kind}{which}_w", it).rearrange("a c n -> (a c) n")).then_inc(s_wsl, 16)
                sp.dma_start(ws_raw[32 * quad + COND:32 * quad + COND + 1, n, :],
                             block_of(f"L2_gnn_{kind}{which}_b", it)).then_inc(s_wsl, 16)
    WS_DMAS = 16

    def split_ws(pool, steps):
        own(pool)
        steps.done(pool.tensor_scalar(ws[:], ws_raw[:], 1.0, 1.0, ALU.mult, ALU.mult))
        for n, quad in enumerate((1, 3)):
            steps.wait(pool)
            rows_q = slice(32 * quad, 32 * quad + 32)
            steps.done(pool.tensor_tensor(ws[rows_q], ws_raw[rows_q], ws[rows_q].bitcast(FP32), ALU.subtract))
        steps.wait(pool)
        pool.sem_inc(s_wss, 2)

    def load_row(sp, n, name, it):
        sp.dma_start(rows[n][:], block_of(name, it).to_broadcast([R, D])).then_inc(s_rows[n], 16)

    with nc.Block() as block:
        @block.sync
        def _(sp):
            sp.dma_start(b2row[:], row(a["L0_gnn_b2"])).then_inc(s_row, 16)
            sp.wait_ge(s_wszero, 1)
            for quad in range(4):
                sp.dma_start(ws_raw[32 * quad + COND + 1:32 * quad + COND + 2, 0, :], one_row[:]).then_inc(s_wsz, 16)
            sp.wait_ge(s_w2z, 1)
            sp.dma_start(w_raw[2][:].rearrange("p c n -> p (c n)")[:, 0:W2COL].rearrange("p (c n) -> p c n", c=C),
                         a["L1_gnn_W1"].rearrange("(c p) n -> p c n", p=128)).then_inc(s_wl[2], 16)
            sp.dma_start(w_l1[0][0:HID, W2COL:W2COL + D], a["L1_gnn_W2"]).then_inc(s_wl[2], 16)
            sp.dma_start(w_l1[0][HID:HID + 1, W2COL:W2COL + D],
                         a["L1_gnn_b2"].rearrange("(a n) -> a n", a=1)).then_inc(s_wl[2], 16)
            load_ws(sp, 1, 0)
            jobs.wait_filled(sp, f"g{C - 1}")
            sp.dma_start(noise[:, 0:N], a["node_vec1"].rearrange("n a -> a n").to_broadcast([64, N])).then_inc(s_in, 16)
            sp.dma_start(f_w1[:], a["L2_gnn_f_w1"]).then_inc(s_in, 16)
            sp.dma_start(f_b1[:], a["L2_gnn_f_b1"].rearrange("(n a) -> n a", a=1)).then_inc(s_in, 16)
            jobs.wait_filled(sp, f"f{C - 1}")
            load_w(sp, 0, "L2_gnn_wv", 0, s_wl2)
            sp.wait_ge(s_k, 2)
            for quad in range(4):
                cols = slice(32 * quad, 32 * quad + COND)
                sp.dma_start(f_w2[0:COND, cols], a["L2_gnn_f_w2"]).then_inc(s_fw, 16)
                sp.dma_start(f_w2[COND:COND + 1, cols], a["L2_gnn_f_b2"].rearrange("(a n) -> a n", a=1)).then_inc(s_fw, 16)
                sp.dma_start(f_w2[COND:COND + 1, 32 * quad + COND:32 * quad + COND + 2],
                             act1[COND:COND + 1, 0:2]).then_inc(s_fw, 16)
            jobs.wait_filled(sp, f"o{TILES - 1}")
            sp.dma_start(b1row[:], a["L1_gnn_b1"].rearrange("(a n) -> a n", a=1).to_broadcast([R, HID])).then_inc(s_r1, 16)
            load_w(sp, 1, "L2_gnn_wq", 0, s_wl2)
            sp.wait_ge(s_m, 2 * TILES)
            sp.dma_start(mask_spill, cnt[:]).then_inc(s_sp, 16)
            for t in range(TILES):
                jobs.wait_drained(sp, f"p{t}")
                sp.dma_start(x_spill[:, t, :], x[:, t, :]).then_inc(s_xs, 16)
            load_w(sp, 2, "L2_gnn_wk", 0, s_wl2)
            sp.wait_ge(s_fw, 12 * 16)
            sp.wait_ge(s_sp, 16)

        @block.gpsimd
        def _(pool):
            steps = Steps(s_pg)
            steps.done(pool.memset(one_row[:], 1.0))
            steps.wait(pool)
            pool.memset(ws_raw[:], 0.0).then_inc(s_wszero, 1)
            pool.memset(w_l1[0][:, W2COL:W2COL + D], 0.0).then_inc(s_w2z, 1)
            pool.memset(mask[:, :, N:W], 0.0).then_inc(s_pad, 1)
            pool.memset(bi[0][:, :, N:W].bitcast(FP32), 0.0).then_inc(s_pad, 1)
            pool.memset(bi[1][:, :, N:W].bitcast(FP32), 0.0).then_inc(s_pad, 1)
            for t in range(TILES):
                steps.done(pool.tensor_scalar(ai(0, t), cnt[:, t, :], 1.0, 1.0, ALU.mult, ALU.mult))
                steps.wait(pool)
                pool.tensor_tensor(ai(1, t), cnt[:, t, :], ai(0, t).bitcast(FP32),
                                   ALU.subtract).then_inc(s_ai, 1)
            pool.wait_ge(s_row, 16)
            for t in range(TILES):
                pool.tensor_tensor(x[:, t, :], x[:, t, :], b2row[:], ALU.add).then_inc(s_xb, 1)
            pool.wait_ge(s_wl[2], 48)
            steps.done(pool.tensor_scalar(w_l1[1][:, 0:W2COL + D], w_l1[0][:, 0:W2COL + D], 1.0, 1.0, ALU.mult,
                                          ALU.mult))
            steps.wait(pool)
            pool.tensor_tensor(w_l1[2][:, 0:W2COL + D], w_l1[0][:, 0:W2COL + D],
                               w_l1[1][:, 0:W2COL + D].bitcast(FP32), ALU.subtract).then_inc(s_w2, 1)
            pool.wait_ge(s_wsl, WS_DMAS * 16)
            pool.wait_ge(s_wsz, 64)
            split_ws(pool, steps)
            jobs.wait_filled(pool, f"g{C - 1}")
            for count, tile, value in ((1, f_w2, 0.0), (2, act1, 1.0)):
                pool.memset(tile[:], value).then_inc(s_k, 1)
                pool.wait_ge(s_k, count)
            for quad in range(2):
                part = slice(32 * quad, 32 * quad + 32)
                steps.done(pool.iota(freq[part, :], [[0, 1]], base=1, channel_multiplier=1,
                                     allow_small_or_imprecise_dtypes=True))
                steps.done(pool.memset(quarter[part, :], 0.25 * quad))
                steps.done(pool.memset(shift[part, :], float(np.pi / 2) * quad))
                steps.wait(pool)
            pool.memset(noise[:, N:W], 0.0).then_inc(s_k, 1)
            pool.tensor_scalar(freq[:], freq[:], float(np.float32(2 * np.pi / 16)), 1.0, ALU.mult,
                               ALU.mult).then_inc(s_k, 1)
            pool.wait_ge(s_k, 4)
            for t in range(TILES):
                pool.wait_ge(s_st, t + 1)
                pool_rstd(pool, steps, t, s_rs)
            jobs.wait_filled(pool, f"o{TILES - 1}")
            pool.memset(r_nat[0][:].bitcast(FP32), 0.0).then_inc(s_pad, 1)
            pool.memset(r_nat[1][:].bitcast(FP32), 0.0).then_inc(s_pad, 1)
            pool.wait_ge(s_pad, 5)
            pool.memset(r_nat[0][:, :, HID:HID + 1].bitcast(FP32), 1.0).then_inc(s_pad, 1)
            pool.wait_ge(s_wl2[0], 16)
            split_weights(pool, steps, 0, s_wsp[0])
            jobs.wait_filled(pool, "ga")
            for part in yt:
                steps.done(pool.memset(part[:, :, N:W].bitcast(FP32), 0.0))
            for t in range(TILES):
                pool.wait_ge(s_st, TILES + t + 1)
                pool_rstd(pool, steps, t, s_rs)
            jobs.wait_drained(pool, "c2")
            pool.wait_ge(s_fw, 12 * 16)
            for part in pt:
                steps.done(pool.memset(part[:, :, N:W].bitcast(FP32), 0.0))
            steps.wait(pool)

        @block.scalar
        def _(act):
            def log(n):
                act.wait_ge(s_max, n + 1)
                act.activation(scratch[:], scratch[:], ACT.Ln).then_inc(s_ln, 1)

            act.wait_ge(s_pad, 3)
            for t in range(TILES):
                s = jobs.wait_filled(act, f"b{t}")
                act.activation(mask[:, t, 0:N].rearrange("p (a b) -> p a b", a=TILES), blocks(s, TILES, R),
                               ACT.Copy).then_inc(s_hn, 1)
                act.activation(bi[0][:, t, 0:N].rearrange("p (a b) -> p a b", a=TILES), blocks(s, TILES, R),
                               ACT.Copy).then_inc(s_hi, 1)
            for c in range(C):
                s = jobs.at[f"g{c}"][0]
                act_hi(act, jobs, f"g{c}", 0, halves(agg[0][:, c, :]), wide(s), s_hi)
                for n in MASKS_AFTER_G[c]:
                    log(n)
            for c in range(C):
                s = jobs.wait_filled(act, f"f{c}")
                if c >= 2:
                    act.wait_ge(s_fd, c - 1)
                act.activation(halves(rtmp[:, c % 2, :]), wide(s), ACT.Relu,
                               bias=b0c[:, c:c + 1]).then_inc(jobs.drained[s], 1)
                for n in MASKS_AFTER_F[c]:
                    log(n)
            act.wait_ge(s_ang, 1)
            act.activation(emb[:], phase[:], ACT.Sin).then_inc(s_sin, 1)
            s = jobs.wait_filled(act, "c1")
            act.activation(halves(pre[:]), wide(s, 0, COND), ACT.Identity, bias=f_b1[:, 0:1]).then_inc(jobs.drained[s], 1)
            jobs.wait_drained(act, "c1")
            act.activation(sig[:], pre[:], ACT.Exp, scale=-1.0).then_inc(s_ex, 1)
            for t in range(TILES + 1):
                if t < TILES:
                    act.wait_ge(s_rs, t + 1)
                    act.activation(res[:, t, :], x[:, t, :], ACT.Relu, bias=nmr[:, t:t + 1],
                                   scale=rstd[:, t:t + 1]).then_inc(s_hn, 1)
                if t > 0:
                    s = jobs.at[f"y{t - 1}"][0]
                    act_hi(act, jobs, f"y{t - 1}", 0, ht1[0][:, :, t_slice(t - 1)], blocks(s, C), s_hi)
            s = jobs.at["ga"][0]
            act_hi(act, jobs, "ga", 0, halves(gt[0][:]), wide(s), s_hi)
            s = jobs.wait_filled(act, "c2")
            act.activation(halves(cond[0:64, :]), wide(s, 0, 64), ACT.Copy).then_inc(s_c2, 1)
            act.activation(halves(cond_hi[64:128, :]), wide(s, 64, 128), ACT.Copy).then_inc(s_c2, 1)
            for t in range(TILES):
                act.wait_ge(s_rs, TILES + t + 1)
                act.activation(res[:, t, :], x[:, t, :], ACT.Relu, bias=nmr[:, t:t + 1],
                               scale=rstd[:, t:t + 1]).then_inc(s_hn, 1)

        @block.vector
        def _(dve):
            steps = Steps(s_vg)
            hi = 0

            def lo(name, out_ap, in_ap, hi_ap):
                nonlocal hi
                hi += 1
                dve.wait_ge(s_hi, hi)
                s = jobs.at[name][0]
                dve.tensor_tensor(out_ap, in_ap(s), hi_ap.bitcast(FP32), ALU.subtract).then_inc(jobs.drained[s], 1)

            def make_mask(n):
                counts, over, t = (mask, SCALE2, n) if n < TILES else (cnt, SCALE3, n - TILES)
                if n < TILES:
                    dve.wait_ge(s_hn, TILES)
                else:
                    dve.wait_ge(s_ai, TILES)
                diagonal = counts[:, t, t_slice(t)]
                steps.done(dve.tensor_tensor(diagonal, diagonal, ident[0:R, 0:R], ALU.subtract))
                steps.wait(dve)
                if n:
                    dve.wait_ge(s_m, n)
                dve.tensor_scalar(scratch[:], counts[:, t, :], 1.0, None, ALU.max).then_inc(s_max, 1)
                dve.wait_ge(s_max, n + 1)
                steps.done(dve.tensor_scalar(counts[:, t, :], counts[:, t, :], 0.0, NOEDGE, ALU.is_equal, ALU.mult))
                steps.wait(dve)
                dve.wait_ge(s_ln, n + 1)
                dve.scalar_tensor_tensor(out=counts[:, t, :], in0=scratch[:], scalar=over, in1=counts[:, t, :],
                                         op0=ALU.mult, op1=ALU.add).then_inc(s_m, 1)

            def embed_noise():
                dve.wait_ge(s_in, 48)
                dve.wait_ge(s_k, 4)
                steps.done(dve.tensor_scalar(phase[:], noise[:], freq[:, 0:1], None, ALU.mult))
                steps.wait(dve)
                steps.done(dve.tensor_scalar(turns[:], phase[:], float(1 / (2 * np.pi)), quarter[:, 0:1], ALU.mult,
                                             ALU.add))
                steps.wait(dve)
                steps.done(dve.scalar_tensor_tensor(out=angle[:], in0=turns[:], scalar=-TWO_PI_HIGH, in1=phase[:],
                                                    op0=ALU.mult, op1=ALU.add))
                steps.wait(dve)
                steps.done(dve.scalar_tensor_tensor(out=phase[:], in0=turns[:], scalar=-TWO_PI_LOW, in1=angle[:],
                                                    op0=ALU.mult, op1=ALU.add))
                steps.wait(dve)
                steps.done(dve.tensor_scalar(angle[:], phase[:], shift[:, 0:1], 3.14159, ALU.add, ALU.min))
                steps.wait(dve)
                dve.tensor_scalar(phase[:], angle[:], -3.14159, None, ALU.max).then_inc(s_ang, 1)

            def act_one():
                dve.wait_ge(s_ex, 1)
                steps.done(dve.tensor_scalar(sig[:], sig[:], 1.0, None, ALU.add))
                steps.wait(dve)
                steps.done(dve.reciprocal(sig[:], sig[:]))
                steps.wait(dve)
                dve.tensor_tensor(act1[0:COND, :], pre[:], sig[:], ALU.mult).then_inc(s_a1, 1)

            dve.wait_ge(s_pad, 3)
            for t in range(TILES):
                five = lambda ap: ap[:, t, 0:N].rearrange("p (a b) -> p a b", a=TILES)
                lo(f"b{t}", five(bi[1]), lambda s: blocks(s, TILES, R), five(bi[0]))
            for c in range(C):
                lo(f"g{c}", halves(agg[1][:, c, :]), wide, halves(agg[0][:, c, :]))
                for n in MASKS_AFTER_G[c]:
                    make_mask(n)
            for c in range(C):
                jobs.wait_drained(dve, f"f{c}")
                steps.done(dve.tensor_copy(ft[0][:, c, :], rtmp[:, c % 2, :]))
                steps.wait(dve)
                dve.tensor_tensor(ft[1][:, c, :], rtmp[:, c % 2, :], ft[0][:, c, :].bitcast(FP32),
                                  ALU.subtract).then_inc(s_fd, 1)
                for n in MASKS_AFTER_F[c]:
                    make_mask(n)
            embed_noise()
            dve.wait_ge(s_xb, TILES)

            def residual(name, t):
                s = jobs.wait_filled(dve, name)
                dve.tensor_tensor(x[:, t, :], ps[s][0:R, 0:D], x[:, t, :], ALU.add).then_inc(jobs.drained[s], 1)

            def lo_y(t):
                lo(f"y{t}", ht1[1][:, :, t_slice(t)], lambda s: blocks(s, C), ht1[0][:, :, t_slice(t)])

            for t in range(TILES):
                residual(f"o{t}", t)
                jobs.wait_drained(dve, f"o{t}")
                dve_stats(dve, steps, t, x[:, t, :], s_st)
                if t > 2:
                    lo_y(t - 3)
            for t in range(2, TILES):
                lo_y(t)
            s = jobs.wait_filled(dve, "r")
            dve.wait_ge(s_r1, 16)
            dve.wait_ge(s_pad, 6)
            dve.tensor_tensor(r_sum[:], ps[s][0:R, 0:TILES * HID].rearrange("p (a b) -> p a b", a=TILES),
                              b1row[:].rearrange("p (a b) -> p a b", a=1).to_broadcast([R, TILES, HID]),
                              ALU.add).then_inc(jobs.drained[s], 1)
            jobs.wait_drained(dve, "r")
            steps.done(dve.tensor_scalar(r_act[:], r_sum[:], 0.0, None, ALU.max))
            steps.wait(dve)
            steps.done(dve.tensor_copy(r_nat[0][:, :, 0:HID], r_act[:]))
            steps.wait(dve)
            dve.tensor_tensor(r_nat[1][:, :, 0:HID], r_act[:], r_nat[0][:, :, 0:HID].bitcast(FP32),
                              ALU.subtract).then_inc(s_r, 1)
            act_one()
            lo("ga", halves(gt[1][:]), wide, halves(gt[0][:]))
            for t in range(TILES):
                residual(f"p{t}", t)
                jobs.wait_drained(dve, f"p{t}")
                dve_stats(dve, steps, t, x[:, t, :], s_st)
                if t == 1:
                    dve.wait_ge(s_c2, 2)
                    s = jobs.at["c2"][0]
                    dve.tensor_tensor(halves(cond[64:128, :]), wide(s, 64, 128), halves(cond_hi[64:128, :].bitcast(FP32)),
                                      ALU.subtract).then_inc(jobs.drained[s], 1)

        @block.tensor
        def _(pe):
            for t in range(TILES):
                pe_transposes(pe, jobs, f"b{t}", 0, lambda b: cnt[:, b, t_slice(t)], TILES, R, R)
            for c in range(C):
                pe_wide(pe, jobs, f"g{c}", 0, lambda i, kk: h_pair[i][:, kk, c * 128:(c + 1) * 128],
                        lambda j, kk: bi[j][:, kk, :], TILES,
                        ready=None if c else lambda kk: jobs.wait_drained(pe, f"b{kk}"))
            lhs, rhs = proj(w[0], agg)
            for c in range(C):
                pe_wide(pe, jobs, f"f{c}", 0, lhs(c), rhs, C,
                        ready=None if c else lambda kk: jobs.wait_drained(pe, f"g{kk}"))
            def condition(name):
                s = jobs.acquire(pe, name)
                for half in range(2):
                    cols = slice(half * H2, half * H2 + H2)
                    if name == "c1":
                        ins = pe.matmul(ps[s][0:COND, 512 * half:512 * half + H2], f_w1[:], emb[:, cols], start=True,
                                        stop=True)
                    else:
                        ins = pe.matmul(ps[s][:, 512 * half:512 * half + H2], f_w2[:], act1[0:COND + 1, cols],
                                        start=True, stop=True)
                ins.then_inc(jobs.filled[s], 1)

            def r_tile(t):
                jobs.wait_drained(pe, f"y{t}")
                return matmul3(pe, ps[r_slot][0:R, t * HID:(t + 1) * HID], lambda i, kk: ht1[i][:, kk, t_slice(t)],
                               lambda j, kk: w_l1[1 + j][:, kk * HID:(kk + 1) * HID], C)

            for name in tail[:-2]:
                t = int(name[1]) if name != "r" else 0
                if name[0] == "o":
                    pe_natural(pe, jobs, name, 0, lambda i, kk: ft[i][:, kk, t_slice(t)],
                               lambda j, kk: w[1][j][:, kk, :], C,
                               None if t else lambda kk: pe.wait_ge(s_fd, kk + 1))
                elif name[0] == "y":
                    pe.wait_ge(s_hn, TILES + t + 1)
                    pe_transposes(pe, jobs, name, 0, lambda b: res[:, t, b * 128:(b + 1) * 128], C, R, 128)
                    if t >= 2:
                        r_tile(t - 1)
                elif name == "r":
                    pe.wait_ge(s_w2, 1)
                    r_slot = jobs.acquire(pe, "r")
                    r_tile(0)
                else:
                    pe.wait_ge(s_sin, 1)
                    condition(name)
            r_tile(TILES - 1).then_inc(jobs.filled[r_slot], 1)
            pe.wait_ge(s_r, 1)
            pe.wait_ge(s_ai, TILES)
            pe_wide(pe, jobs, "ga", 0, lambda i, kk: r_nat[i][:, kk, :], ai, TILES)
            pe.wait_ge(s_a1, 1)
            pe.wait_ge(s_fw, 12 * 16)
            condition("c2")
            jobs.wait_drained(pe, "ga")
            for t in range(TILES):
                pe_natural(pe, jobs, f"p{t}", 0, lambda i, kk: gt[i][:, t_slice(t)],
                           lambda j, kk: w_l1[1 + j][:, W2COL:W2COL + D], 1)

    names = ["n1_0", "n1_1", "a1_0", "n1_2", "a1_1", "v0", "n1_3", "a1_2", "v1", "n1_4", "a1_3", "v2", "a1_4", "v3", "v4"]
    names += ["q0", "k0"]
    attn = attention_jobs(HEADS2, lambda h: [f"q{h + 1}"] if h + 1 < HEADS2 else [],
                          lambda h: ["q1", "k1"] if h == 0 else [f"k{h + 1}"] if h + 1 < HEADS2 else [])
    names += attn
    ln2 = ["o0", "o1", "n2_0", "o2", "a2_0", "n2_1", "o3", "a2_1", "n2_2", "o4", "a2_2", "n2_3", "n2_4"]
    names += ln2 + ["f0", "f1", "a2_3", "a2_4", "f2", "f3"] + [f"p{t}" for t in range(TILES)]
    before_p = [n for n in names if n[0] != "f" and n not in {f"p{t}" for t in range(TILES)}]
    jobs = Jobs(ring, names, BLOCKS)
    UNITS = HEADS2 * TILES
    bias_order = [t for c in range(C) for t in range(c, TILES, C)]
    xe = sb("xe", "qk", [R, TILES, D])
    s_xin, s_sp, s_h = sem("m_x_added"), sem("sum_spilled"), sem("h_copied")
    s_x, s_mask = sem("x_loaded_again"), sem("mask_loaded")
    s_wl3 = [sem(f"l3_w{n}_loaded") for n in range(3)]
    s_wsp3 = [sem(f"l3_w{n}_split") for n in range(3)]
    hi_index = {n: i for i, n in enumerate(n for n in names if n[0] in "aqkt" or n[:2] == "pv")}
    s_hi, s_st, s_rs, s_hn = sem("m_hi"), sem("m_stats"), sem("m_rstd"), sem("m_norm")
    s_ex, s_ri, s_sc = sem("m_exp"), sem("m_inverse"), sem("m_scaled")
    s_vh, s_vd, s_fd, s_xb = sem("m_v_hi"), sem("m_v_split"), sem("m_f_split"), sem("m_bias_added")
    s_pm, s_vm, s_xb2, s_w2h = sem("m_pool_steps"), sem("m_dve_steps"), sem("m_bias2_added"), sem("m_w2_hi")
    POOL_STEPS, DVE_STEPS = 2 * 2 * TILES + 6 + 5 * C, 2 * (2 * TILES) + UNITS + C

    def body(eng, run, last_differs):
        n = BLOCKS - 1 if last_differs else BLOCKS
        with eng.Fori(0, n) as it:
            run(it, True)
        if last_differs:
            run(BLOCKS - 1, False)

    with nc.Block() as block:
        @block.sync
        def _(sp):
            for n, name in enumerate(("L2_gnn_bv", "L2_gnn_bo", "L2_gnn_m_b2")):
                load_row(sp, n, name, 0)

            def run(it, more):
                jobs.wait_filled(sp, f"v{TILES - 1}", it)
                load_w(sp, 0, "L2_gnn_wo", it, s_wl2)
                if more:
                    jobs.wait_drained(sp, f"v{TILES - 1}", it)
                    load_row(sp, 0, "L2_gnn_bv", it + 1)
                sp.wait_ge(s_wss, it * 4 + 2)
                load_ws(sp, 2, it)
                if more:
                    sp.wait_ge(s_xb, it * TILES + TILES)
                    load_row(sp, 1, "L2_gnn_bo", it + 1)
                jobs.wait_filled(sp, f"q{HEADS2 - 1}", it)
                load_w(sp, 1, "L2_gnn_m_w1", it, s_wl2)
                jobs.wait_filled(sp, f"k{HEADS2 - 1}", it)
                load_w(sp, 2, "L2_gnn_m_w2", it, s_wl2)
                if more:
                    jobs.wait_filled(sp, f"o{TILES - 1}", it)
                    load_w(sp, 0, "L2_gnn_wv", it + 1, s_wl2)
                    sp.wait_ge(s_wss, it * 4 + 4)
                    load_ws(sp, 1, it + 1)
                    jobs.wait_filled(sp, f"f{C - 1}", it)
                    load_w(sp, 1, "L2_gnn_wq", it + 1, s_wl2)
                    sp.wait_ge(s_xb2, it * TILES + TILES)
                    load_row(sp, 2, "L2_gnn_m_b2", it + 1)
                    jobs.wait_filled(sp, f"p{TILES - 1}", it)
                    load_w(sp, 2, "L2_gnn_wk", it + 1, s_wl2)
                else:
                    jobs.wait_drained(sp, f"s{HEADS2 - 1}_{TILES - 1}", it)
                    sp.dma_start(xe[:], x_spill).then_inc(s_x, 16)
                    sp.dma_start(mask[:], mask_spill).then_inc(s_mask, 16)
                    jobs.wait_filled(sp, f"o{TILES - 1}", it)
                    load_w(sp, 0, "L3_gnn_Wv", 0, s_wl3)
                    jobs.wait_filled(sp, f"f{C - 1}", it)
                    load_w(sp, 1, "L3_gnn_Wq", 0, s_wl3)
            body(sp, run, True)
            for t in range(TILES):
                jobs.wait_drained(sp, f"p{t}", BLOCKS - 1)
                sp.dma_start(x_spill[:, t, :], res[:, t, :]).then_inc(s_sp, 16)

        @block.gpsimd
        def _(pool):
            steps = Steps(s_pm, POOL_STEPS)

            def run(it, more):
                steps.body(it)

                def add_row(n, t):
                    pool.wait_ge(s_hn, it * 2 * TILES + TILES)
                    pool.wait_ge(s_rows[n], it * 16 + 16)
                    pool.tensor_tensor(res[:, t, :], res[:, t, :], rows[n][:], ALU.add).then_inc(s_xb, 1)

                def weights(n, loads, pieces=range(C)):
                    pool.wait_ge(s_wl2[n], it * 32 + 16 * loads)
                    split_weights(pool, steps, n, s_wsp[n], pieces)

                for t in range(TILES):
                    pool.wait_ge(s_st, it * 2 * TILES + t + 1)
                    pool_rstd(pool, steps, t, s_rs)
                weights(1, 1)
                weights(2, 1)
                for u in range(UNITS):
                    pool_scale(pool, u, it, UNITS, s_ri, s_sc)
                    if u < TILES:
                        add_row(1, u)
                    if u == 6:
                        jobs.wait_filled(pool, f"n1_{TILES - 1}", it)
                        pool.wait_ge(s_wsl, (it * 2 + 2) * WS_DMAS * 16)
                        split_ws(pool, steps)
                    if 8 <= u < 8 + C:
                        weights(0, 2, [u - 8])
                    if UNITS - C <= u:
                        weights(1, 2, [u - (UNITS - C)])
                for t in range(TILES):
                    pool.wait_ge(s_st, it * 2 * TILES + TILES + t + 1)
                    pool_rstd(pool, steps, t, s_rs)
                if more:
                    jobs.wait_filled(pool, f"n2_{TILES - 1}", it)
                    pool.wait_ge(s_wsl, (it * 2 + 3) * WS_DMAS * 16)
                    split_ws(pool, steps)
                    weights(0, 3)
                    steps.end()
                    pool.sem_inc(s_xin, TILES)
                else:
                    pool.wait_ge(s_x, 16)
                    pool.wait_ge(s_wl3[0], 16)
                    for n, t in enumerate(bias_order):
                        pool.wait_ge(s_xb2, it * TILES + n + 1)
                        pool.tensor_tensor(res[:, t, :], res[:, t, :], xe[:, t, :], ALU.add).then_inc(s_xin, 1)
                        if n > 0:
                            split_weights(pool, steps, 0, s_wsp3[0], [n - 1])
                    for t in range(TILES):
                        pool.wait_ge(s_st, BLOCKS * 2 * TILES + t + 1)
                        pool_rstd(pool, steps, t, s_rs)
            body(pool, run, True)

        def modulate(dve, steps, it, name, t, norm_index):
            s = jobs.wait_filled(dve, name, it)
            dve.wait_ge(s_hn, it * 2 * TILES + norm_index * TILES + t + 1)
            if t > 0:
                jobs.wait_drained(dve, f"{name[:3]}{t - 1}", it)
            steps.done(dve.tensor_tensor(y1[:], xn[:, t % 2, :], ps[s][0:R, 0:D], ALU.mult))
            steps.wait(dve)
            dve.tensor_tensor(y2[:, t % 2, :], y1[:], ps[s][0:R, D:2 * D], ALU.add).then_inc(jobs.drained[s], 1)

        @block.vector
        def _(dve):
            first = Steps(sem("m_dve_first"))
            for t in range(TILES):
                dve_stats(dve, first, t, res[:, t, :], s_st)
            steps = Steps(s_vm, DVE_STEPS)

            def run(it, more):
                steps.body(it)

                def wait_hi(name):
                    dve.wait_ge(s_hi, it * len(hi_index) + hi_index[name] + 1)
                    return jobs.at[name][0]

                def prob_lo(name):
                    if name:
                        t = int(name[3])
                        s = wait_hi(name)
                        dve.tensor_tensor(pt_view(1, t), blocks(s, TILES, R), pt_view(0, t).bitcast(FP32),
                                          ALU.subtract).then_inc(jobs.drained[s], 1)

                held = None
                for name in before_p:
                    kind = name[0]
                    if kind != "s":
                        held = prob_lo(held)
                    if kind == "n":
                        modulate(dve, steps, it, name, int(name[3]), int(name[1]) - 1)
                    elif kind == "a":
                        t = int(name[3])
                        s = wait_hi(name)
                        dve.tensor_tensor(yt[1][:, :, t_slice(t)], blocks(s, C), yt[0][:, :, t_slice(t)].bitcast(FP32),
                                          ALU.subtract).then_inc(jobs.drained[s], 1)
                    elif kind == "v":
                        t = int(name[1])
                        s = jobs.wait_filled(dve, name, it)
                        dve.wait_ge(s_rows[0], it * 16 + 16)
                        if t >= 2:
                            dve.wait_ge(s_vd, it * TILES + t - 1)
                        dve.tensor_tensor(vtmp[:, t % 2, :], ps[s][0:R, 0:D], rows[0][:], ALU.add).then_inc(jobs.drained[s], 1)
                        if t > 0:
                            v_lo(dve, it, t - 1)
                        if t == TILES - 1:
                            v_lo(dve, it, t)
                    elif kind in "qk":
                        h = int(name[1])
                        s = wait_hi(name)
                        buf, bias = (q, bq2) if kind == "q" else (k, bk2)
                        dve.scalar_tensor_tensor(out=halves(buf[h % 2][1][:]), in0=wide(s),
                                                 scalar=bias[:, bass.ds(it * C + h, 1)],
                                                 in1=halves(buf[h % 2][0][:]).bitcast(FP32), op0=ALU.add,
                                                 op1=ALU.subtract).then_inc(jobs.drained[s], 1)
                    elif kind == "s":
                        u = int(name[1]) * TILES + int(name[3])
                        dve_scores(dve, jobs, u, it, 1 / SCALE2)
                        if u > 0:
                            dve_inverse(dve, steps, u - 1, it, UNITS, s_ex, s_ri)
                        held = prob_lo(held)
                        if u == UNITS - 1:
                            dve_inverse(dve, steps, u, it, UNITS, s_ex, s_ri)
                    elif kind == "t":
                        held = name
                    elif kind == "p":
                        h = int(name[2])
                        s = wait_hi(name)
                        dve.tensor_tensor(halves(ot[1][:, h, :]), wide(s), halves(ot[0][:, h, :]).bitcast(FP32),
                                          ALU.subtract).then_inc(jobs.drained[s], 1)
                    elif kind == "o":
                        t = int(name[1])
                        dve.wait_ge(s_xb, it * TILES + t + 1)
                        residual(dve, steps, it, name, t)
                for c in range(C):
                    dve.wait_ge(s_w2h, it * C + c + 1)
                    dve.tensor_tensor(w[2][1][:, c, :], w_raw[2][:, c, :], w[2][0][:, c, :].bitcast(FP32),
                                      ALU.subtract).then_inc(s_wsp[2], 1)
                    for t in range(c, TILES, C):
                        dve.wait_ge(s_hn, it * 2 * TILES + 2 * TILES)
                        dve.wait_ge(s_rows[2], it * 16 + 16)
                        dve.tensor_tensor(res[:, t, :], res[:, t, :], rows[2][:], ALU.add).then_inc(s_xb2, 1)
                    jobs.wait_drained(dve, f"f{c}", it)
                    steps.done(dve.tensor_copy(ht[0][:, c, :], ftmp[:, c % 2, :]))
                    steps.wait(dve)
                    dve.tensor_tensor(ht[1][:, c, :], ftmp[:, c % 2, :], ht[0][:, c, :].bitcast(FP32),
                                      ALU.subtract).then_inc(s_fd, 1)
                for t in range(TILES):
                    dve.wait_ge(s_xb2, it * TILES + TILES)
                    dve.wait_ge(s_xin, it * TILES + TILES)
                    residual(dve, steps, it, f"p{t}", t)
                steps.end()

            def v_lo(dve, it, t):
                dve.wait_ge(s_vh, it * TILES + t + 1)
                dve.tensor_tensor(v[1][:, t, :], vtmp[:, t % 2, :], v[0][:, t, :].bitcast(FP32),
                                  ALU.subtract).then_inc(s_vd, 1)

            def residual(dve, steps, it, name, t):
                s = jobs.wait_filled(dve, name, it)
                dve.tensor_tensor(res[:, t, :], ps[s][0:R, 0:D], res[:, t, :], ALU.add).then_inc(jobs.drained[s], 1)
                jobs.wait_drained(dve, name, it)
                dve_stats(dve, steps, t, res[:, t, :], s_st)
            body(dve, run, False)

        @block.scalar
        def _(act):
            def run(it, more):
                for name in before_p:
                    kind = name[0]
                    s = jobs.at[name][0]
                    if kind == "n":
                        t, first = int(name[3]), name[1] == "1"
                        index = 0 if first else TILES
                        act.wait_ge(s_rs, it * 2 * TILES + index + t + 1)
                        if t >= 2:
                            jobs.wait_drained(act, f"{name[:3]}{t - 2}", it)
                        act.activation(xn[:, t % 2, :], res[:, t, :], ACT.Identity, bias=nmr[:, t:t + 1],
                                       scale=rstd[:, t:t + 1]).then_inc(s_hn, 1)
                    elif kind == "a":
                        act_hi(act, jobs, name, it, yt[0][:, :, t_slice(int(name[3]))], blocks(s, C), s_hi)
                    elif kind == "v":
                        t = int(name[1])
                        jobs.wait_drained(act, name, it)
                        act.wait_ge(s_xs, TILES * 16)
                        act.activation(v[0][:, t, :], vtmp[:, t % 2, :], ACT.Copy).then_inc(s_vh, 1)
                    elif kind in "qk":
                        h = int(name[1])
                        buf, bias = (q, bq2) if kind == "q" else (k, bk2)
                        act_hi(act, jobs, name, it, halves(buf[h % 2][0][:]), wide(s), s_hi, bias[:, bass.ds(it * C + h, 1)])
                    elif kind == "s":
                        act_exp(act, jobs, int(name[1]) * TILES + int(name[3]), it, s_ex)
                    elif kind == "t":
                        act_hi(act, jobs, name, it, pt_view(0, int(name[3])), blocks(s, TILES, R), s_hi)
                    elif kind == "p":
                        act_hi(act, jobs, name, it, halves(ot[0][:, int(name[2]), :]), wide(s), s_hi)
                for c in range(C):
                    act.wait_ge(s_wl2[2], it * 32 + 32)
                    act.activation(w[2][0][:, c, :], w_raw[2][:, c, :], ACT.Copy).then_inc(s_w2h, 1)
                    s = jobs.wait_filled(act, f"f{c}", it)
                    if c >= 2:
                        act.wait_ge(s_fd, it * C + c - 1)
                    act.activation(halves(ftmp[:, c % 2, :]), wide(s), ACT.Relu,
                                   bias=bm2[:, bass.ds(it * C + c, 1)]).then_inc(jobs.drained[s], 1)
            body(act, run, False)
            for t in range(TILES):
                act.wait_ge(s_rs, BLOCKS * 2 * TILES + t + 1)
                act.activation(xe[:, t, :], res[:, t, :], ACT.Relu, bias=nmr[:, t:t + 1],
                               scale=rstd[:, t:t + 1]).then_inc(s_hn, 1)

        @block.tensor
        def _(pe):
            def weights_ready(n, it, which):
                pe.wait_ge(s_wsp[n], it * 2 * C + which * C)

            def run(it, more):
                lhs_q, rhs_y = proj(w[1], yt)
                lhs_k, _ = proj(w[2], yt)
                for name in names:
                    kind = name[0]
                    if kind == "n":
                        t = int(name[3])
                        pe.wait_ge(s_wss, it * 4 + 2 * int(name[1]))
                        s = jobs.acquire(pe, name, it)
                        for n in range(2):
                            ins = pe.matmul(ps[s][0:R, D * n:D * n + D], cond[:, t_slice(t)], ws[:, n, :], start=True,
                                            stop=True)
                        ins.then_inc(jobs.filled[s], 1)
                    elif kind == "a":
                        t = int(name[3])
                        jobs.wait_drained(pe, f"n{name[1:]}", it)
                        pe_transposes(pe, jobs, name, it, lambda b: y2[:, t % 2, b * 128:(b + 1) * 128], C, R, 128)
                    elif kind == "v":
                        t = int(name[1])
                        if t == 0:
                            weights_ready(0, it, 1)
                        jobs.wait_drained(pe, f"a1_{t}", it)
                        pe_natural(pe, jobs, name, it, lambda i, kk: yt[i][:, kk, t_slice(t)],
                                   lambda j, kk: w[0][j][:, kk, :], C)
                    elif kind in "qk":
                        h = int(name[1])
                        if h == 0:
                            weights_ready(1 if kind == "q" else 2, it, 1)
                        pe_wide(pe, jobs, name, it, (lhs_q if kind == "q" else lhs_k)(h), rhs_y, C)
                    elif kind == "s":
                        h, t = int(name[1]), int(name[3])
                        if t == 0:
                            jobs.wait_drained(pe, f"q{h}", it)
                            jobs.wait_drained(pe, f"k{h}", it)
                        pe_scores(pe, jobs, h, t, it, q[h % 2], k[h % 2], 0, 128)
                    elif kind == "t":
                        pe_prob_transposes(pe, jobs, int(name[1]) * TILES + int(name[3]), it, UNITS, s_sc)
                    elif name[:2] == "pv":
                        h = int(name[2])
                        if h == 0:
                            pe.wait_ge(s_vd, it * TILES + TILES)
                        pe_values(pe, jobs, h, h, it)
                    elif kind == "o":
                        t = int(name[1])
                        if t == 0:
                            weights_ready(0, it, 2)
                        pe_natural(pe, jobs, name, it, lambda i, kk: ot[i][:, kk, t_slice(t)],
                                   lambda j, kk: w[0][j][:, kk, :], C,
                                   None if t else lambda kk: jobs.wait_drained(pe, f"pv{kk}", it))
                    elif kind == "f":
                        c = int(name[1])
                        if c == 0:
                            jobs.wait_drained(pe, "a2_2", it)
                            weights_ready(1, it, 2)
                        if c == 2:
                            jobs.wait_drained(pe, f"a2_{TILES - 1}", it)
                            for early in range(2):
                                pe_wide(pe, jobs, f"f{early}", it, lhs_q(early), rhs_y, C, parts=(1,))
                        pe_wide(pe, jobs, name, it, lhs_q(c), rhs_y, C, parts=(0,) if c < 2 else (0, 1))
                    else:
                        t = int(name[1])
                        if t == 0:
                            weights_ready(2, it, 2)
                        pe_natural(pe, jobs, name, it, lambda i, kk: ht[i][:, kk, t_slice(t)],
                                   lambda j, kk: w[2][j][:, kk, :], C,
                                   None if t else lambda kk: pe.wait_ge(s_fd, it * C + kk + 1))
            body(pe, run, False)

    enc = sb("enc", "ot", [128, C, W])
    acc = sb("acc", "ot", [128, C, W], FP32, C * W * 4)

    jobs = Jobs(ring, [f"a{t}" for t in range(TILES)])
    s_hi, s_enc, s_pad = sem("e_hi"), sem("e_enc"), sem("e_pads")
    s_row3 = [sem(f"l3_row{n}_loaded") for n in range(3)]

    def load_row3(sp, n, src):
        sp.dma_start(rows[n][:], src).then_inc(s_row3[n], 16)

    with nc.Block() as block:
        @block.sync
        def _(sp):
            load_w(sp, 2, "L3_gnn_Wk", 0, s_wl3)
            load_row3(sp, 0, block_of("L3_gnn_bv", 0).to_broadcast([R, D]))
            sp.wait_ge(s_sp, 16 * TILES)
            sp.dma_start(res[:], xe[:]).then_inc(s_h, 16)

        @block.gpsimd
        def _(pool):
            pool.memset(enc[:, :, N:W], 0.0).then_inc(s_pad, 1)

        @block.vector
        def _(dve):
            for t in range(TILES):
                dve.wait_ge(s_hi, t + 1)
                s = jobs.at[f"a{t}"][0]
                dve.tensor_tensor(yt[1][:, :, t_slice(t)], blocks(s, C), yt[0][:, :, t_slice(t)].bitcast(FP32),
                                  ALU.subtract).then_inc(jobs.drained[s], 1)

        @block.scalar
        def _(act):
            for t in range(TILES):
                s = jobs.wait_filled(act, f"a{t}")
                act.activation(enc[:, :, t_slice(t)], blocks(s, C), ACT.Copy).then_inc(s_enc, 1)
                act.activation(yt[0][:, :, t_slice(t)], blocks(s, C), ACT.Copy).then_inc(s_hi, 1)

        @block.tensor
        def _(pe):
            for t in range(TILES):
                pe_transposes(pe, jobs, f"a{t}", 0, lambda b: xe[:, t, b * 128:(b + 1) * 128], C, R, 128)

    def spot1(h):
        return [f"k{h // 2 + 1}"] if h % 2 and h // 2 + 1 < C else ["w3"] if h == 6 else []

    def spot2(h):
        return ([f"q{h // 2 + 1}"] if h // 2 + 1 < C else []) if h % 2 == 0 else [f"w{h // 2}"] if h < 6 else []

    names = [f"v{t}" for t in range(TILES)] + ["q0", "k0"] + attention_jobs(HEADS3, spot1, spot2)
    jobs = Jobs(ring, names, LAYERS)
    UNITS3 = HEADS3 * TILES
    hi_index3 = {n: i for i, n in enumerate(n for n in names if n[0] in "qkt")}
    into_acc = {c: [n for n in names if n in (f"w{c}", f"pv{2 * c}", f"pv{2 * c + 1}")] for c in range(C)}
    s_hi, s_ex, s_ri, s_sc = sem("t_hi"), sem("t_exp"), sem("t_inverse"), sem("t_scaled")
    s_vh, s_vd, s_acc, s_xh, s_xt = sem("t_v_hi"), sem("t_v_split"), sem("t_acc_set"), sem("t_x_hi"), sem("t_x_split")
    s_pt, s_vt = sem("t_pool_steps"), sem("t_dve_steps")

    def layers(eng, run):
        with eng.Fori(0, LAYERS - 1) as it:
            run(it, True)
        run(LAYERS - 1, False)

    def layers_alike(eng, run):
        with eng.Fori(0, LAYERS) as it:
            run(it)

    def load_half(sp, n, src):
        sp.dma_start(w_raw[n][:], src.rearrange("(c p) n -> p c n", p=128)).then_inc(s_wl3[n], 16)

    with nc.Block() as block:
        @block.sync
        def _(sp):
            def run(it, more):
                jobs.wait_filled(sp, f"v{TILES - 1}", it)
                load_w(sp, 0, "L3_gnn_Ws", it, s_wl3)
                if more:
                    jobs.wait_drained(sp, f"v{TILES - 1}", it)
                    load_row3(sp, 0, block_of("L3_gnn_bv", it + 1).to_broadcast([R, D]))
                jobs.wait_filled(sp, f"q{C - 1}", it)
                if more:
                    load_w(sp, 1, "L3_gnn_Wq", it + 1, s_wl3)
                else:
                    load_half(sp, 1, a["L3_gnn_W1"][:, 0:D])
                jobs.wait_filled(sp, f"k{C - 1}", it)
                if more:
                    load_w(sp, 2, "L3_gnn_Wk", it + 1, s_wl3)
                else:
                    load_half(sp, 2, a["L3_gnn_W1"][:, D:2 * D])
                jobs.wait_filled(sp, f"w{C - 1}", it)
                if more:
                    load_w(sp, 0, "L3_gnn_Wv", it + 1, s_wl3)
                else:
                    load_half(sp, 0, a["L3_gnn_W2"][0:D, :])
            layers(sp, run)

        @block.gpsimd
        def _(pool):
            per = 2 * C + C + C
            steps = Steps(s_pt, per)
            first = Steps(sem("t_pool_first"))
            for n in (1, 2):
                pool.wait_ge(s_wl3[n], 16)
                split_weights(pool, first, n, s_wsp3[n])

            def run(it, more):
                steps.body(it)
                for u in range(UNITS3):
                    pool_scale(pool, u, it, UNITS3, s_ri, s_sc)
                    for n, from_unit, loads, per_layer in ((0, 3, 2, 2), (1, 28, 2, 1), (2, 32, 2, 1)):
                        if from_unit <= u < from_unit + C:
                            pool.wait_ge(s_wl3[n], it * 16 * per_layer + 16 * loads)
                            split_weights(pool, steps, n, s_wsp3[n], [u - from_unit])
                pool.wait_ge(s_wl3[0], it * 32 + 48)
                split_weights(pool, steps, 0, s_wsp3[0])
                steps.end()
            layers_alike(pool, lambda it: run(it, True))

        @block.vector
        def _(dve):
            steps = Steps(s_vt, UNITS3)
            dve.sem_inc(s_xt, 1)

            def run(it):
                steps.body(it)

                def wait_hi(name):
                    dve.wait_ge(s_hi, it * len(hi_index3) + hi_index3[name] + 1)
                    return jobs.at[name][0]

                def v_lo(t):
                    dve.wait_ge(s_vh, it * TILES + t + 1)
                    dve.tensor_tensor(v[1][:, t, :], xn[:, t % 2, :], v[0][:, t, :].bitcast(FP32),
                                      ALU.subtract).then_inc(s_vd, 1)

                def prob_lo(name):
                    if name:
                        t = int(name[3])
                        s = wait_hi(name)
                        dve.tensor_tensor(pt_view(1, t), blocks(s, TILES, R), pt_view(0, t).bitcast(FP32),
                                          ALU.subtract).then_inc(jobs.drained[s], 1)

                held = None
                for name in names:
                    kind = name[0]
                    if kind != "s":
                        held = prob_lo(held)
                    if kind == "v":
                        t = int(name[1])
                        s = jobs.wait_filled(dve, name, it)
                        dve.wait_ge(s_row3[0], it * 16 + 16)
                        if t >= 2:
                            dve.wait_ge(s_vd, it * TILES + t - 1)
                        dve.tensor_tensor(xn[:, t % 2, :], ps[s][0:R, 0:D], rows[0][:], ALU.add).then_inc(jobs.drained[s], 1)
                        if t > 0:
                            v_lo(t - 1)
                        if t == TILES - 1:
                            v_lo(t)
                    elif kind in "qk":
                        c = int(name[1])
                        s = wait_hi(name)
                        buf, bias = (q, bq3) if kind == "q" else (k, bk3)
                        dve.scalar_tensor_tensor(out=halves(buf[c % 2][1][:]), in0=wide(s),
                                                 scalar=bias[:, bass.ds(it * C + c, 1)],
                                                 in1=halves(buf[c % 2][0][:]).bitcast(FP32), op0=ALU.add,
                                                 op1=ALU.subtract).then_inc(jobs.drained[s], 1)
                    elif kind == "s":
                        u = int(name[1]) * TILES + int(name[3])
                        if u == 0:
                            dve.wait_ge(s_mask, 16)
                        dve_scores(dve, jobs, u, it, 1 / SCALE3)
                        if u > 0:
                            dve_inverse(dve, steps, u - 1, it, UNITS3, s_ex, s_ri)
                        held = prob_lo(held)
                        if u == UNITS3 - 1:
                            dve_inverse(dve, steps, u, it, UNITS3, s_ex, s_ri)
                    elif kind == "t":
                        held = name
                    else:
                        c = int(name[1]) if kind == "w" else int(name[2]) // 2
                        p0, p1 = (0, 128) if kind == "w" else (64 * (int(name[2]) % 2), 64 * (int(name[2]) % 2) + 64)
                        s = jobs.wait_filled(dve, name, it)
                        dve.wait_ge(s_acc, it * C + c + 1)
                        before = into_acc[c][:into_acc[c].index(name)]
                        if before:
                            jobs.wait_drained(dve, before[-1], it)
                        if kind == "w":
                            dve.scalar_tensor_tensor(out=halves(acc[:, c, :]), in0=wide(s),
                                                     scalar=bs3[:, bass.ds(it * C + c, 1)], in1=halves(acc[:, c, :]),
                                                     op0=ALU.add, op1=ALU.add).then_inc(jobs.drained[s], 1)
                        else:
                            dve.tensor_tensor(halves(acc[p0:p1, c, :]), wide(s, p0, p1), halves(acc[p0:p1, c, :]),
                                              ALU.add).then_inc(jobs.drained[s], 1)
                for c in range(C):
                    dve.wait_ge(s_xh, it * C + c + 1)
                    dve.tensor_tensor(yt[1][:, c, :], acc[:, c, :], yt[0][:, c, :].bitcast(FP32),
                                      ALU.subtract).then_inc(s_xt, 1)
                steps.end()
            layers_alike(dve, run)

        @block.scalar
        def _(act):
            def run(it):
                act.wait_ge(s_xt, it * C + 1)
                for c in range(C):
                    act.activation(acc[:, c, :], enc[:, c, :], ACT.Copy).then_inc(s_acc, 1)
                for name in names:
                    kind = name[0]
                    s = jobs.at[name][0]
                    if kind == "v":
                        t = int(name[1])
                        jobs.wait_drained(act, name, it)
                        act.activation(v[0][:, t, :], xn[:, t % 2, :], ACT.Copy).then_inc(s_vh, 1)
                    elif kind in "qk":
                        c = int(name[1])
                        buf, bias = (q, bq3) if kind == "q" else (k, bk3)
                        if name == "q0":
                            act.wait_ge(s_h, 16)
                        act_hi(act, jobs, name, it, halves(buf[c % 2][0][:]), wide(s), s_hi, bias[:, bass.ds(it * C + c, 1)])
                    elif kind == "s":
                        act_exp(act, jobs, int(name[1]) * TILES + int(name[3]), it, s_ex)
                    elif kind == "t":
                        act_hi(act, jobs, name, it, pt_view(0, int(name[3])), blocks(s, TILES, R), s_hi)
                for c in range(C):
                    jobs.wait_drained(act, into_acc[c][-1], it)
                    if c == 0:
                        jobs.wait_filled(act, f"w{C - 1}", it)
                    act.activation(yt[0][:, c, :], acc[:, c, :], ACT.Copy).then_inc(s_xh, 1)
            layers_alike(act, run)

        @block.tensor
        def _(pe):
            def run(it):
                pe.wait_ge(s_xt, it * C + 1)
                ops = {n: proj(w[slot], yt) for n, slot in (("q", 1), ("k", 2), ("w", 0))}
                for name in names:
                    kind = name[0]
                    if kind == "v":
                        t = int(name[1])
                        if t == 0:
                            pe.wait_ge(s_wsp3[0], it * 2 * C + C)
                        pe_natural(pe, jobs, name, it, lambda i, kk: yt[i][:, kk, t_slice(t)],
                                   lambda j, kk: w[0][j][:, kk, :], C)
                    elif kind in "qkw":
                        c = int(name[1])
                        if c == 0 and kind == "w":
                            pe.wait_ge(s_wsp3[0], it * 2 * C + 2 * C)
                        elif c == 0:
                            pe.wait_ge(s_wsp3[1 if kind == "q" else 2], it * C + C)
                        lhs, rhs = ops[kind]
                        pe_wide(pe, jobs, name, it, lhs(c), rhs, C)
                    elif kind == "s":
                        h, t = int(name[1]), int(name[3])
                        c, r0 = h // 2, 64 * (h % 2)
                        if t == 0:
                            jobs.wait_drained(pe, f"q{c}", it)
                            jobs.wait_drained(pe, f"k{c}", it)
                        pe_scores(pe, jobs, h, t, it, q[c % 2], k[c % 2], r0, r0 + 64)
                    elif kind == "t":
                        pe_prob_transposes(pe, jobs, int(name[1]) * TILES + int(name[3]), it, UNITS3, s_sc)
                    else:
                        h = int(name[2])
                        if h == 0:
                            pe.wait_ge(s_vd, it * TILES + TILES)
                        pe_values(pe, jobs, h, h // 2, it)
            layers_alike(pe, run)

    z = sb("z", "pt", [R, TILES, D])
    nrm = sb("nrm", "pt", [R, TILES, D], FP32, TILES * D * 4)
    ut = [sb("ut_hi", "qk", [128, 2 * C, W], F32R), sb("ut_lo", "qk", [128, 2 * C, W], F32R, 2 * C * W * 4)]
    xo = sb("xo", "mask", [R, TILES, D])

    names = [f"n{t}" for t in range(TILES)] + ["a0", "a1", "a2", "f0", "f1", "a3", "a4"]
    names += [f"f{c}" for c in range(2, 2 * C)]
    names += [f"p{t}" for t in range(TILES)]
    jobs = Jobs(ring, names)
    s_st, s_rs, s_hn, s_hi, s_fd = sem("d_stats"), sem("d_rstd"), sem("d_norm"), sem("d_hi"), sem("d_f_split")
    s_pd, s_vd_, s_n, s_nb, s_xo = sem("d_pool_steps"), sem("d_dve_steps"), sem("d_affine"), sem("d_bias_added"), sem("d_xo_loaded")
    s_xs, s_o, s_out = sem("d_residual"), sem("d_result"), sem("d_stored")

    def lo_t(dve, t):
        dve.wait_ge(s_hi, t + 1)
        s = jobs.at[f"a{t}"][0]
        dve.tensor_tensor(yt[1][:, :, t_slice(t)], blocks(s, C), yt[0][:, :, t_slice(t)].bitcast(FP32),
                          ALU.subtract).then_inc(jobs.drained[s], 1)

    def hi_t(act, t):
        s = jobs.at[f"a{t}"][0]
        act_hi(act, jobs, f"a{t}", 0, yt[0][:, :, t_slice(t)], blocks(s, C), s_hi)

    with nc.Block() as block:
        @block.sync
        def _(sp):
            load_row3(sp, 1, row(a["L3_gnn_ln_g"]))
            load_row3(sp, 2, row(a["L3_gnn_ln_b"]))
            load_row3(sp, 0, row(a["L3_gnn_b2"]))
            sp.dma_start(xo[:], x_spill).then_inc(s_xo, 16)
            jobs.wait_filled(sp, f"f{C - 1}")
            load_half(sp, 1, a["L3_gnn_W2"][D:2 * D, :])
            for t in range(TILES):
                sp.wait_ge(s_o, t + 1)
                sp.dma_start(out[t * R:(t + 1) * R, :], xo[:, t, :]).then_inc(s_out, 16)
            sp.wait_ge(s_out, 16 * TILES)

        @block.gpsimd
        def _(pool):
            steps = Steps(s_pd)
            for t in range(TILES):
                pool.wait_ge(s_st, t + 1)
                pool_rstd(pool, steps, t, s_rs)
            pool.wait_ge(s_xo, 16)
            pool.wait_ge(s_row3[0], 16 * (LAYERS + 1))
            for t in range(TILES):
                pool.tensor_tensor(xo[:, t, :], xo[:, t, :], res[:, t, :], ALU.add).then_inc(s_xs, 1)
                jobs.wait_filled(pool, f"a{t}")
                pool.tensor_tensor(nrm[:, t, :], nrm[:, t, :], rows[0][:], ALU.add).then_inc(s_nb, 1)
            pool.wait_ge(s_wl3[1], 16 * (LAYERS + 2))
            split_weights(pool, steps, 1, s_wsp3[1])
            for t in range(TILES):
                pool.wait_ge(s_st, TILES + t + 1)
                pool_rstd(pool, steps, t, s_rs)

        @block.vector
        def _(dve):
            steps = Steps(s_vd_)

            def affine(t, n, out_ap):
                dve.wait_ge(s_hn, n * TILES + t + 1)
                if n + t > 0:
                    dve.wait_ge(s_n, n * TILES + t)
                steps.done(dve.tensor_tensor(y1[:], xn[:, t % 2, :], rows[1][:], ALU.mult))
                steps.wait(dve)
                dve.tensor_tensor(out_ap, y1[:], rows[2][:], ALU.add).then_inc(s_n, 1)

            for t in range(TILES):
                jobs.wait_drained(dve, f"n{t}")
                dve_stats(dve, steps, t, z[:, t, :], s_st)
            dve.wait_ge(s_row3[1], 16)
            dve.wait_ge(s_row3[2], 16)
            for t in range(TILES):
                affine(t, 0, nrm[:, t, :])
                if t > 0:
                    lo_t(dve, t - 1)
            lo_t(dve, TILES - 1)
            for c in range(2 * C):
                jobs.wait_drained(dve, f"f{c}")
                steps.done(dve.tensor_copy(ut[0][:, c, :], ftmp[:, c % 2, :]))
                steps.wait(dve)
                dve.tensor_tensor(ut[1][:, c, :], ftmp[:, c % 2, :], ut[0][:, c, :].bitcast(FP32),
                                  ALU.subtract).then_inc(s_fd, 1)
            dve.wait_ge(s_nb, TILES)

            def result(t):
                affine(t, 1, y2[:, t % 2, :])
                dve.wait_ge(s_n, TILES + t + 1)
                dve.tensor_tensor(xo[:, t, :], y2[:, t % 2, :], xo[:, t, :], ALU.add).then_inc(s_o, 1)

            for t in range(TILES):
                s = jobs.wait_filled(dve, f"p{t}")
                dve.tensor_tensor(z[:, t, :], ps[s][0:R, 0:D], nrm[:, t, :], ALU.add).then_inc(jobs.drained[s], 1)
                jobs.wait_drained(dve, f"p{t}")
                dve_stats(dve, steps, t, z[:, t, :], s_st)
                if t >= 2:
                    if t >= 4:
                        dve.wait_ge(s_o, t - 3)
                    result(t - 2)
            for t in (TILES - 2, TILES - 1):
                dve.wait_ge(s_o, t - 1)
                result(t)

        @block.scalar
        def _(act):
            for t in range(TILES):
                s = jobs.wait_filled(act, f"n{t}")
                act.activation(z[:, t, :], ps[s][0:R, 0:D], ACT.Copy).then_inc(jobs.drained[s], 1)

            def normalise(t, n):
                act.wait_ge(s_rs, n * TILES + t + 1)
                if t >= 2:
                    act.wait_ge(s_n, n * TILES + t - 1)
                act.activation(xn[:, t % 2, :], z[:, t, :], ACT.Identity, bias=nmr[:, t:t + 1],
                               scale=rstd[:, t:t + 1]).then_inc(s_hn, 1)

            for t in range(TILES):
                normalise(t, 0)
                if t > 0:
                    hi_t(act, t - 1)
            hi_t(act, TILES - 1)
            for c in range(2 * C):
                s = jobs.wait_filled(act, f"f{c}")
                if c >= 2:
                    act.wait_ge(s_fd, c - 1)
                act.activation(halves(ftmp[:, c % 2, :]), wide(s), ACT.Relu,
                               bias=b1c3[:, c:c + 1]).then_inc(jobs.drained[s], 1)
            for t in range(TILES):
                normalise(t, 1)

        @block.tensor
        def _(pe):
            for t in range(TILES):
                pe_transposes(pe, jobs, f"n{t}", 0, lambda b: acc[:, b, t_slice(t)], C, 128, R)
            def ffn(c, parts=(0, 1)):
                if c % C == 0:
                    pe.wait_ge(s_wsp3[1 + c // C], C * (LAYERS + 1))
                lhs, rhs = proj(w[1 + c // C], yt)
                pe_wide(pe, jobs, f"f{c}", 0, lhs(c % C), rhs, C, parts=parts)

            for t in range(TILES):
                if t == 3:
                    jobs.wait_drained(pe, "a2")
                    ffn(0, (0,))
                    ffn(1, (0,))
                pe.wait_ge(s_n, t + 1)
                pe_transposes(pe, jobs, f"a{t}", 0, lambda b: nrm[:, t, b * 128:(b + 1) * 128], C, R, 128)
            jobs.wait_drained(pe, f"a{TILES - 1}")
            ffn(0, (1,))
            ffn(1, (1,))
            for c in range(2, 2 * C):
                ffn(c)
            pe.wait_ge(s_wsp3[0], C * (2 * LAYERS + 1))
            pe.wait_ge(s_wsp3[1], C * (LAYERS + 2))
            for t in range(TILES):
                pe_natural(pe, jobs, f"p{t}", 0, lambda i, kk: ut[i][:, kk, t_slice(t)],
                           lambda j, kk: w[kk // C][j][:, kk % C, :], 2 * C,
                           None if t else lambda kk: pe.wait_ge(s_fd, kk + 1))


INPUTS = ["x", "src", "dst", "node_vec1"]
INPUTS += [f"L{n}_gnn_{p}" for n in (0, 1) for p in ("W1", "b1", "W2", "b2")]
INPUTS += [f"L2_gnn_{p}" for p in ("f_w1", "f_b1", "f_w2", "f_b2", "s1_w", "s1_b", "b1_w", "b1_b", "wq", "bq", "wk",
                                   "bk", "wv", "bv", "wo", "bo", "s2_w", "s2_b", "b2_w", "b2_b", "m_w1", "m_b1",
                                   "m_w2", "m_b2")]
INPUTS += [f"L3_gnn_{p}" for p in ("Wq", "bq", "Wk", "bk", "Wv", "bv", "Ws", "bs", "W1", "b1", "W2", "b2", "ln_g",
                                   "ln_b")]


def program(nc, shapes):
    a = {n: nc.dram_tensor(n, s, mybir.dt.from_np(d), kind="ExternalInput").ap() for n, (s, d) in shapes.items()}
    out = nc.dram_tensor("out", [N, D], FP32, kind="ExternalOutput").ap()
    build(nc, a, out)


def kernel(**inputs):
    import concourse.bacc as bacc
    from concourse.bass_utils import run_bass_kernel_spmd

    nc = bacc.Bacc("TRN2", target_bir_lowering=False, num_devices=1)
    arrays = {n: np.ascontiguousarray(inputs[n]) for n in INPUTS}
    program(nc, {n: (list(v.shape), v.dtype) for n, v in arrays.items()})
    r = run_bass_kernel_spmd(nc, [arrays], core_ids=[0])
    return r.results[0]["out"]
```
